# Optimizing a Trainium2 kernel written in Bass

```python
import numpy as np
import jax
import jax.numpy as jnp

def _softmax(x, axis=-1):
    return jax.nn.softmax(x, axis=axis)

def _gelu(x):
    return jax.nn.gelu(x, approximate=True)

def _silu(x):
    return jax.nn.silu(x)

def _sigmoid(x):
    return jax.nn.sigmoid(x)

def _layernorm(x, axis=-1, eps=1e-05):
    m = jnp.mean(x, axis=axis, keepdims=True)
    v = jnp.var(x, axis=axis, keepdims=True)
    return (x - m) / jnp.sqrt(v + eps)

def _scatter_add(tgt, idx, src, axis=0):
    return tgt.at[idx].add(src)

def _segment_sum(src, seg, n):
    return jax.ops.segment_sum(src, seg, n)
kernel_name = 'mk_perceiver_d2_seqx_r8_a39833'

def setup_inputs(seed: int=0):
    np.random.seed(seed)
    _w = jnp.asarray

    def _rec_inputs():
        import jax
        import jax.numpy as jnp
        _rk = jax.random.key(seed)
        x = -0.000929 + 1 * jax.random.normal(jax.random.fold_in(_rk, 1), (64, 32, 256), jnp.float32)
        _lenS = 32 - jax.random.randint(jax.random.fold_in(_rk, 7), (64,), 0, max(1, 32 // 4) + 1, jnp.int32)
        _lenS2 = 257 - jax.random.randint(jax.random.fold_in(_rk, 8), (64,), 0, max(1, 257 // 4) + 1, jnp.int32)
        _ctx_2048P = jax.random.normal(jax.random.fold_in(_rk, 11), (64, 16, 256), jnp.float32)
        _ctx_2048c = jax.random.dirichlet(jax.random.fold_in(_rk, 511), 0.3 * jnp.ones((16,), jnp.float32), (64, 257))
        _ctx_2048t = jnp.einsum('bsk,bkd->bsd', _ctx_2048c, _ctx_2048P)
        _ctx_2048t = _ctx_2048t * jax.lax.rsqrt(jnp.mean(jnp.square(_ctx_2048t)) + 1e-12) * 0.953939
        ctx_2048 = 2.81802e-05 + 1.00001 * (_ctx_2048t + 0.3 * jax.random.normal(jax.random.fold_in(_rk, 611), (64, 257, 256), jnp.float32))
        itok_BxS_0_1023 = jax.random.randint(jax.random.fold_in(_rk, 12), (64, 32), 0, 128, jnp.int32)
        return (x, ctx_2048, itok_BxS_0_1023)
    x, ctx_2048, itok_BxS_0_1023 = _rec_inputs()

    def _L0_xattn_setup():
        import jax, jax.numpy as jnp
        import numpy as np
        from jax import lax
        LN_EPS = 1e-05
        key = jax.random.key(seed)
        ks = jax.random.split(key, 8)
        B, S, T, D = (4, 128, 256, 256)
        scale = 0.02
        return {'Z': jax.random.normal(ks[0], (B, S, D), dtype=jnp.float32), 'kv': jax.random.normal(ks[1], (B, T, D), dtype=jnp.float32), 'decay': jnp.float32(0.9), 'W_in': jax.random.normal(ks[2], (D, D), dtype=jnp.float32) * scale, 'b_in': jnp.zeros((D,), dtype=jnp.float32), 'W_out': jax.random.normal(ks[3], (D, D), dtype=jnp.float32) * scale, 'b_out': jnp.zeros((D,), dtype=jnp.float32), 'gamma': jnp.ones((D,), dtype=jnp.float32), 'beta': jnp.zeros((D,), dtype=jnp.float32)}
    _L0_xattn_all = _L0_xattn_setup()
    _L0_xattn_in = {k: v for k, v in _L0_xattn_all.items() if k in ('decay', 'W_in', 'b_in', 'W_out', 'b_out', 'gamma', 'beta')}
    del _L0_xattn_all

    def _L0_attn_setup():
        import jax, jax.numpy as jnp
        import numpy as np
        EMBED_DIM = 256
        NUM_HEADS = 32
        HEAD_DIM = EMBED_DIM // NUM_HEADS
        BATCH = 2
        SEQ_LEN = 256
        key = jax.random.key(seed)
        ks = jax.random.split(key, 5)
        scale = 1.0 / np.sqrt(EMBED_DIM)
        x = jax.random.normal(ks[0], (BATCH, SEQ_LEN, EMBED_DIM), dtype=jnp.float32)
        Wq = jax.random.normal(ks[1], (EMBED_DIM, EMBED_DIM), dtype=jnp.float32) * scale
        Wk = jax.random.normal(ks[2], (EMBED_DIM, EMBED_DIM), dtype=jnp.float32) * scale
        Wv = jax.random.normal(ks[3], (EMBED_DIM, EMBED_DIM), dtype=jnp.float32) * scale
        Wo = jax.random.normal(ks[4], (EMBED_DIM, EMBED_DIM), dtype=jnp.float32) * scale
        return {'x': x, 'Wq': Wq, 'Wk': Wk, 'Wv': Wv, 'Wo': Wo}
    _L0_attn_all = _L0_attn_setup()
    _L0_attn_in = {k: v for k, v in _L0_attn_all.items() if k in ('Wq', 'Wk', 'Wv', 'Wo')}
    del _L0_attn_all

    def _L0_ffn_setup():
        import jax, jax.numpy as jnp
        import numpy as np
        D_MODEL = 256
        HIDDEN = int(2 * D_MODEL * 4 / 3)

        def ternary_quant(w):
            s = jnp.mean(jnp.abs(w))
            q = jnp.clip(jnp.round(w / s), -1.0, 1.0) * s
            return w + jax.lax.stop_gradient(q - w)
        key = jax.random.key(seed)
        k0, k1, k2, k3 = jax.random.split(key, 4)
        x = jax.random.normal(k0, (4, 512, D_MODEL), dtype=jnp.float32)
        std_in = 1.0 / np.sqrt(D_MODEL)
        std_h = 1.0 / np.sqrt(HIDDEN)
        w1 = jax.random.uniform(k1, (HIDDEN, D_MODEL), jnp.float32, -std_in, std_in)
        w3 = jax.random.uniform(k2, (HIDDEN, D_MODEL), jnp.float32, -std_in, std_in)
        w2 = jax.random.uniform(k3, (D_MODEL, HIDDEN), jnp.float32, -std_h, std_h)
        return {'x': x, 'w1': w1, 'w3': w3, 'w2': w2}
    _L0_ffn_all = _L0_ffn_setup()
    _L0_ffn_in = {k: v for k, v in _L0_ffn_all.items() if k in ('w1', 'w3', 'w2')}
    del _L0_ffn_all

    def _L1_xattn_setup():
        import jax, jax.numpy as jnp
        import numpy as np
        B, Lq, Lk = (2, 512, 128)
        Q_DIM, KV_DIM = (256, 256)
        H, HD = (16, 128)
        KVC, QC, R = (64, 96, 64)
        LOOKBACK = 8
        NEG = -1e+30

        def _rope(x, L):
            half = x.shape[-1] // 2
            inv_freq = 1.0 / 10000.0 ** (jnp.arange(half, dtype=jnp.float32) / half)
            ang = jnp.arange(L, dtype=jnp.float32)[:, None] * inv_freq
            cos, sin = (jnp.cos(ang), jnp.sin(ang))
            x1, x2 = (x[..., :half], x[..., half:])
            return jnp.concatenate([x1 * cos - x2 * sin, x1 * sin + x2 * cos], axis=-1)
        key = jax.random.key(seed)
        ks = jax.random.split(key, 11)

        def w(k, shape, fan_in):
            return jax.random.normal(k, shape, jnp.float32) / np.sqrt(fan_in).astype(np.float32)
        return {'q': jax.random.normal(ks[0], (B, Lq, Q_DIM), jnp.float32), 'kv': jax.random.normal(ks[1], (B, Lk, KV_DIM), jnp.float32), 'seg_id': jnp.sort(jax.random.randint(ks[2], (B, Lq), 0, Lk), axis=-1), 'W_kvc': w(ks[3], (KV_DIM, KVC), KV_DIM), 'W_dq': w(ks[4], (Q_DIM, QC), Q_DIM), 'W_uq': w(ks[5], (QC, H * HD), QC), 'W_qr': w(ks[6], (QC, H * R), QC), 'W_uk': w(ks[7], (KVC, H * HD), KVC), 'W_kr': w(ks[8], (KVC, R), KVC), 'W_uv': w(ks[9], (KVC, H * HD), KVC), 'W_o': w(ks[10], (H * HD, Q_DIM), H * HD)}
    _L1_xattn_all = _L1_xattn_setup()
    _L1_xattn_in = {k: v for k, v in _L1_xattn_all.items() if k in ('W_kvc', 'W_dq', 'W_uq', 'W_qr', 'W_uk', 'W_kr', 'W_uv', 'W_o')}
    del _L1_xattn_all

    def _L1_attn_setup():
        import jax, jax.numpy as jnp
        import numpy as np
        HIDDEN = 256
        NUM_HEADS = 6
        HEAD_DIM = 32
        KEY_DIM = NUM_HEADS * HEAD_DIM
        VALUE_DIM = KEY_DIM
        CONV_K = 4
        EPS = 1e-05

        def _causal_depthwise_conv(x, w):
            B, T, C = x.shape
            K = w.shape[1]
            xp = jnp.pad(x, ((0, 0), (K - 1, 0), (0, 0)))
            y = jnp.zeros_like(x)
            for i in range(K):
                y = y + xp[:, i:i + T, :] * w[:, i]
            return jax.nn.silu(y)

        def _l2norm(x, eps=1e-06):
            return x * jax.lax.rsqrt(jnp.sum(x * x, axis=-1, keepdims=True) + eps)
        key = jax.random.key(seed)
        ks = jax.random.split(key, 16)
        s = lambda fan: 1.0 / np.sqrt(fan)
        inp = {'hidden_states': jax.random.normal(ks[0], (2, 256, HIDDEN), jnp.float32), 'Wq': jax.random.normal(ks[1], (KEY_DIM, HIDDEN), jnp.float32) * s(HIDDEN), 'Wk': jax.random.normal(ks[2], (KEY_DIM, HIDDEN), jnp.float32) * s(HIDDEN), 'Wv': jax.random.normal(ks[3], (VALUE_DIM, HIDDEN), jnp.float32) * s(HIDDEN), 'Wo': jax.random.normal(ks[4], (HIDDEN, VALUE_DIM), jnp.float32) * s(VALUE_DIM), 'Wb': jax.random.normal(ks[5], (NUM_HEADS, HIDDEN), jnp.float32) * s(HIDDEN), 'Wa': jax.random.normal(ks[6], (NUM_HEADS, HIDDEN), jnp.float32) * s(HIDDEN), 'Wg': jax.random.normal(ks[7], (VALUE_DIM, HIDDEN), jnp.float32) * s(HIDDEN), 'conv_q': jax.random.normal(ks[8], (KEY_DIM, CONV_K), jnp.float32) * s(CONV_K), 'conv_k': jax.random.normal(ks[9], (KEY_DIM, CONV_K), jnp.float32) * s(CONV_K), 'conv_v': jax.random.normal(ks[10], (VALUE_DIM, CONV_K), jnp.float32) * s(CONV_K), 'o_norm_w': jnp.ones((HEAD_DIM,), jnp.float32)}
        A = jax.random.uniform(ks[11], (NUM_HEADS,), jnp.float32, 0.0001, 16.0)
        inp['A_log'] = jnp.log(A)
        dt = jnp.exp(jax.random.uniform(ks[12], (NUM_HEADS,), jnp.float32) * (np.log(0.1) - np.log(0.001)) + np.log(0.001))
        dt = jnp.clip(dt, 0.0001, None)
        inp['dt_bias'] = dt + jnp.log(-jnp.expm1(-dt))
        return inp
    _L1_attn_all = _L1_attn_setup()
    _L1_attn_in = {k: v for k, v in _L1_attn_all.items() if k in ('Wq', 'Wk', 'Wv', 'Wo', 'Wb', 'Wa', 'Wg', 'conv_q', 'conv_k', 'conv_v', 'o_norm_w', 'A_log', 'dt_bias')}
    del _L1_attn_all

    def _L1_ffn_setup():
        import jax, jax.numpy as jnp
        import numpy as np
        TOP_K = 2
        key = jax.random.key(seed)
        ks = jax.random.split(key, 5)
        B, T, D, E, H = (4, 256, 256, 8, 176)
        s = 1.0 / np.sqrt(D)
        sh = 1.0 / np.sqrt(H)
        return {'x': jax.random.normal(ks[0], (B, T, D), dtype=jnp.float32), 'Wg': jax.random.normal(ks[1], (E, D), dtype=jnp.float32) * s, 'W1': jax.random.normal(ks[2], (E, H, D), dtype=jnp.float32) * s, 'W2': jax.random.normal(ks[3], (E, H, D), dtype=jnp.float32) * s, 'W3': jax.random.normal(ks[4], (E, D, H), dtype=jnp.float32) * sh}
    _L1_ffn_all = _L1_ffn_setup()
    _L1_ffn_in = {k: v for k, v in _L1_ffn_all.items() if k in ('Wg', 'W1', 'W2', 'W3')}
    del _L1_ffn_all
    return {'x': x, 'ctx_2048': ctx_2048, 'itok_BxS_0_1023': itok_BxS_0_1023, 'L0_xattn_decay': _L0_xattn_in['decay'], 'L0_xattn_W_in': _L0_xattn_in['W_in'], 'L0_xattn_b_in': _L0_xattn_in['b_in'], 'L0_xattn_W_out': _L0_xattn_in['W_out'], 'L0_xattn_b_out': _L0_xattn_in['b_out'], 'L0_xattn_gamma': _L0_xattn_in['gamma'], 'L0_xattn_beta': _L0_xattn_in['beta'], 'L0_attn_Wq': _L0_attn_in['Wq'], 'L0_attn_Wk': _L0_attn_in['Wk'], 'L0_attn_Wv': _L0_attn_in['Wv'], 'L0_attn_Wo': _L0_attn_in['Wo'], 'L0_ffn_w1': _L0_ffn_in['w1'], 'L0_ffn_w3': _L0_ffn_in['w3'], 'L0_ffn_w2': _L0_ffn_in['w2'], 'L1_xattn_W_kvc': _L1_xattn_in['W_kvc'], 'L1_xattn_W_dq': _L1_xattn_in['W_dq'], 'L1_xattn_W_uq': _L1_xattn_in['W_uq'], 'L1_xattn_W_qr': _L1_xattn_in['W_qr'], 'L1_xattn_W_uk': _L1_xattn_in['W_uk'], 'L1_xattn_W_kr': _L1_xattn_in['W_kr'], 'L1_xattn_W_uv': _L1_xattn_in['W_uv'], 'L1_xattn_W_o': _L1_xattn_in['W_o'], 'L1_attn_Wq': _L1_attn_in['Wq'], 'L1_attn_Wk': _L1_attn_in['Wk'], 'L1_attn_Wv': _L1_attn_in['Wv'], 'L1_attn_Wo': _L1_attn_in['Wo'], 'L1_attn_Wb': _L1_attn_in['Wb'], 'L1_attn_Wa': _L1_attn_in['Wa'], 'L1_attn_Wg': _L1_attn_in['Wg'], 'L1_attn_conv_q': _L1_attn_in['conv_q'], 'L1_attn_conv_k': _L1_attn_in['conv_k'], 'L1_attn_conv_v': _L1_attn_in['conv_v'], 'L1_attn_o_norm_w': _L1_attn_in['o_norm_w'], 'L1_attn_A_log': _L1_attn_in['A_log'], 'L1_attn_dt_bias': _L1_attn_in['dt_bias'], 'L1_ffn_Wg': _L1_ffn_in['Wg'], 'L1_ffn_W1': _L1_ffn_in['W1'], 'L1_ffn_W2': _L1_ffn_in['W2'], 'L1_ffn_W3': _L1_ffn_in['W3']}

def reference(x, ctx_2048, itok_BxS_0_1023, L0_xattn_decay, L0_xattn_W_in, L0_xattn_b_in, L0_xattn_W_out, L0_xattn_b_out, L0_xattn_gamma, L0_xattn_beta, L0_attn_Wq, L0_attn_Wk, L0_attn_Wv, L0_attn_Wo, L0_ffn_w1, L0_ffn_w3, L0_ffn_w2, L1_xattn_W_kvc, L1_xattn_W_dq, L1_xattn_W_uq, L1_xattn_W_qr, L1_xattn_W_uk, L1_xattn_W_kr, L1_xattn_W_uv, L1_xattn_W_o, L1_attn_Wq, L1_attn_Wk, L1_attn_Wv, L1_attn_Wo, L1_attn_Wb, L1_attn_Wa, L1_attn_Wg, L1_attn_conv_q, L1_attn_conv_k, L1_attn_conv_v, L1_attn_o_norm_w, L1_attn_A_log, L1_attn_dt_bias, L1_ffn_Wg, L1_ffn_W1, L1_ffn_W2, L1_ffn_W3):
    import jax
    import jax.numpy as jnp

    def _L0_xattn_ref(Z, kv, decay, W_in, b_in, W_out, b_out, gamma, beta):
        import jax, jax.numpy as jnp
        import numpy as np
        from jax import lax
        LN_EPS = 1e-05
        B, T, D = kv.shape
        K = jax.nn.sigmoid(decay)
        x = jnp.einsum('btd,ed->bte', kv, W_in) + b_in

        def scan_fn(s, xt):
            s = K * s + xt
            return (s, s)
        s0 = jnp.zeros((B, D), dtype=kv.dtype)
        _, states = lax.scan(scan_fn, s0, jnp.swapaxes(x, 0, 1))
        states = jnp.swapaxes(states, 0, 1)
        proj = jnp.einsum('btd,ed->bte', states, W_out) + b_out
        summary = jnp.mean(proj, axis=1, keepdims=True)
        y = Z + summary
        mu = jnp.mean(y, axis=-1, keepdims=True)
        var = jnp.mean((y - mu) ** 2, axis=-1, keepdims=True)
        return (y - mu) / jnp.sqrt(var + LN_EPS) * gamma + beta

    def _L0_attn_ref(x, Wq, Wk, Wv, Wo):
        import jax, jax.numpy as jnp
        import numpy as np
        EMBED_DIM = 256
        NUM_HEADS = 32
        HEAD_DIM = EMBED_DIM // NUM_HEADS
        BATCH = 2
        SEQ_LEN = 256
        q = jnp.einsum('bse,ef->bsf', x, Wq)
        k = jnp.einsum('bse,ef->bsf', x, Wk)
        v = jnp.einsum('bse,ef->bsf', x, Wv)
        qT = jnp.swapaxes(q, 1, 2)
        kT = jnp.swapaxes(k, 1, 2)
        vT = jnp.swapaxes(v, 1, 2)
        attn_scores = jnp.einsum('bes,bfs->bef', qT, kT) / np.sqrt(HEAD_DIM)
        attn_weights = jax.nn.softmax(attn_scores, axis=-1)
        attn_output = jnp.einsum('bef,bfs->bes', attn_weights, vT)
        attn_output = jnp.swapaxes(attn_output, 1, 2)
        return jnp.einsum('bse,ef->bsf', attn_output, Wo)

    def _L0_ffn_ref(x, w1, w3, w2):
        import jax, jax.numpy as jnp
        import numpy as np
        D_MODEL = 256
        HIDDEN = int(2 * D_MODEL * 4 / 3)

        def ternary_quant(w):
            s = jnp.mean(jnp.abs(w))
            q = jnp.clip(jnp.round(w / s), -1.0, 1.0) * s
            return w + jax.lax.stop_gradient(q - w)
        w1q = ternary_quant(w1)
        w3q = ternary_quant(w3)
        w2q = ternary_quant(w2)
        h1 = jnp.einsum('bsd,hd->bsh', x, w1q)
        h3 = jnp.einsum('bsd,hd->bsh', x, w3q)
        g = jax.nn.silu(h1) * h3
        return jnp.einsum('bsh,dh->bsd', g, w2q)

    def _L1_xattn_ref(q, kv, seg_id, W_kvc, W_dq, W_uq, W_qr, W_uk, W_kr, W_uv, W_o):
        import jax, jax.numpy as jnp
        import numpy as np
        B, Lq, Lk = (2, 512, 128)
        Q_DIM, KV_DIM = (256, 256)
        H, HD = (16, 128)
        KVC, QC, R = (64, 96, 64)
        LOOKBACK = 8
        NEG = -1e+30

        def _rope(x, L):
            half = x.shape[-1] // 2
            inv_freq = 1.0 / 10000.0 ** (jnp.arange(half, dtype=jnp.float32) / half)
            ang = jnp.arange(L, dtype=jnp.float32)[:, None] * inv_freq
            cos, sin = (jnp.cos(ang), jnp.sin(ang))
            x1, x2 = (x[..., :half], x[..., half:])
            return jnp.concatenate([x1 * cos - x2 * sin, x1 * sin + x2 * cos], axis=-1)
        b, lq, _ = q.shape
        lk = kv.shape[1]
        kv_c = kv @ W_kvc
        q_c = q @ W_dq
        q_nope = (q_c @ W_uq).reshape(b, lq, H, HD).transpose(0, 2, 1, 3)
        q_rope = (q_c @ W_qr).reshape(b, lq, H, R).transpose(0, 2, 1, 3)
        k_nope = (kv_c @ W_uk).reshape(b, lk, H, HD)
        v = (kv_c @ W_uv).reshape(b, lk, H, HD)
        k_rope = kv_c @ W_kr
        q_rope = _rope(q_rope, lq)
        k_rope = _rope(k_rope, lk)
        scale = 1.0 / np.sqrt(HD + R).astype(np.float32)
        scores = (jnp.einsum('bhqd,bkhd->bhqk', q_nope, k_nope) + jnp.einsum('bhqr,bkr->bhqk', q_rope, k_rope)) * scale
        k_ids = jnp.arange(lk)[None, None, :]
        qs = seg_id[:, :, None]
        good = (k_ids <= qs) & (k_ids >= qs - LOOKBACK)
        scores = jnp.where(good[:, None, :, :], scores, NEG)
        attn = jax.nn.softmax(scores, axis=-1)
        out = jnp.einsum('bhqk,bkhd->bqhd', attn, v).reshape(b, lq, H * HD)
        return out @ W_o

    def _L1_attn_ref(hidden_states, Wq, Wk, Wv, Wo, Wb, Wa, Wg, conv_q, conv_k, conv_v, o_norm_w, A_log, dt_bias):
        import jax, jax.numpy as jnp
        import numpy as np
        HIDDEN = 256
        NUM_HEADS = 6
        HEAD_DIM = 32
        KEY_DIM = NUM_HEADS * HEAD_DIM
        VALUE_DIM = KEY_DIM
        CONV_K = 4
        EPS = 1e-05

        def _causal_depthwise_conv(x, w):
            B, T, C = x.shape
            K = w.shape[1]
            xp = jnp.pad(x, ((0, 0), (K - 1, 0), (0, 0)))
            y = jnp.zeros_like(x)
            for i in range(K):
                y = y + xp[:, i:i + T, :] * w[:, i]
            return jax.nn.silu(y)

        def _l2norm(x, eps=1e-06):
            return x * jax.lax.rsqrt(jnp.sum(x * x, axis=-1, keepdims=True) + eps)
        x = hidden_states
        B, T, D = x.shape
        H, dk, dv = (NUM_HEADS, HEAD_DIM, HEAD_DIM)
        q = _causal_depthwise_conv(jnp.einsum('btd,kd->btk', x, Wq), conv_q)
        k = _causal_depthwise_conv(jnp.einsum('btd,kd->btk', x, Wk), conv_k)
        v = _causal_depthwise_conv(jnp.einsum('btd,kd->btk', x, Wv), conv_v)
        q = _l2norm(q.reshape(B, T, H, dk))
        k = _l2norm(k.reshape(B, T, H, dk))
        v = v.reshape(B, T, H, dv)
        beta = jax.nn.sigmoid(jnp.einsum('btd,hd->bth', x, Wb))
        g = -jnp.exp(A_log) * jax.nn.softplus(jnp.einsum('btd,hd->bth', x, Wa) + dt_bias)
        scale = dk ** (-0.5)

        def step(S, inputs):
            q_t, k_t, v_t, g_t, b_t = inputs
            S = S * jnp.exp(g_t)[..., None, None]
            kv = jnp.einsum('bhk,bhkv->bhv', k_t, S)
            u = b_t[..., None] * (v_t - kv)
            S = S + jnp.einsum('bhk,bhv->bhkv', k_t, u)
            o_t = jnp.einsum('bhk,bhkv->bhv', q_t * scale, S)
            return (S, o_t)
        tfirst = lambda a: jnp.moveaxis(a, 1, 0)
        S0 = jnp.zeros((B, H, dk, dv), x.dtype)
        _, o = jax.lax.scan(step, S0, (tfirst(q), tfirst(k), tfirst(v), tfirst(g), tfirst(beta)))
        o = jnp.moveaxis(o, 0, 1)
        gate = jnp.einsum('btd,vd->btv', x, Wg).reshape(B, T, H, dv)
        o = o * jax.lax.rsqrt(jnp.mean(o * o, axis=-1, keepdims=True) + EPS)
        o = o * o_norm_w * jax.nn.silu(gate)
        out = jnp.einsum('btv,dv->btd', o.reshape(B, T, H * dv), Wo)
        return out

    def _L1_ffn_ref(x, Wg, W1, W2, W3):
        import jax, jax.numpy as jnp
        import numpy as np
        TOP_K = 2
        E = Wg.shape[0]
        scores = jnp.einsum('btd,ed->bte', x, Wg)
        topk_s, topk_i = jax.lax.top_k(scores, TOP_K)
        probs = jax.nn.softmax(topk_s, axis=-1)
        onehot = (topk_i[..., None] == jnp.arange(E)).astype(x.dtype)
        w = jnp.einsum('btk,btke->bte', probs, onehot)
        y = jnp.zeros_like(x)
        for e in range(E):
            h = jax.nn.silu(jnp.einsum('btd,hd->bth', x, W1[e])) * jnp.einsum('btd,hd->bth', x, W2[e])
            y = y + w[..., e:e + 1] * jnp.einsum('bth,dh->btd', h, W3[e])
        return y
    x = x + _L0_xattn_ref(_layernorm(x, axis=-1), ctx_2048, L0_xattn_decay, L0_xattn_W_in, L0_xattn_b_in, L0_xattn_W_out, L0_xattn_b_out, L0_xattn_gamma, L0_xattn_beta)
    x = x + _L0_attn_ref(_layernorm(x, axis=-1), L0_attn_Wq, L0_attn_Wk, L0_attn_Wv, L0_attn_Wo)
    x = x + _L0_ffn_ref(_layernorm(x, axis=-1), L0_ffn_w1, L0_ffn_w3, L0_ffn_w2)
    x = x + _L1_xattn_ref(_layernorm(x, axis=-1), ctx_2048, itok_BxS_0_1023, L1_xattn_W_kvc, L1_xattn_W_dq, L1_xattn_W_uq, L1_xattn_W_qr, L1_xattn_W_uk, L1_xattn_W_kr, L1_xattn_W_uv, L1_xattn_W_o)
    x = x + _L1_attn_ref(_layernorm(x, axis=-1), L1_attn_Wq, L1_attn_Wk, L1_attn_Wv, L1_attn_Wo, L1_attn_Wb, L1_attn_Wa, L1_attn_Wg, L1_attn_conv_q, L1_attn_conv_k, L1_attn_conv_v, L1_attn_o_norm_w, L1_attn_A_log, L1_attn_dt_bias)
    x = x + _L1_ffn_ref(_layernorm(x, axis=-1), L1_ffn_Wg, L1_ffn_W1, L1_ffn_W2, L1_ffn_W3)
    return x

_drawn_inputs = setup_inputs


def setup_inputs(seed=0):
    import zlib

    import numpy as np

    out = dict(_drawn_inputs(seed))
    spreads = {'L0_xattn_b_in': (0.0, 0.1),
     'L0_xattn_b_out': (0.0, 0.1),
     'L0_xattn_gamma': (1.0, 0.2),
     'L0_xattn_beta': (0.0, 0.1),
     'L1_attn_o_norm_w': (1.0, 0.2)}
    factors = {}
    for name, (base, spread) in spreads.items():
        noise = np.random.default_rng([zlib.crc32(name.encode()), seed]).standard_normal(out[name].shape)
        drawn = base * np.exp(spread * noise) if base else spread * noise
        out[name] = jnp.asarray(drawn.astype(out[name].dtype))
    for name, factor in factors.items():
        out[name] = (out[name] * factor).astype(out[name].dtype)
    return out
```

```python
from contextlib import ExitStack

import numpy as np
import concourse.bass as bass
from concourse import mybir

B, S, D, T = 64, 32, 256, 257
P = 128
BT = P // S
TILES = B // BT
STREAMS = 2
ROUNDS = TILES // STREAMS
DC = D // P
EPS = 1e-5
L0_HEAD = 8
FF, FFC = 682, 6
FFT = FF - (FFC - 1) * P
XH, HD, KVC, QC, R = 16, 128, 64, 96, 64
LOOKBACK = 8
NEG = -1e30
SH, SD = 6, 32
SV = SH * SD
CK = 4
QKVC = 5
NE, EH = 8, 176
MH = NE * EH
MHC = MH // P
HALF = MH // 2
STEPS = BT * 2
LEVELS = [2, 4, 8, 16]

_widths = [("ident", P), ("same", P), ("later", P), ("incl", S), ("strict", S), ("eye", S), ("off1", S)]
_widths += [(f"off{m}", P) for m in LEVELS]
_widths += [("qcos", R), ("qnsin", R // 2), ("qsin", R // 2), ("kcos", 2 * R), ("knsin", R), ("ksin", R),
            ("lcos", R), ("lnsin", R // 2), ("lsin", R // 2), ("spread", BT * P), ("pick", BT * P),
            ("iota", NE), ("key", T)]
CONST = {}
_at = 0
for _n, _w in _widths:
    CONST[_n] = (_at, _at + _w)
    _at += _w
NCONST = _at


def constant_table():
    t = np.zeros((P, NCONST), np.float32)
    p = np.arange(P)[:, None]
    j = np.arange(P)[None, :]
    s = np.arange(S)[None, :]

    def put(name, v):
        a, b = CONST[name]
        t[:v.shape[0], a:b] = v

    put("ident", p == j)
    put("same", p // S == j // S)
    put("later", (p // S == j // S) & (p > j))
    put("incl", p % S <= s)
    put("strict", p % S < s)
    put("eye", p % S == s)
    put("off1", (p % S // 2 == s // 2) & (p % S < s))
    for m in LEVELS:
        put(f"off{m}", (p // (2 * m) == j // (2 * m)) & (p // m < j // m))
    half = R // 2
    inv = 1.0 / 10000.0 ** (np.arange(half, dtype=np.float32) / np.float32(half))

    def angles(pos):
        a = pos.astype(np.float32)[:, None] * inv[None, :].astype(np.float32)
        return np.cos(a).astype(np.float32), np.sin(a).astype(np.float32)

    c, n = angles(np.arange(P) % S)
    put("qcos", np.concatenate([c, c], 1))
    put("qnsin", -n)
    put("qsin", n)
    c0, n0 = angles(np.arange(P))
    c1, n1 = angles(np.arange(P) + P)
    put("kcos", np.concatenate([c0, c0, c1, c1], 1))
    put("knsin", -np.concatenate([n0, n1], 1))
    put("ksin", np.concatenate([n0, n1], 1))
    c, n = angles(np.full(BT, T - 1))
    put("lcos", np.concatenate([c, c], 1))
    put("lnsin", -n)
    put("lsin", n)
    put("spread", np.concatenate([(p // S == b) & (p % S == j % S) for b in range(BT)], 1))
    put("pick", np.concatenate([np.broadcast_to(p == b, (P, P)) for b in range(BT)], 1))
    put("iota", np.broadcast_to(np.arange(NE), (P, NE)))
    put("key", np.broadcast_to(np.arange(T), (P, T)))
    return t


SEMS = """
ld_const ld_x0 ld_xs prep_pool ld_f0 ld_a0 ld_xw ld_s ld_m ternary kleft_ps pool_terms residual segf ln_var
ln_rstd seg8 good_lo good_both maskb kleft krope1 krope kleft1 kleft2 qr2 qrope qkvn rn gates gl dexp dts atp
abd pmp pbd onorm orn prep_ps binrep prep_act biasrep absum q_scaled ln_x lnT_ps pooledrep residual_ps lnT
vT_ps vT s0_ps e0 at_ps at av_ps attn0 f_ps ffn kleftT_ps qc_ps qc kleftT q_ps qT_ps s_ps qT e pT_ps pT oT o_ps
oc oT_ps cv_ps gb_ps dec_ps cv_u nat_ps kqT_ps kqT gram_ps t2inv lz_ps lz xbd lt_ps apply_ps applied uu onT_ps
onT rt_ps route m_g m_ps gT_ps gT f_tanh qlat s_max g_tanh softplus conv cv_tanh natural osq rdiff rtanh m_tanh
prep_dve neg_a ln_stats ln_mv ysum gammad o_rinv o_left cv_pad cvx tri xnew m_u
""".split()


def perceiver_kernel(nc, x, ctxT, itok, consts, w, out):
    f32, bf16, i32, u32 = mybir.dt.float32, mybir.dt.bfloat16, mybir.dt.int32, mybir.dt.uint32
    ALU, ACT, AX = mybir.AluOpType, mybir.ActivationFunctionType, mybir.AxisListType
    MUL, ADD, SUB = ALU.mult, ALU.add, ALU.subtract
    U = range(STREAMS)
    ctx = ExitStack()
    with ctx:
        def sb(name, shape, dt=f32):
            return ctx.enter_context(nc.sbuf_tensor(name, shape, dt))

        C = sb("C", [P, NCONST])
        Wc = sb("Wc", [P, DC, D])
        biasrep = sb("biasrep", [P, D])
        gamma = sb("gamma", [P, D])
        beta = sb("beta", [P, D])
        coef = sb("coef", [P, T])
        Wqk0 = sb("Wqk0", [P, DC, 2 * D])
        Wv0 = sb("Wv0", [P, DC, D])
        Wo0 = sb("Wo0", [P, DC, D])
        W13 = sb("W13", [P, 2, DC, FFC * P])
        W2 = sb("W2", [P, FFC, D])
        Wdq = sb("Wdq", [P, DC, QC])
        WQ = sb("WQ", [QC, XH, P])
        WK = sb("WK", [P, DC, P])
        WVO = sb("WVO", [P, XH // 2, D])
        Wqkv = sb("Wqkv", [P, DC, QKVC * P])
        convw = sb("convw", [P, QKVC, CK])
        Wgba = sb("Wgba", [P, DC, SV + 2 * SH])
        dtb = sb("dtb", [P, SH])
        nega = sb("nega", [P, SH])
        onw = sb("onw", [P, SD])
        Wo1 = sb("Wo1", [P, 2, D])
        Wr = sb("Wr", [P, DC, NE])
        W1m = sb("W1m", [P, DC, MH])
        W2m = sb("W2m", [P, DC, MH])
        W3m = sb("W3m", [P, MHC, D])
        spread = sb("spread", [P, BT, P], bf16)
        mhalf = sb("mhalf", [P, 2 * SH])
        small = sb("small", [P, 16])

        def const(name, rows=P):
            a, b = CONST[name]
            return C[0:rows, a:b]

        ident = const("ident")

        BIG = [sb(f"big{u}", [P, 4640]) for u in U]
        MID = [sb(f"mid{u}", [P, 2432]) for u in U]
        xin = [sb(f"xin{u}", [P, D]) for u in U]
        X = [sb(f"X{u}", [P, D]) for u in U]
        XN = [sb(f"XN{u}", [P, D]) for u in U]
        XNT = [sb(f"XNT{u}", [P, DC, P]) for u in U]
        CT = [sb(f"CT{u}", [P, DC, BT, T]) for u in U]
        segi = [sb(f"segi{u}", [P, 1], i32) for u in U]
        seg = [sb(f"seg{u}", [P, 2]) for u in U]
        mask = [sb(f"mask{u}", [P, T], bf16) for u in U]
        st = [sb(f"st{u}", [P, 6]) for u in U]
        mv = [sb(f"mv{u}", [P, 2]) for u in U]
        ve = [sb(f"ve{u}", [P, 2]) for u in U]
        pooled = [sb(f"pooled{u}", [P, DC * BT]) for u in U]
        stat = [sb(f"stat{u}", [P, 64]) for u in U]
        oidx = [sb(f"oidx{u}", [P, NE], u32) for u in U]
        kltmp = [sb(f"kltmp{u}", [BT, R]) for u in U]
        KL = [sb(f"KL{u}", [BT, P + R]) for u in U]

        def view(t, a, *dims):
            n = 1
            for d in dims:
                n *= d
            v = t[:, a:a + n]
            if len(dims) == 2:
                return v.rearrange("p (a b) -> p a b", a=dims[0])
            if len(dims) == 3:
                return v.rearrange("p (a b c) -> p a b c", a=dims[0], b=dims[1])
            return v

        KR = [view(MID[u], 0, BT * 2, P) for u in U]
        KT = [view(MID[u], 1024, BT, T) for u in U]
        VL = [view(MID[u], 2052, BT, KVC) for u in U]
        KRtmp = [sb(f"krt{u}", [P, 2, BT * 2, R]) for u in U]
        good = [sb(f"good{u}", [P, 2, T]) for u in U]
        crep = [view(BIG[u], 1024, DC, BT, S) for u in U]
        prod = [view(BIG[u], 1280, DC * BT, T) for u in U]
        ytmp = [view(BIG[u], 3400, D) for u in U]
        QK0 = [view(BIG[u], 4096, 2 * D) for u in U]
        VT0 = [XN[u][:].rearrange("p (a b) -> p a b", a=DC) for u in U]
        E0 = [view(BIG[u], 0, BT * DC, D) for u in U]
        AT0 = [view(BIG[u], 2048, BT * DC, D) for u in U]
        AV0 = [view(BIG[u], 0, DC, P) for u in U]
        FT = [view(BIG[u], 0, 2, FFC * P // 2) for u in U]
        FU = [view(BIG[u], 768, 2, FFC * P // 2) for u in U]
        FG = [view(BIG[u], 1536, FFC, P) for u in U]
        QR = [view(BIG[u], 0, XH, P) for u in U]
        QT = [view(BIG[u], 2568, BT, XH * S) for u in U]
        QCT = [BIG[u][0:QC, 2048:2048 + P] for u in U]
        QRt = [view(BIG[u], 2568, XH, R) for u in U]
        OT = [view(BIG[u], 0, XH // 2, P) for u in U]
        PT = [view(BIG[u], 1024, 4, P) for u in U]
        EX = [[view(BIG[u], 1536 + 514 * k, 2, T) for k in range(2)] for u in U]
        OC = [[XN[u][:, k * P:(k + 1) * P] for k in range(2)] for u in U]
        CX = [BIG[u][:, 0:QKVC * BT * (S + CK - 1)].rearrange("p (c b s) -> p c b s", c=QKVC, b=BT) for u in U]
        CY = [view(BIG[u], 700, QKVC, P) for u in U]
        CTH = [view(BIG[u], 1340, QKVC, P) for u in U]
        SQ = [view(BIG[u], 1980, 2 * SH, SD) for u in U]
        QKVN = [view(BIG[u], 2364, 3 * SH, SD) for u in U]
        KQT = [view(BIG[u], 3840, 6, P) for u in U]
        ABD = {m: [view(BIG[u], 768 * k, SH, P) for u in U] for k, m in enumerate(LEVELS)}
        XBD = [view(BIG[u], 3072, SH, P) for u in U]
        PBD = [view(BIG[u], 3840, SH, P) for u in U]
        NAT = [view(MID[u], 0, 3 * SH + 6, SD) for u in U]
        BV = [view(MID[u], 576, SH, SD) for u in U]
        GS = [view(MID[u], 768, SH, SD) for u in U]
        DTI = [view(MID[u], 960, SH, S) for u in U]
        DTS = [view(MID[u], 1152, SH, S) for u in U]
        ATP = [view(MID[u], 1344, SH, S) for u in U]
        PMP = [view(MID[u], 1536, SH, S) for u in U]
        TP = [view(MID[u], 1728, SH, S) for u in U]
        XP = [view(MID[u], 1920, SH, S) for u in U]
        ZP = [view(MID[u], 2112, SH, S) for u in U]
        GL = ATP
        DEX = PMP
        WV = [view(MID[u], 0, SH, SD) for u in U]
        RV = [view(MID[u], 192, SH, SD) for u in U]
        UU = [view(MID[u], 384, SH, SD) for u in U]
        ON = [view(MID[u], 1728, SH, SD) for u in U]
        OSQ = [view(MID[u], 1920, SH, SD) for u in U]
        ONT = [view(MID[u], 0, 2, P) for u in U]
        GB = [view(BIG[u], 2940, SV + 2 * SH) for u in U]
        GTH = [view(BIG[u], 3144, SV + 2 * SH) for u in U]
        MT = [view(BIG[u], 0, 2, HALF // 2) for u in U]
        MU = [view(BIG[u], HALF, 2, HALF // 2) for u in U]
        MG = [view(BIG[u], 2 * HALF, MH) for u in U]
        GT = [view(MID[u], 0, MHC, P) for u in U]

        Win_n = view(MID[0], 0, DC, D)
        WoutT = view(MID[0], 512, DC, D)
        binc = MID[0][:, 1024:1024 + DC]
        binrep = view(MID[0], 1032, DC, P)
        boutrep = MID[0][:, 1288:1288 + D]
        ones = MID[0][:, 1544:1544 + T]
        kfill = MID[0][:, 1804:1804 + T]
        crev = MID[0][:, 2064:2064 + T]
        Wo_x = view(BIG[0], 0, XH, D)
        WuqT = view(BIG[1], 0, XH, QC)
        WukT = view(BIG[1], 1536, XH, KVC)
        WuvT = view(BIG[1], 2560, XH, KVC)
        Wqr = BIG[1][0:QC, 3584:3584 + XH * R].rearrange("p (h r) -> p h r", h=XH)
        WkvcT = MID[1][0:KVC, 0:D]
        Wkr = MID[1][0:KVC, 256:256 + R]
        quant = [view(CT[u][:].rearrange("p a b c -> p (a b c)"), 0, 1536) for u in U]

        PS = [ctx.enter_context(nc.psum_tensor(f"ps{u}", [P, 4, 512], f32)) for u in U]
        s = {n: ctx.enter_context(nc.semaphore(n)) for n in SEMS}
        ld_xin = [ctx.enter_context(nc.semaphore(f"ld_xin{u}")) for u in U]
        ld_ctx = [ctx.enter_context(nc.semaphore(f"ld_ctx{u}")) for u in U]
        ld_seg = [ctx.enter_context(nc.semaphore(f"ld_seg{u}")) for u in U]
        stored = [ctx.enter_context(nc.semaphore(f"stored{u}")) for u in U]

        x_v = x.rearrange("(t p) d -> t p d", p=P)
        out_v = out.rearrange("(t p) d -> t p d", p=P)
        itok_v = itok.rearrange("(t p) o -> t p o", p=P)

        def nth(i, u, k=0, n=1):
            return 2 * n * i + 2 * k + u + 1

        def wait_apart(eng, *pairs):
            pairs = [(sem, eng.snap(eng.to_reg(value))) for sem, value in pairs]
            eng.wait_ge(s["ld_const"], 16)
            for sem, value in pairs:
                eng.wait_ge(sem, value)

        LNS = 7

        block = ctx.enter_context(nc.Block())

        @block.sync
        def _(sp):
            def load(t, u):
                sp.dma_start(xin[u][:], x_v[bass.ds(t, 1)].rearrange("a p d -> (a p) d")).then_inc(ld_xin[u], 16)
                sp.dma_start(segi[u][:], itok_v[bass.ds(t, 1)].rearrange("a p d -> (a p) d")).then_inc(ld_seg[u], 16)
            
            def load_ctx(t, u):
                for c in range(DC):
                    sp.dma_start(CT[u][:, c], ctxT[c * P:(c + 1) * P, bass.ds(t * BT, BT), :]).then_inc(ld_ctx[u], 16)

            for u in U:
                sp.sem_inc(stored[u], 16)
            sp.dma_start(C[:], consts).then_inc(s["ld_const"], 16)
            for src, dst in ((w["W_in"], Win_n), (w["W_outT"], WoutT), (w["Wqk0"], Wqk0[:])):
                sp.dma_start(dst, src.rearrange("(c p) n -> p c n", p=P)).then_inc(s["ld_x0"], 16)
            sp.dma_start(binc, w["b_in"]).then_inc(s["ld_x0"], 16)
            for dst, src in ((boutrep, w["b_out"]), (gamma[:], w["gamma"]), (beta[:], w["beta"]), (small[:, 0:1], w["decay"]),
                             (dtb[:], w["dt_bias"]), (small[:, 8:8 + SH], w["A_log"]), (onw[:], w["o_norm"])):
                sp.dma_start(dst, src.to_broadcast([P, src.shape[1]])).then_inc(s["ld_x0"], 16)
            for dst, src in ((WuqT, w["W_uqT"]), (WukT, w["W_ukT"]), (WuvT, w["W_uvT"]), (Wo_x, w["W_o"])):
                sp.dma_start(dst, src.rearrange("(h p) n -> p h n", p=HD)).then_inc(s["ld_xs"], 16)
            sp.dma_start(Wqr, w["W_qr"].rearrange("p (h r) -> p h r", h=XH)).then_inc(s["ld_xs"], 16)
            sp.dma_start(WkvcT, w["W_kvcT"]).then_inc(s["ld_xs"], 16)
            sp.dma_start(Wkr, w["W_kr"]).then_inc(s["ld_xs"], 16)
            sp.dma_start(WK[:, :, 0:KVC], w["W_kvc"].rearrange("(c p) n -> p c n", p=P)).then_inc(s["ld_xs"], 16)
            sp.wait_ge(s["prep_pool"], 1)
            for k, src in enumerate((w["w1T"], w["w3T"])):
                sp.dma_start(W13[:, k, :, 0:FF], src.rearrange("(c p) n -> p c n", p=P)).then_inc(s["ld_f0"], 16)
            sp.dma_start(W2[:, 0:FFC - 1], w["w2T"][0:(FFC - 1) * P].rearrange("(c p) n -> p c n", p=P)).then_inc(s["ld_f0"], 16)
            sp.dma_start(W2[0:FFT, FFC - 1], w["w2T"][(FFC - 1) * P:FF]).then_inc(s["ld_f0"], 16)
            for u in U:
                load(u, u)
            for src, dst in ((w["Wv0"], Wv0), (w["Wo0"], Wo0)):
                sp.dma_start(dst[:], src.rearrange("(c p) n -> p c n", p=P)).then_inc(s["ld_a0"], 16)
            sp.dma_start(Wdq[:], w["W_dq"].rearrange("(c p) n -> p c n", p=P)).then_inc(s["ld_xw"], 16)
            for src, dst in ((w["Wqkv1"], Wqkv), (w["Wgba"], Wgba)):
                sp.dma_start(dst[:], src.rearrange("(c p) n -> p c n", p=P)).then_inc(s["ld_s"], 16)
            sp.dma_start(convw[:], w["conv"].rearrange("(c p) n -> p c n", p=P)).then_inc(s["ld_s"], 16)
            sp.dma_start(Wo1[:, 0], w["WoT1"][0:P]).then_inc(s["ld_s"], 16)
            sp.dma_start(Wo1[SV - P:P, 1], w["WoT1"][P:SV]).then_inc(s["ld_s"], 16)
            for src, dst in ((w["WgT"], Wr), (w["W1T"], W1m), (w["W2T"], W2m), (w["W3T"], W3m)):
                sp.dma_start(dst[:], src.rearrange("(c p) n -> p c n", p=P)).then_inc(s["ld_m"], 16)
            sp.wait_ge(s["ternary"], 3)
            for u in U:
                load_ctx(u, u)
            with sp.Fori(0, ROUNDS - 1) as i:
                for u in U:
                    sp.wait_ge(s["kleft_ps"], nth(i, u))
                    sp.wait_ge(s["pool_terms"], nth(i, u))
                    load_ctx(2 * i + (2 + u), u)
                for u in U:
                    sp.wait_ge(s["residual"], nth(i, u, 0, 6))
                    sp.wait_ge(s["segf"], nth(i, u))
                    load(2 * i + (2 + u), u)
                for u in U:
                    sp.wait_ge(s["residual"], nth(i, u, 5, 6))
                    sp.dma_start(out_v[bass.ds(2 * i + u, 1)].rearrange("a p d -> (a p) d"),
                                 XN[u][:]).then_inc(stored[u], 16)
            for u in U:
                sp.wait_ge(s["residual"], nth(ROUNDS - 1, u, 5, 6))
                sp.dma_start(out_v[2 * (ROUNDS - 1) + u], XN[u][:]).then_inc(stored[u], 16)
            for u in U:
                sp.wait_ge(stored[u], 16 * (ROUNDS + 1))

        @block.gpsimd
        def _(pool):
            pool.memset(W13[:, :, :, FF:FFC * P], 0.0)
            pool.memset(W2[:, FFC - 1], 0.0).then_inc(s["prep_pool"], 1)
            pool.memset(mhalf[:], -0.5).then_inc(s["prep_pool"], 1)
            pool.wait_ge(s["ld_const"], 16)
            pool.tensor_copy(spread[:], const("spread").rearrange("p (b q) -> p b q", b=BT)).then_inc(s["prep_pool"], 1)
            pool.wait_ge(s["prep_pool"], 2)
            with pool.Fori(0, ROUNDS) as i:
                def rstd(k):
                    for u in U:
                        pool.wait_ge(s["ln_var"], nth(i, u, k, LNS))
                        pool.tensor_tensor(ve[u][:, 1:2], ve[u][:, 0:1], mhalf[:, 0:1], ALU.pow).then_inc(s["ln_rstd"], 1)

                rstd(0)
                rstd(1)
                rstd(2)
                for u in U:
                    wait_apart(pool, (ld_seg[u], 16 * i + 16))
                    pool.tensor_copy(seg[u][:, 0:1], segi[u][:]).then_inc(s["segf"], 1)
                    wait_apart(pool, (s["segf"], nth(i, u)))
                    pool.tensor_scalar(seg[u][:, 1:2], seg[u][:, 0:1], float(-LOOKBACK), None, ADD).then_inc(s["seg8"], 1)
                    pool.tensor_scalar(good[u][:, 0], const("key"), seg[u][:, 0:1], None, ALU.is_le)
                    wait_apart(pool, (s["seg8"], nth(i, u)))
                    pool.tensor_scalar(good[u][:, 1], const("key"), seg[u][:, 1:2], None, ALU.is_ge).then_inc(s["good_lo"], 1)
                    pool.wait_ge(s["good_lo"], nth(i, u))
                    pool.tensor_tensor(good[u][:, 0], good[u][:, 0], good[u][:, 1], MUL).then_inc(s["good_both"], 1)
                    wait_apart(pool, (s["good_both"], nth(i, u)))
                    pool.tensor_scalar(mask[u][:], good[u][:, 0], -1.0, -NEG, ADD, MUL).then_inc(s["maskb"], 1)
                for u in U:
                    pool.wait_ge(s["kleft"], nth(i, u))
                    kr = KR[u].rearrange("p (b c) d -> p b c d", b=BT)
                    for b in range(BT):
                        kb, t0, t1 = kr[:, b], KRtmp[u][:, 0, 2 * b:2 * b + 2], KRtmp[u][:, 1, 2 * b:2 * b + 2]
                        pool.tensor_tensor(t0, kb[:, :, KVC:P], const("kcos").rearrange("p (c d) -> p c d", c=2), MUL)
                        pool.tensor_tensor(t1[:, :, 0:R // 2], kb[:, :, KVC + R // 2:P],
                                           const("knsin").rearrange("p (c d) -> p c d", c=2), MUL)
                        last = pool.tensor_tensor(t1[:, :, R // 2:R], kb[:, :, KVC:KVC + R // 2],
                                                  const("ksin").rearrange("p (c d) -> p c d", c=2), MUL)
                    last.then_inc(s["krope1"], 1)
                    pool.wait_ge(s["krope1"], nth(i, u))
                    pool.tensor_tensor(KR[u][:, :, KVC:P], KRtmp[u][:, 0], KRtmp[u][:, 1], ADD).then_inc(s["krope"], 1)
                for u in U:
                    pool.wait_ge(s["kleft"], nth(i, u))
                    pool.tensor_tensor(KL[u][:, P:P + R], KL[u][:, KVC:P], const("lcos", BT), MUL)
                    pool.tensor_tensor(kltmp[u][:, 0:R // 2], KL[u][:, KVC + R // 2:P], const("lnsin", BT), MUL)
                    pool.tensor_tensor(kltmp[u][:, R // 2:R], KL[u][:, KVC:KVC + R // 2], const("lsin", BT),
                                       MUL).then_inc(s["kleft1"], 1)
                    pool.wait_ge(s["kleft1"], nth(i, u))
                    pool.tensor_tensor(KL[u][:, KVC:P], KL[u][:, P:P + R], kltmp[u][:], ADD).then_inc(s["kleft2"], 1)
                rstd(3)
                rstd(4)
                for u in U:
                    pool.wait_ge(s["qr2"], nth(i, u))
                    pool.tensor_tensor(QR[u][:, :, KVC:P], QR[u][:, :, KVC:P], QRt[u], ADD).then_inc(s["qrope"], 1)
                rstd(5)
                for u in U:
                    pool.wait_ge(s["gates"], nth(i, u, 3, 7))
                    pool.tensor_tensor(GL[u], const("incl").unsqueeze(1).to_broadcast([P, SH, S]),
                                       stat[u][:, 36:42].unsqueeze(2).to_broadcast([P, SH, S]), MUL).then_inc(s["gl"], 1)
                for u in U:
                    pool.wait_ge(s["dexp"], nth(i, u))
                    pool.tensor_tensor(DTI[u], DEX[u], const("incl").unsqueeze(1).to_broadcast([P, SH, S]),
                                       MUL)
                    pool.tensor_tensor(DTS[u], DEX[u], const("strict").unsqueeze(1).to_broadcast([P, SH, S]),
                                       MUL).then_inc(s["dts"], 1)
                for u in U:
                    pool.wait_ge(s["qkvn"], nth(i, u, 1, 4))
                    pool.tensor_tensor(stat[u][:, 12:24], stat[u][:, 0:12], mhalf[:], ALU.pow).then_inc(s["rn"], 1)

                def expand(u, dst, src, maskname, done):
                    pool.tensor_tensor(dst.rearrange("p h (b j) -> p h b j", b=BT)[:],
                                       src.unsqueeze(2).to_broadcast([P, SH, BT, S]),
                                       const(maskname).rearrange("p (b j) -> p b j", b=BT).unsqueeze(1)
                                       .to_broadcast([P, SH, BT, S]), MUL).then_inc(done, 1)

                for k, m in enumerate(LEVELS):
                    for u in U:
                        if k == 0:
                            pool.wait_ge(s["atp"], nth(i, u))
                        expand(u, ABD[m][u], ATP[u], f"off{m}", s["abd"])
                for u in U:
                    pool.wait_ge(s["pmp"], nth(i, u))
                    expand(u, PBD[u], PMP[u], "same", s["pbd"])
                for u in U:
                    pool.wait_ge(s["onorm"], nth(i, u, 1, 4))
                    pool.tensor_tensor(stat[u][:, 48:54], stat[u][:, 42:48], mhalf[:, 0:SH], ALU.pow).then_inc(s["orn"], 1)
                rstd(6)

        @block.tensor
        def _(pe):
            mm, tr = pe.matmul, pe.transpose

            def chunks(o, lhs, rhs, n):
                for c in range(n):
                    last = mm(o, lhs(c), rhs(c), start=c == 0, stop=c == n - 1)
                return last

            pe.wait_ge(s["ld_x0"], 16 * 11)
            for d in range(DC):
                last = chunks(PS[0][:, 0, d * D:(d + 1) * D], lambda c: Win_n[:, c, d * P:(d + 1) * P],
                              lambda c: WoutT[:, c], DC)
            last.then_inc(s["prep_ps"], 1)
            pe.wait_ge(s["binrep"], 1)
            chunks(PS[0][:, 1, 0:D], lambda c: binrep[:, c], lambda c: WoutT[:, c], DC).then_inc(s["prep_ps"], 1)
            pe.wait_ge(s["ld_xs"], 16 * 8)
            for h in range(XH):
                slot = h % 2 * 4 + h % 8 // 2
                last = mm(PS[1][0:QC, h // 8, slot * KVC:(slot + 1) * KVC], WuqT[:, h], WukT[:, h],
                          start=True, stop=True)
            last.then_inc(s["prep_ps"], 1)
            for c in range(DC):
                last = mm(PS[1][:, 2, c * R:(c + 1) * R], WkvcT[:, c * P:(c + 1) * P], Wkr, start=True, stop=True)
            last.then_inc(s["prep_ps"], 1)
            pe.wait_ge(s["prep_act"], 3)
            pe.wait_ge(s["biasrep"], 1)
            for h in range(XH):
                q = h % 2
                last = mm(PS[0][64 * q:64 * q + KVC, h // 4, (h // 2 % 2) * D:(h // 2 % 2 + 1) * D],
                          WuvT[:, h], Wo_x[:, h], start=True, stop=True)
            last.then_inc(s["prep_ps"], 1)
            pe.wait_ge(s["absum"], 1)
            mm(PS[1][:, 3, 0:3], ones[:, 0:P], small[:, 1:4], start=True, stop=True).then_inc(s["prep_ps"], 1)
            for sem, n in ((s["ld_a0"], 2), (s["ld_xw"], 1), (s["ld_s"], 5), (s["ld_m"], 4)):
                pe.wait_ge(sem, 16 * n)
            pe.wait_ge(s["prep_act"], 5)
            pe.wait_ge(s["prep_act"], 4)
            pe.wait_ge(s["q_scaled"], 1)
            pe.wait_ge(s["prep_pool"], 3)
            pe.wait_ge(s["ternary"], 3)

            with pe.Fori(0, ROUNDS) as i:
                def norm_T(k, need):
                    for u in U:
                        pe.wait_ge(s["ln_x"], nth(i, u, need, LNS))
                        for c in range(DC):
                            last = tr(PS[u][:, 3, c * P:(c + 1) * P], XN[u][:, c * P:(c + 1) * P], ident)
                        last.then_inc(s["lnT_ps"], 1)

                for u in U:
                    pe.wait_ge(ld_ctx[u], 32 * i + 32)
                    for b in range(BT):
                        for tc in range(2):
                            last = chunks(PS[u][:, b // 2, (b % 2 * 2 + tc) * P:(b % 2 * 2 + tc + 1) * P],
                                          lambda c: CT[u][:, c, b, tc * P:(tc + 1) * P], lambda c: WK[:, c], DC)
                    last
                    chunks(PS[u][0:BT, 2, 0:P], lambda c: CT[u][:, c, :, T - 1], lambda c: WK[:, c],
                           DC).then_inc(s["kleft_ps"], 1)
                for u in U:
                    pe.wait_ge(s["pooledrep"], nth(i, u))
                    chunks(PS[u][:, 3, 0:D], lambda c: crep[u][:, c], lambda c: Wc[:, c], DC).then_inc(s["residual_ps"], 1)
                norm_T(0, 2)
                for u in U:
                    pe.wait_ge(s["lnT"], nth(i, u, 0, 5))
                    pe.wait_ge(s["kleft"], nth(i, u))
                    pe.wait_ge(s["kleft"], nth(i, u))
                    chunks(PS[u][:, 0], lambda c: XNT[u][:, c], lambda c: Wqk0[:, c], DC)
                    for f in range(DC):
                        last = chunks(PS[u][:, 1, f * P:(f + 1) * P], lambda c: Wv0[:, c, f * P:(f + 1) * P],
                                      lambda c: XNT[u][:, c], DC)
                    last.then_inc(s["vT_ps"], 1)
                for u in U:
                    pe.wait_ge(s["vT"], nth(i, u))
                    pe.wait_ge(s["vT"], nth(i, u))
                    for b in range(BT):
                        rows = slice(b * S, (b + 1) * S)
                        for e in range(DC):
                            last = mm(PS[u][:, b, e * D:(e + 1) * D], QK0[u][rows, e * P:(e + 1) * P],
                                      QK0[u][rows, D:2 * D], start=True, stop=True)
                    last.then_inc(s["s0_ps"], 1)
                for u in U:
                    pe.wait_ge(s["e0"], nth(i, u))
                    for b in range(BT):
                        for f in range(DC):
                            for e in range(DC):
                                last = tr(PS[u][:, b, (f * DC + e) * P:(f * DC + e + 1) * P],
                                          E0[u][:, b * DC + e, f * P:(f + 1) * P], ident)
                    last.then_inc(s["at_ps"], 1)
                for u in U:
                    pe.wait_ge(s["at"], nth(i, u))
                    for b in range(BT):
                        for e in range(DC):
                            last = chunks(PS[u][:, 0, e * P + b * S:e * P + (b + 1) * S],
                                          lambda f: AT0[u][:, b * DC + f, e * P:(e + 1) * P],
                                          lambda f: VT0[u][:, f, b * S:(b + 1) * S], DC)
                    last.then_inc(s["av_ps"], 1)
                for u in U:
                    pe.wait_ge(s["attn0"], nth(i, u, 3, 4))
                    chunks(PS[u][:, 1, 0:D], lambda c: AV0[u][:, c], lambda c: Wo0[:, c], DC).then_inc(s["residual_ps"], 1)
                norm_T(1, 3)
                for u in U:
                    pe.wait_ge(s["lnT"], nth(i, u, 1, 5))
                    for k in range(2):
                        for f in range(FFC):
                            last = chunks(PS[u][:, 2 * k + f // 3, (f % 3) * P:(f % 3 + 1) * P],
                                          lambda c: W13[:, k, c, f * P:(f + 1) * P], lambda c: XNT[u][:, c], DC)
                    last.then_inc(s["f_ps"], 1)
                for u in U:
                    pe.wait_ge(s["ffn"], nth(i, u, 1, 2))
                    for f in range(FFC):
                        r = P if f < FFC - 1 else FFT
                        last = mm(PS[u][:, 0, 0:D], FG[u][0:r, f], W2[0:r, f], start=f == 0, stop=f == FFC - 1)
                    last.then_inc(s["residual_ps"], 1)
                for u in U:
                    pe.wait_ge(s["krope"], nth(i, u))
                    pe.wait_ge(s["kleft2"], nth(i, u))
                    pe.wait_ge(s["residual"], nth(i, u, 2, 6))
                    for k in range(BT * 2):
                        last = tr(PS[u][:, k // 4, (k % 4) * P:(k % 4 + 1) * P], KR[u][:, k], ident)
                    last
                    tr(PS[u][:, 2, 0:BT], KL[u][:, 0:P], ident[0:BT, 0:BT])
                    for b in range(BT):
                        last = mm(PS[u][:, 2, P + b * KVC:P + (b + 1) * KVC], const("pick", BT)[:, b * P:(b + 1) * P],
                                  KL[u][:, 0:KVC], start=True, stop=True)
                    last.then_inc(s["kleftT_ps"], 1)
                norm_T(2, 4)
                for u in U:
                    pe.wait_ge(s["lnT"], nth(i, u, 2, 5))
                    chunks(PS[u][0:QC, 3, 0:P], lambda c: Wdq[:, c], lambda c: XNT[u][:, c], DC).then_inc(s["qc_ps"], 1)
                for u in U:
                    pe.wait_ge(s["qc"], nth(i, u))
                    pe.wait_ge(s["kleftT"], nth(i, u))
                    pe.wait_ge(s["kleftT"], nth(i, u))
                    for g in range(4):
                        last = mm(PS[u][:, g], QCT[u], WQ[:, 4 * g:4 * g + 4], start=True, stop=True)
                    last.then_inc(s["q_ps"], 1)
                for u in U:
                    pe.wait_ge(s["qrope"], nth(i, u))
                    for h in range(XH):
                        last = tr(PS[u][:, h // 4, (h % 4) * P:(h % 4 + 1) * P], QR[u][:, h], ident)
                    last.then_inc(s["qT_ps"], 1)
                def scores(k, u):
                    b, pb = divmod(k, 2)
                    for q in range(2):
                        o = PS[u][:, q, 0:T]
                        mm(o, spread[:, b], mask[u][:], start=True, stop=False)
                        last = mm(o, QT[u][:, b, (2 * pb + q) * P:(2 * pb + q + 1) * P], KT[u][:, b],
                                  start=False, stop=True)
                    last.then_inc(s["s_ps"], 1)

                for u in U:
                    pe.wait_ge(s["qT"], nth(i, u))
                    pe.wait_ge(s["maskb"], nth(i, u))
                    scores(0, u)
                for k in range(STEPS):
                    b, pb = divmod(k, 2)
                    for u in U:
                        pe.wait_ge(s["e"], nth(i, u, k, STEPS))
                        for q in range(2):
                            for tc in range(2):
                                last = tr(PS[u][:, 2, (2 * q + tc) * P:(2 * q + tc + 1) * P],
                                          EX[u][k % 2][:, q, tc * P:(tc + 1) * P], ident)
                        last.then_inc(s["pT_ps"], 1)
                        if k + 1 < STEPS:
                            scores(k + 1, u)
                    for u in U:
                        pe.wait_ge(s["pT"], nth(i, u, k, STEPS))
                        if k > 0:
                            pe.wait_ge(s["oT"], nth(i, u, k - 1, STEPS))
                        for q in range(2):
                            last = chunks(PS[u][:, 3, q * KVC:(q + 1) * KVC], lambda tc: PT[u][:, 2 * q + tc],
                                          lambda tc: KR[u][:, 2 * b + tc, 0:KVC], 2)
                        last.then_inc(s["o_ps"], 1)
                    for u in U:
                        pe.wait_ge(s["oc"], nth(i, u, k, STEPS))
                        tr(PS[u][:, 3, P:2 * P], OC[u][k % 2], ident).then_inc(s["oT_ps"], 1)
                for u in U:
                    pe.wait_ge(s["oT"], nth(i, u, STEPS - 1, STEPS))
                    for hp in range(XH // 2):
                        last = mm(PS[u][:, 0, 0:D], OT[u][:, hp], WVO[:, hp],
                                  start=hp == 0, stop=hp == XH // 2 - 1)
                    last.then_inc(s["residual_ps"], 1)
                norm_T(3, 5)
                for u in U:
                    pe.wait_ge(s["lnT"], nth(i, u, 3, 5))
                    for f in range(QKVC):
                        last = chunks(PS[u][:, f // 3, (f % 3) * P:(f % 3 + 1) * P],
                                      lambda c: Wqkv[:, c, f * P:(f + 1) * P], lambda c: XNT[u][:, c], DC)
                    last.then_inc(s["cv_ps"], 1)
                    chunks(PS[u][:, 2, 0:SV + 2 * SH], lambda c: XNT[u][:, c], lambda c: Wgba[:, c],
                           DC).then_inc(s["gb_ps"], 1)
                for u in U:
                    pe.wait_ge(s["gl"], nth(i, u))
                    mm(PS[u][:, 3, 0:SH * S], const("later"), GL[u].rearrange("p h s -> p (h s)"),
                       start=True, stop=True).then_inc(s["dec_ps"], 1)
                for u in U:
                    pe.wait_ge(s["cv_u"], nth(i, u))
                    for f in range(QKVC):
                        r = P if f < QKVC - 1 else 3 * SV - (QKVC - 1) * P
                        last = tr(PS[u][:, f // 3, (f % 3) * P:(f % 3) * P + P][:, 0:r] if r < P else
                                  PS[u][:, f // 3, (f % 3) * P:(f % 3 + 1) * P],
                                  CTH[u][:, f, :][0:r], ident[0:r, 0:r])
                    last.then_inc(s["nat_ps"], 1)
                for u in U:
                    pe.wait_ge(s["qkvn"], nth(i, u, 3, 4))
                    nat = MID[u][:, 0:3 * SV + SV]
                    for g in range(2):
                        for k, o in enumerate((SV, 2 * SV, 0)):
                            j = 3 * g + k
                            last = tr(PS[u][:, j // 3, (j % 3) * P:(j % 3 + 1) * P],
                                      nat[:, o + g * P:o + (g + 1) * P], ident)
                    last.then_inc(s["kqT_ps"], 1)
                for u in U:
                    wait_apart(pe, (s["kqT"], nth(i, u)), (s["dexp"], nth(i, u)))
                    for h in range(SH):
                        r, g = h % 4, h // 4
                        rows = slice(r * SD, (r + 1) * SD)
                        for b in range(BT):
                            ts = slice(b * S, (b + 1) * S)
                            last = mm(PS[u][b * S:(b + 1) * S, r, g * 2 * S:(g + 1) * 2 * S],
                                      KQT[u][rows, 3 * g, ts], KQT[u][rows, 3 * g + 1:3 * g + 3, ts],
                                      start=True, stop=True, tile_position=(r * SD, b * S))
                    last.then_inc(s["gram_ps"], 1)

                def product(u, o, stationary, moving, done):
                    for h in range(SH):
                        last = mm(o[:, h * S:(h + 1) * S], stationary[:, h], moving[:, h], start=True, stop=True)
                    last.then_inc(done, 1)

                for k, m in enumerate(LEVELS[:-1]):
                    for u in U:
                        pe.wait_ge(s["abd"], nth(i, u, k, 4))
                        pe.wait_ge(s["t2inv"], nth(i, u, k, 4))
                        product(u, PS[u][:, 0], ABD[m][u], TP[u], s["lz_ps"])
                    for u in U:
                        pe.wait_ge(s["lz"], nth(i, u, k, 3))
                        pe.wait_ge(s["xbd"], nth(i, u, k, 4))
                        product(u, PS[u][:, 1], XBD[u], ZP[u], s["lt_ps"])
                for u in U:
                    pe.wait_ge(s["xbd"], nth(i, u, 3, 4))
                    product(u, PS[u][:, 0], XBD[u], BV[u], s["apply_ps"])
                for u in U:
                    pe.wait_ge(s["applied"], nth(i, u, 0, 2))
                    pe.wait_ge(s["abd"], nth(i, u, 3, 4))
                    product(u, PS[u][:, 1], ABD[LEVELS[-1]][u], WV[u], s["apply_ps"])
                for u in U:
                    pe.wait_ge(s["applied"], nth(i, u, 1, 2))
                    product(u, PS[u][:, 0], XBD[u], RV[u], s["apply_ps"])
                for u in U:
                    pe.wait_ge(s["uu"], nth(i, u))
                    pe.wait_ge(s["pbd"], nth(i, u))
                    product(u, PS[u][:, 1], PBD[u], UU[u], s["apply_ps"])
                for u in U:
                    pe.wait_ge(s["onorm"], nth(i, u, 3, 4))
                    on = ON[u].rearrange("p h d -> p (h d)")
                    tr(PS[u][:, 2, 0:P], on[:, 0:P], ident)
                    tr(PS[u][:, 2, P:2 * P], on[:, SV - P:SV], ident).then_inc(s["onT_ps"], 1)
                for u in U:
                    pe.wait_ge(s["onT"], nth(i, u))
                    mm(PS[u][:, 3, 0:D], ONT[u][:, 0], Wo1[:, 0], start=True, stop=False)
                    mm(PS[u][:, 3, 0:D], ONT[u][SV - P:P, 1], Wo1[SV - P:P, 1], start=False,
                       stop=True).then_inc(s["residual_ps"], 1)
                norm_T(4, 6)
                for u in U:
                    pe.wait_ge(s["lnT"], nth(i, u, 4, 5))
                    chunks(PS[u][:, 3, 0:NE], lambda c: XNT[u][:, c], lambda c: Wr[:, c], DC).then_inc(s["rt_ps"], 1)
                for k in range(2):
                    for u in U:
                        if k == 0:
                            pe.wait_ge(s["route"], nth(i, u, 0, 7))
                        else:
                            pe.wait_ge(s["m_g"], nth(i, u, 0, 2))
                        for j, Wm in enumerate((W1m, W2m)):
                            for q in range(2):
                                a = k * HALF + q * HALF // 2
                                last = chunks(PS[u][:, 2 * j + q, 0:HALF // 2], lambda c: XNT[u][:, c],
                                              lambda c: Wm[:, c, a:a + HALF // 2], DC)
                        last.then_inc(s["m_ps"], 1)
                for u in U:
                    pe.wait_ge(s["m_g"], nth(i, u, 1, 2))
                    for f in range(MHC):
                        last = tr(PS[u][:, f // 4, (f % 4) * P:(f % 4 + 1) * P], MG[u][:, f * P:(f + 1) * P], ident)
                    last.then_inc(s["gT_ps"], 1)
                for u in U:
                    pe.wait_ge(s["gT"], nth(i, u))
                    chunks(PS[u][:, 3, 0:D], lambda c: GT[u][:, c], lambda c: W3m[:, c], MHC).then_inc(s["residual_ps"], 1)

        @block.scalar
        def _(act):
            act.wait_ge(s["ld_x0"], 16 * 11)
            act.activation(small[:, 4:5], small[:, 0:1], ACT.Tanh, scale=0.5).then_inc(s["prep_act"], 1)
            act.activation(small[:, 8:8 + SH], small[:, 8:8 + SH], ACT.Exp).then_inc(s["prep_act"], 1)
            act.wait_ge(s["prep_ps"], 1)
            act.copy(Wc[:].rearrange("p c d -> p (c d)"), PS[0][:, 0]).then_inc(s["prep_act"], 1)
            act.wait_ge(s["prep_ps"], 4)
            act.copy(WK[:, :, KVC:P], PS[1][:, 2, 0:DC * R].rearrange("p (c r) -> p c r", c=DC)).then_inc(s["prep_act"], 1)
            act.wait_ge(s["prep_ps"], 5)
            act.copy(WVO[:].rearrange("p h d -> p (h d)"), PS[0][:].rearrange("p b n -> p (b n)")).then_inc(s["prep_act"], 1)

            with act.Fori(0, ROUNDS) as i:
                def norm_T(k):
                    for u in U:
                        act.wait_ge(s["lnT_ps"], nth(i, u, k, 5))
                        act.copy(XNT[u][:].rearrange("p c n -> p (c n)"), PS[u][:, 3, 0:D]).then_inc(s["lnT"], 1)

                for u in U:
                    act.wait_ge(s["kleft_ps"], nth(i, u))
                    act.copy(MID[u][:, 0:1024].rearrange("p (a b) -> p a b", a=2), PS[u][:, 0:2])
                    act.wait_ge(s["kleft_ps"], nth(i, u))
                    act.copy(KL[u][:, 0:P], PS[u][0:BT, 2, 0:P]).then_inc(s["kleft"], 1)
                norm_T(0)
                for u in U:
                    act.wait_ge(s["vT_ps"], nth(i, u))
                    act.copy(QK0[u], PS[u][:, 0])
                    act.wait_ge(s["vT_ps"], nth(i, u))
                    act.copy(XN[u][:], PS[u][:, 1, 0:D]).then_inc(s["vT"], 1)
                for u in U:
                    act.wait_ge(s["attn0"], nth(i, u, 1, 4))
                    for k in range(BT * DC):
                        last = act.activation(E0[u][:, k], PS[u][:, k // DC, (k % DC) * D:(k % DC + 1) * D], ACT.Exp,
                                              bias=stat[u][:, 8 + k:9 + k], scale=float(1 / np.sqrt(L0_HEAD)),
                                              accum_out=stat[u][:, 16 + k:17 + k])
                    last.then_inc(s["e0"], 1)
                for u in U:
                    act.wait_ge(s["at_ps"], nth(i, u))
                    act.copy(AT0[u].rearrange("p (a c) e -> p a (c e)", a=BT), PS[u][:]).then_inc(s["at"], 1)
                norm_T(1)
                for u in U:
                    act.wait_ge(s["f_ps"], nth(i, u))
                    act.activation(FT[u], PS[u][:, 0:2, 0:3 * P], ACT.Tanh, scale=0.5).then_inc(s["f_tanh"], 1)
                for u in U:
                    act.wait_ge(s["kleftT_ps"], nth(i, u))
                    act.copy(KT[u][:, :, 0:2 * P], PS[u][:, 0:2].rearrange("p a (b n) -> p (a b) n", b=2))
                    act.wait_ge(s["kleftT_ps"], nth(i, u))
                    act.copy(KT[u][:, :, T - 1:T], PS[u][:, 2, 0:BT].unsqueeze(2))
                    act.copy(VL[u].rearrange("p b n -> p (b n)"), PS[u][:, 2, P:P + BT * KVC]).then_inc(s["kleftT"], 1)
                norm_T(2)
                for u in U:
                    act.wait_ge(s["qc_ps"], nth(i, u))
                    act.copy(QCT[u], PS[u][0:QC, 3, 0:P]).then_inc(s["qc"], 1)
                for u in U:
                    act.wait_ge(s["q_ps"], nth(i, u))
                    act.copy(QR[u][:, :, 0:KVC], PS[u][:].rearrange("p g (h d) -> p (g h) d", d=P)[:, :, 0:KVC]).then_inc(s["qlat"], 1)
                for u in U:
                    act.wait_ge(s["qT_ps"], nth(i, u))
                    act.copy(QT[u].rearrange("p b (h s) -> p h b s", s=S),
                             PS[u][:].rearrange("p g (h b s) -> p (g h) b s", b=BT, s=S)).then_inc(s["qT"], 1)
                for k in range(STEPS):
                    for u in U:
                        act.wait_ge(s["s_max"], nth(i, u, k, STEPS))
                        if k > 1:
                            act.wait_ge(s["oc"], nth(i, u, k - 2, STEPS))
                        for q in range(2):
                            m = 4 * (k % 2) + q
                            last = act.activation(EX[u][k % 2][:, q], PS[u][:, q, 0:T], ACT.Exp,
                                                  bias=stat[u][:, m:m + 1], accum_out=stat[u][:, m + 2:m + 3])
                        last.then_inc(s["e"], 1)
                    for u in U:
                        act.wait_ge(s["oT_ps"], nth(i, u, k, STEPS))
                        b, pb = divmod(k, 2)
                        act.copy(OT[u][:, 4 * pb:4 * pb + 4, b * S:(b + 1) * S],
                                 PS[u][:, 3, P:2 * P].rearrange("p (j s) -> p j s", s=S)).then_inc(s["oT"], 1)
                norm_T(3)
                for u in U:
                    act.wait_ge(s["gb_ps"], nth(i, u))
                    act.copy(GB[u], PS[u][:, 2, 0:SV + 2 * SH])
                    act.activation(GTH[u], PS[u][:, 2, 0:SV + 2 * SH], ACT.Tanh, scale=0.5).then_inc(s["g_tanh"], 1)
                for u in U:
                    act.wait_ge(s["gates"], nth(i, u, 1, 7))
                    act.activation(stat[u][:, 30:36], stat[u][:, 30:36], ACT.Exp).then_inc(s["softplus"], 1)
                for u in U:
                    act.wait_ge(s["softplus"], nth(i, u, 0, 2))
                    act.activation(stat[u][:, 30:36], stat[u][:, 30:36], ACT.Ln, bias=1.0).then_inc(s["softplus"], 1)
                for u in U:
                    act.wait_ge(s["dec_ps"], nth(i, u))
                    act.activation(DEX[u].rearrange("p h s -> p (h s)"), PS[u][:, 3, 0:SH * S], ACT.Exp).then_inc(s["dexp"], 1)
                for u in U:
                    act.wait_ge(s["conv"], nth(i, u, CK - 1, CK))
                    act.activation(CTH[u], CY[u], ACT.Tanh, scale=0.5).then_inc(s["cv_tanh"], 1)
                for u in U:
                    act.wait_ge(s["nat_ps"], nth(i, u))
                    act.copy(QKVN[u].rearrange("p h d -> p (h d)")[:, 0:3 * P], PS[u][:, 0, 0:3 * P])
                    act.copy(QKVN[u].rearrange("p h d -> p (h d)")[:, 3 * P:3 * SV], PS[u][:, 1, 0:3 * SV - 3 * P]).then_inc(s["natural"], 1)
                for u in U:
                    act.wait_ge(s["natural"], nth(i, u, 0, 2))
                    act.activation(SQ[u], QKVN[u][:, 0:2 * SH], ACT.Square).then_inc(s["natural"], 1)
                for u in U:
                    act.wait_ge(s["kqT_ps"], nth(i, u))
                    act.copy(KQT[u].rearrange("p (a b) n -> p a (b n)", a=2), PS[u][:, 0:2, 0:3 * P]).then_inc(s["kqT"], 1)
                for k in range(3):
                    for u in U:
                        act.wait_ge(s["lz_ps"], nth(i, u, k, 3))
                        act.copy(ZP[u].rearrange("p h s -> p (h s)"), PS[u][:, 0, 0:SH * S]).then_inc(s["lz"], 1)
                for u in U:
                    act.wait_ge(s["apply_ps"], nth(i, u, 0, 4))
                    act.copy(WV[u].rearrange("p h s -> p (h s)"), PS[u][:, 0, 0:SH * S]).then_inc(s["applied"], 1)
                for u in U:
                    act.wait_ge(s["apply_ps"], nth(i, u, 1, 4))
                    act.copy(RV[u].rearrange("p h s -> p (h s)"), PS[u][:, 1, 0:SH * S]).then_inc(s["applied"], 1)
                for u in U:
                    act.wait_ge(s["apply_ps"], nth(i, u, 3, 4))
                    act.activation(OSQ[u].rearrange("p h s -> p (h s)"), PS[u][:, 1, 0:SH * S], ACT.Square).then_inc(s["osq"], 1)
                for u in U:
                    act.wait_ge(s["onT_ps"], nth(i, u))
                    act.copy(ONT[u].rearrange("p a n -> p (a n)"), PS[u][:, 2, 0:2 * P]).then_inc(s["onT"], 1)
                norm_T(4)
                for u in U:
                    act.wait_ge(s["rdiff"], nth(i, u))
                    act.activation(stat[u][:, 25:26], stat[u][:, 24:25], ACT.Tanh, scale=0.5).then_inc(s["rtanh"], 1)
                for k in range(2):
                    for u in U:
                        act.wait_ge(s["m_ps"], nth(i, u, k, 2))
                        act.activation(MT[u], PS[u][:, 0:2, 0:HALF // 2], ACT.Tanh, scale=0.5).then_inc(s["m_tanh"], 1)
                for u in U:
                    act.wait_ge(s["gT_ps"], nth(i, u))
                    act.copy(GT[u].rearrange("p c n -> p (c n)"), PS[u][:].rearrange("p b n -> p (b n)")[:, 0:MH]).then_inc(s["gT"], 1)

        @block.vector
        def _(dve):
            steps = [0]

            def then(ins):
                steps[0] += 1
                ins.then_inc(s["prep_dve"], 1)
                dve.wait_ge(s["prep_dve"], steps[0])

            dve.memset(kfill, 1.0 / T)
            then(dve.memset(ones, 1.0))
            dve.wait_ge(s["prep_act"], 1)
            then(dve.tensor_scalar(small[:, 5:6], small[:, 4:5], 0.5, 0.5, MUL, ADD))
            then(dve.tensor_scalar(coef[:], ones, small[:, 5:6], None, MUL))
            then(dve.tensor_tensor_scan(crev, coef[:], kfill, 0.0, MUL, ADD))
            dve.tensor_copy(coef[:], crev[:, ::-1])
            then(dve.reduce_sum(small[:, 6:7], crev, AX.X))
            then(dve.tensor_scalar(small[:, 14:16], binc, small[:, 6:7], None, MUL))
            dve.tensor_copy(binrep, small[:, 14:16].unsqueeze(2).to_broadcast([P, DC, P])).then_inc(s["binrep"], 1)
            dve.wait_ge(s["prep_ps"], 2)
            dve.tensor_tensor(biasrep[:], PS[0][:, 1, 0:D], boutrep, ADD).then_inc(s["biasrep"], 1)
            dve.wait_ge(s["prep_act"], 2)
            dve.tensor_scalar(nega[:], small[:, 8:8 + SH], -1.0, None, MUL).then_inc(s["neg_a"], 1)
            scale = float(1.0 / np.sqrt(np.float32(HD + R)))
            dve.wait_ge(s["prep_ps"], 3)
            dve.tensor_scalar(WQ[:, :, 0:KVC], PS[1][0:QC, 0:2].rearrange("p a (h d) -> p (a h) d", d=KVC), scale,
                              None, MUL)
            dve.wait_ge(s["ld_xs"], 16 * 8)
            for half in range(2):
                last = dve.tensor_scalar(WQ[:, 8 * half:8 * half + 8, KVC:P].rearrange("p (q j) r -> p j q r", q=2),
                                         Wqr[:, 8 * half:8 * half + 8].rearrange("p (j q) r -> p j q r", q=2), scale,
                                         None, MUL)
            last.then_inc(s["q_scaled"], 1)
            dve.wait_ge(s["ld_f0"], 16 * 4)
            dve.wait_ge(s["prep_pool"], 1)
            mats = [W13[:, 0].rearrange("p c n -> p (c n)"), W13[:, 1].rearrange("p c n -> p (c n)"),
                    W2[:].rearrange("p c n -> p (c n)")]
            for k, m in enumerate(mats):
                last = dve.tensor_reduce(small[:, 1 + k:2 + k], m, AX.X, ADD, apply_absolute_value=True)
            last.then_inc(s["absum"], 1)
            dve.wait_ge(s["prep_ps"], 6)
            then(dve.tensor_scalar(stat[0][:, 0:3], PS[1][:, 3, 0:3], 1.0 / (FF * D), None, MUL))
            dve.tensor_scalar(stat[0][:, 3:6], stat[0][:, 0:3], 0.5, None, MUL)
            then(dve.tensor_scalar(stat[0][:, 6:9], stat[0][:, 0:3], -0.5, None, MUL))
            for k, m in enumerate(mats):
                sc = stat[0][:, k:k + 1]
                dve.tensor_scalar(quant[0], m, stat[0][:, 3 + k:4 + k], sc, ALU.is_gt, MUL)
                then(dve.tensor_scalar(quant[1], m, stat[0][:, 6 + k:7 + k], sc, ALU.is_lt, MUL))
                then(dve.tensor_tensor(quant[0], quant[0], quant[1], SUB))
                then(dve.tensor_tensor(quant[0], quant[0], m, SUB))
                dve.tensor_tensor(m, m, quant[0], ADD).then_inc(s["ternary"], 1)
                dve.wait_ge(s["ternary"], k + 1)

            with dve.Fori(0, ROUNDS) as i:
                def norm(k, src, src_sem, which=0, n=1):
                    for u in U:
                        if src_sem is None:
                            dve.wait_ge(ld_xin[u], 16 * i + 16)
                        else:
                            dve.wait_ge(src_sem, nth(i, u, which, n))
                        dve.bn_stats(st[u][:], src[u]).then_inc(s["ln_stats"], 1)
                    for u in U:
                        wait_apart(dve, (s["ln_stats"], nth(i, u, k, LNS)))
                        dve.bn_aggr(mv[u][:], st[u][:]).then_inc(s["ln_mv"], 1)
                    for u in U:
                        dve.wait_ge(s["ln_mv"], nth(i, u, k, LNS))
                        dve.tensor_scalar(ve[u][:, 0:1], mv[u][:, 1:2], EPS, None, ADD).then_inc(s["ln_var"], 1)
                    for u in U:
                        dve.wait_ge(s["ln_rstd"], nth(i, u, k, LNS))
                        if k == 0:
                            dve.wait_ge(stored[u], 16 * i + 16)
                        dve.tensor_scalar(XN[u][:], src[u], mv[u][:, 0:1], ve[u][:, 1:2], SUB, MUL).then_inc(s["ln_x"], 1)

                for u in U:
                    dve.wait_ge(ld_ctx[u], 32 * i + 32)
                    for c in range(DC):
                        for b in range(BT):
                            k = c * BT + b
                            last = dve.tensor_tensor_reduce(prod[u][:, k], CT[u][:, c, b], coef[:], 1.0, 0.0, MUL, ADD,
                                                            pooled[u][:, k:k + 1])
                    last.then_inc(s["pool_terms"], 1)
                for u in U:
                    dve.wait_ge(s["pool_terms"], nth(i, u))
                    dve.tensor_copy(crep[u].rearrange("p c b s -> p (c b) s"),
                                    pooled[u][:].unsqueeze(2).to_broadcast([P, DC * BT, S])).then_inc(s["pooledrep"], 1)
                norm(0, [xin[u][:] for u in U], None)
                for u in U:
                    dve.wait_ge(s["residual_ps"], nth(i, u, 0, 6))
                    dve.wait_ge(s["ln_x"], nth(i, u, 0, LNS))
                    dve.tensor_tensor(ytmp[u], XN[u][:], biasrep[:], ADD).then_inc(s["ysum"], 1)
                for u in U:
                    dve.wait_ge(s["ysum"], 4 * i + u + 1)
                    dve.tensor_tensor(ytmp[u], ytmp[u], PS[u][:, 3, 0:D], ADD).then_inc(s["ysum"], 1)
                norm(1, ytmp, s["ysum"], 1, 2)
                for u in U:
                    dve.wait_ge(s["ln_x"], nth(i, u, 1, LNS))
                    dve.tensor_tensor(ytmp[u], XN[u][:], gamma[:], MUL).then_inc(s["gammad"], 1)
                for u in U:
                    dve.wait_ge(s["gammad"], 4 * i + u + 1)
                    dve.tensor_tensor(ytmp[u], ytmp[u], beta[:], ADD).then_inc(s["gammad"], 1)
                for u in U:
                    dve.wait_ge(s["gammad"], 4 * i + 2 + u + 1)
                    dve.tensor_tensor(X[u][:], ytmp[u], xin[u][:], ADD).then_inc(s["residual"], 1)
                norm(2, [X[u][:] for u in U], s["residual"], 0, 6)
                for u in U:
                    dve.wait_ge(s["s0_ps"], nth(i, u))
                    dve.reduce_max(stat[u][:, 0:8], PS[u][:].rearrange("p b (e f) -> p (b e) f", e=DC), AX.X,
                                   negate=True).then_inc(s["attn0"], 1)
                for u in U:
                    dve.wait_ge(s["attn0"], nth(i, u, 0, 4))
                    dve.tensor_scalar(stat[u][:, 8:16], stat[u][:, 0:8], float(1 / np.sqrt(L0_HEAD)), None,
                                      MUL).then_inc(s["attn0"], 1)
                for u in U:
                    dve.wait_ge(s["e0"], nth(i, u))
                    dve.reciprocal(stat[u][:, 24:32], stat[u][:, 16:24]).then_inc(s["attn0"], 1)
                for u in U:
                    dve.wait_ge(s["attn0"], nth(i, u, 2, 4))
                    dve.wait_ge(s["av_ps"], nth(i, u))
                    for e in range(DC):
                        last = dve.tensor_tensor(
                            AV0[u][:, e].rearrange("p (b s) -> p b s", b=BT),
                            PS[u][:, 0, e * P:(e + 1) * P].rearrange("p (b s) -> p b s", b=BT),
                            stat[u][:, 24 + e:32:2].unsqueeze(2).to_broadcast([P, BT, S]), MUL)
                    last.then_inc(s["attn0"], 1)
                for u in U:
                    dve.wait_ge(s["residual_ps"], nth(i, u, 1, 6))
                    dve.tensor_tensor(X[u][:], X[u][:], PS[u][:, 1, 0:D], ADD).then_inc(s["residual"], 1)
                norm(3, [X[u][:] for u in U], s["residual"], 1, 6)
                for u in U:
                    dve.wait_ge(s["f_tanh"], nth(i, u))
                    dve.scalar_tensor_tensor(FU[u], FT[u], 1.0, PS[u][:, 0:2, 0:3 * P], ADD, MUL).then_inc(s["ffn"], 1)
                for u in U:
                    dve.wait_ge(s["ffn"], nth(i, u, 0, 2))
                    dve.scalar_tensor_tensor(FG[u].rearrange("p (a c) n -> p a (c n)", a=2), FU[u], 0.5,
                                             PS[u][:, 2:4, 0:3 * P], MUL, MUL).then_inc(s["ffn"], 1)
                for u in U:
                    dve.wait_ge(s["residual_ps"], nth(i, u, 2, 6))
                    dve.tensor_tensor(X[u][:], X[u][:], PS[u][:, 0, 0:D], ADD).then_inc(s["residual"], 1)
                norm(4, [X[u][:] for u in U], s["residual"], 2, 6)
                for u in U:
                    dve.wait_ge(s["qlat"], nth(i, u))
                    q = PS[u][:].rearrange("p g (h d) -> p (g h) d", d=P)
                    dve.tensor_tensor(QR[u][:, :, KVC:P], q[:, :, KVC:P],
                                      const("qcos").unsqueeze(1).to_broadcast([P, XH, R]), MUL)
                    dve.tensor_tensor(QRt[u][:, :, 0:R // 2], q[:, :, KVC + R // 2:P],
                                      const("qnsin").unsqueeze(1).to_broadcast([P, XH, R // 2]), MUL)
                    dve.tensor_tensor(QRt[u][:, :, R // 2:R], q[:, :, KVC:KVC + R // 2],
                                      const("qsin").unsqueeze(1).to_broadcast([P, XH, R // 2]), MUL).then_inc(s["qr2"], 1)
                def maxima(k, u):
                    dve.wait_ge(s["s_ps"], nth(i, u, k, STEPS))
                    m = 4 * (k % 2)
                    dve.reduce_max(stat[u][:, m:m + 2], PS[u][:, 0:2, 0:T], AX.X, negate=True).then_inc(s["s_max"], 1)

                for u in U:
                    maxima(0, u)
                for k in range(STEPS):
                    m = 4 * (k % 2)
                    for u in U:
                        dve.wait_ge(s["pT_ps"], nth(i, u, k, STEPS))
                        dve.tensor_copy(PT[u].rearrange("p a n -> p (a n)"), PS[u][:, 2]).then_inc(s["pT"], 1)
                        dve.reciprocal(stat[u][:, 8 + m:10 + m], stat[u][:, m + 2:m + 4]).then_inc(s["o_rinv"], 1)
                    if k + 1 < STEPS:
                        for u in U:
                            maxima(k + 1, u)
                    for u in U:
                        dve.wait_ge(s["o_ps"], nth(i, u, k, STEPS))
                        for q in range(2):
                            last = dve.scalar_tensor_tensor(OC[u][k % 2][:, q * KVC:(q + 1) * KVC], VL[u][:, k // 2],
                                                            EX[u][k % 2][:, q, T - 1:T],
                                                            PS[u][:, 3, q * KVC:(q + 1) * KVC], MUL, ADD)
                        last.then_inc(s["o_left"], 1)
                    for u in U:
                        dve.wait_ge(s["o_left"], nth(i, u, k, STEPS))
                        dve.wait_ge(s["o_rinv"], nth(i, u, k, STEPS))
                        oc = OC[u][k % 2].rearrange("p (q d) -> p q d", q=2)
                        dve.tensor_tensor(oc, oc, stat[u][:, 8 + m:10 + m].unsqueeze(2).to_broadcast([P, 2, KVC]),
                                          MUL).then_inc(s["oc"], 1)
                for u in U:
                    dve.wait_ge(s["residual_ps"], nth(i, u, 3, 6))
                    dve.tensor_tensor(X[u][:], X[u][:], PS[u][:, 0, 0:D], ADD).then_inc(s["residual"], 1)
                for u in U:
                    dve.wait_ge(s["residual"], nth(i, u, 3, 6))
                    dve.memset(CX[u][:, :, :, 0:CK - 1], 0.0).then_inc(s["cv_pad"], 1)
                norm(5, [X[u][:] for u in U], s["residual"], 3, 6)
                for u in U:
                    dve.wait_ge(s["cv_ps"], nth(i, u))
                    dve.tensor_copy(CX[u][:, 0:3, :, CK - 1:], PS[u][:, 0, 0:3 * P].rearrange("p (c b s) -> p c b s", c=3, b=BT))
                    dve.tensor_copy(CX[u][:, 3:5, :, CK - 1:], PS[u][:, 1, 0:2 * P].rearrange("p (c b s) -> p c b s", c=2, b=BT)).then_inc(s["cvx"], 1)
                for u in U:
                    dve.wait_ge(s["g_tanh"], nth(i, u))
                    dve.tensor_tensor(stat[u][:, 24:30], GB[u][:, SV + SH:SV + 2 * SH], dtb[:], ADD).then_inc(s["gates"], 1)
                for u in U:
                    dve.wait_ge(s["gates"], nth(i, u, 0, 7))
                    dve.scalar_tensor_tensor(stat[u][:, 30:36], stat[u][:, 24:30], -1.0, stat[u][:, 24:30], MUL, ALU.min)
                    dve.tensor_scalar(stat[u][:, 54:60], stat[u][:, 24:30], 0.0, None, ALU.max).then_inc(s["gates"], 1)
                for u in U:
                    dve.wait_ge(s["gates"], nth(i, u, 1, 7))
                    dve.wait_ge(s["softplus"], nth(i, u, 1, 2))
                    dve.tensor_tensor(stat[u][:, 36:42], stat[u][:, 30:36], stat[u][:, 54:60], ADD).then_inc(s["gates"], 1)
                for u in U:
                    dve.wait_ge(s["gates"], nth(i, u, 2, 7))
                    dve.wait_ge(s["neg_a"], 1)
                    dve.tensor_tensor(stat[u][:, 36:42], stat[u][:, 36:42], nega[:], MUL).then_inc(s["gates"], 1)
                for u in U:
                    dve.wait_ge(s["g_tanh"], nth(i, u))
                    dve.tensor_scalar(stat[u][:, 24:30], GTH[u][:, SV:SV + SH], 0.5, 0.5, MUL, ADD)
                    dve.tensor_scalar(stat[u][:, 30:36], GTH[u][:, SV:SV + SH], 0.25, 0.25, MUL, ADD).then_inc(s["gates"], 1)
                for u in U:
                    dve.scalar_tensor_tensor(GS[u].rearrange("p h d -> p (h d)"), GTH[u][:, 0:SV], 1.0, GB[u][:, 0:SV],
                                             ADD, MUL).then_inc(s["gates"], 1)
                for u in U:
                    dve.wait_ge(s["gates"], nth(i, u, 5, 7))
                    dve.tensor_tensor(GS[u], GS[u], onw[:].unsqueeze(1).to_broadcast([P, SH, SD]), MUL).then_inc(s["gates"], 1)
                for k in range(CK):
                    for u in U:
                        if k == 0:
                            dve.wait_ge(s["cvx"], nth(i, u))
                            dve.wait_ge(s["cv_pad"], nth(i, u))
                        else:
                            dve.wait_ge(s["conv"], nth(i, u, k - 1, CK))
                        for c in range(QKVC):
                            y = CY[u][:, c].rearrange("p (b s) -> p b s", b=BT)
                            src = CX[u][:, c, :, k:k + S]
                            if k == 0:
                                last = dve.tensor_scalar(y, src, convw[:, c, k:k + 1], None, MUL)
                            else:
                                last = dve.scalar_tensor_tensor(y, src, convw[:, c, k:k + 1], y, MUL, ADD)
                        last.then_inc(s["conv"], 1)
                for u in U:
                    dve.wait_ge(s["cv_tanh"], nth(i, u))
                    dve.scalar_tensor_tensor(CTH[u], CTH[u], 1.0, CY[u], ADD, MUL).then_inc(s["cv_u"], 1)
                for u in U:
                    dve.wait_ge(s["natural"], nth(i, u, 1, 2))
                    dve.reduce_sum(stat[u][:, 0:12], SQ[u], AX.X).then_inc(s["qkvn"], 1)
                for u in U:
                    dve.wait_ge(s["qkvn"], nth(i, u, 0, 4))
                    dve.tensor_scalar(stat[u][:, 0:6], stat[u][:, 0:6], 4e-6, float(SD), ADD, MUL)
                    dve.tensor_scalar(stat[u][:, 6:12], stat[u][:, 6:12], 4e-6, None, ADD).then_inc(s["qkvn"], 1)
                for u in U:
                    dve.wait_ge(s["rn"], nth(i, u))
                    dve.tensor_tensor(NAT[u][:, 0:2 * SH], QKVN[u][:, 0:2 * SH],
                                      stat[u][:, 12:24].unsqueeze(2).to_broadcast([P, 2 * SH, SD]), MUL).then_inc(s["qkvn"], 1)
                for u in U:
                    dve.wait_ge(s["qkvn"], nth(i, u, 2, 4))
                    dve.wait_ge(s["gates"], nth(i, u, 4, 7))
                    dve.tensor_tensor(NAT[u][:, 2 * SH:3 * SH], NAT[u][:, SH:2 * SH],
                                      stat[u][:, 24:30].unsqueeze(2).to_broadcast([P, SH, SD]), MUL)
                    dve.tensor_tensor(BV[u], QKVN[u][:, 2 * SH:3 * SH],
                                      stat[u][:, 30:36].unsqueeze(2).to_broadcast([P, SH, SD]), MUL).then_inc(s["qkvn"], 1)
                for u in U:
                    dve.wait_ge(s["gram_ps"], nth(i, u))
                    dve.wait_ge(s["dts"], nth(i, u))
                    dve.wait_ge(s["dts"], nth(i, u))
                    for g, n in ((0, 4), (1, 2)):
                        last = dve.tensor_tensor(ATP[u][:, 4 * g:4 * g + n], PS[u][:, 0:n, 2 * g * S:(2 * g + 1) * S],
                                                 DTS[u][:, 4 * g:4 * g + n], MUL)
                    last.then_inc(s["atp"], 1)
                    for g, n in ((0, 4), (1, 2)):
                        last = dve.tensor_tensor(PMP[u][:, 4 * g:4 * g + n], PS[u][:, 0:n, (2 * g + 1) * S:(2 * g + 2) * S],
                                                 DTI[u][:, 4 * g:4 * g + n], MUL)
                    last.then_inc(s["pmp"], 1)
                for u in U:
                    dve.wait_ge(s["atp"], nth(i, u))
                    dve.tensor_tensor(XP[u], ATP[u], const("off1").unsqueeze(1).to_broadcast([P, SH, S]), MUL).then_inc(s["tri"], 1)
                for u in U:
                    dve.wait_ge(s["tri"], nth(i, u, 0, 2))
                    dve.tensor_tensor(XP[u], const("eye").unsqueeze(1).to_broadcast([P, SH, S]), XP[u], SUB).then_inc(s["tri"], 1)

                def expand_x(k):
                    for u in U:
                        dve.tensor_tensor(XBD[u].rearrange("p h (b j) -> p h b j", b=BT),
                                          XP[u].unsqueeze(2).to_broadcast([P, SH, BT, S]),
                                          const("same").rearrange("p (b j) -> p b j", b=BT).unsqueeze(1)
                                          .to_broadcast([P, SH, BT, S]), MUL).then_inc(s["xbd"], 1)

                for u in U:
                    dve.wait_ge(s["tri"], nth(i, u, 1, 2))
                    dve.transpose(TP[u].rearrange("p h s -> p (h s)"), XP[u].rearrange("p h s -> p (h s)")).then_inc(s["t2inv"], 1)
                expand_x(0)
                for k in range(3):
                    for u in U:
                        dve.wait_ge(s["lt_ps"], nth(i, u, k, 3))
                        if k == 0:
                            dve.wait_ge(s["t2inv"], nth(i, u, 0, 4))
                        dve.tensor_tensor(TP[u].rearrange("p h s -> p (h s)"), TP[u].rearrange("p h s -> p (h s)"),
                                          PS[u][:, 1, 0:SH * S], SUB).then_inc(s["t2inv"], 1)
                    for u in U:
                        dve.wait_ge(s["t2inv"], nth(i, u, k + 1, 4))
                        dve.transpose(XP[u].rearrange("p h s -> p (h s)"), TP[u].rearrange("p h s -> p (h s)")).then_inc(s["xnew"], 1)
                    for u in U:
                        dve.wait_ge(s["xnew"], nth(i, u, k, 3))
                    expand_x(k + 1)
                for u in U:
                    dve.wait_ge(s["apply_ps"], nth(i, u, 2, 4))
                    dve.tensor_tensor(UU[u].rearrange("p h s -> p (h s)"), WV[u].rearrange("p h s -> p (h s)"),
                                      PS[u][:, 0, 0:SH * SD], SUB).then_inc(s["uu"], 1)
                for u in U:
                    dve.wait_ge(s["osq"], nth(i, u))
                    dve.reduce_sum(stat[u][:, 42:48], OSQ[u], AX.X).then_inc(s["onorm"], 1)
                for u in U:
                    dve.wait_ge(s["onorm"], nth(i, u, 0, 4))
                    dve.tensor_scalar(stat[u][:, 42:48], stat[u][:, 42:48], 1.0 / SD, EPS, MUL, ADD).then_inc(s["onorm"], 1)
                for u in U:
                    dve.wait_ge(s["gates"], nth(i, u, 6, 7))
                    dve.tensor_tensor(ON[u], PS[u][:, 1, 0:SV].rearrange("p (h d) -> p h d", h=SH), GS[u], MUL).then_inc(s["onorm"], 1)
                for u in U:
                    dve.wait_ge(s["onorm"], nth(i, u, 2, 4))
                    dve.wait_ge(s["orn"], nth(i, u))
                    dve.scalar_tensor_tensor(ON[u], ON[u], 0.5, stat[u][:, 48:54].unsqueeze(2).to_broadcast([P, SH, SD]),
                                             MUL, MUL).then_inc(s["onorm"], 1)
                for u in U:
                    dve.wait_ge(s["residual_ps"], nth(i, u, 4, 6))
                    dve.tensor_tensor(X[u][:], X[u][:], PS[u][:, 3, 0:D], ADD).then_inc(s["residual"], 1)
                norm(6, [X[u][:] for u in U], s["residual"], 4, 6)
                for u in U:
                    dve.wait_ge(s["rt_ps"], nth(i, u))
                    dve.tensor_copy(stat[u][:, 0:8], PS[u][:, 3, 0:NE]).then_inc(s["route"], 1)
                for u in U:
                    wait_apart(dve, (s["route"], nth(i, u, 0, 7)))
                    dve.max(stat[u][:, 8:16], stat[u][:, 0:8]).then_inc(s["route"], 1)
                for u in U:
                    wait_apart(dve, (s["route"], nth(i, u, 1, 7)))
                    dve.max_index(oidx[u][:], stat[u][:, 8:16], stat[u][:, 0:8]).then_inc(s["route"], 1)
                    dve.tensor_tensor(stat[u][:, 24:25], stat[u][:, 8:9], stat[u][:, 9:10], SUB).then_inc(s["rdiff"], 1)
                for u in U:
                    dve.wait_ge(s["route"], nth(i, u, 2, 7))
                    dve.tensor_copy(stat[u][:, 16:24], oidx[u][:]).then_inc(s["route"], 1)
                for u in U:
                    dve.wait_ge(s["rtanh"], nth(i, u))
                    dve.tensor_scalar(stat[u][:, 26:27], stat[u][:, 25:26], 0.25, 0.25, MUL, ADD)
                    dve.tensor_scalar(stat[u][:, 27:28], stat[u][:, 25:26], -0.25, 0.25, MUL, ADD).then_inc(s["route"], 1)
                for u in U:
                    dve.wait_ge(s["route"], nth(i, u, 3, 7))
                    dve.wait_ge(s["route"], nth(i, u, 4, 7))
                    dve.tensor_scalar(stat[u][:, 32:40], const("iota"), stat[u][:, 16:17], stat[u][:, 26:27],
                                      ALU.is_equal, MUL)
                    dve.tensor_scalar(stat[u][:, 40:48], const("iota"), stat[u][:, 17:18], stat[u][:, 27:28],
                                      ALU.is_equal, MUL).then_inc(s["route"], 1)
                for u in U:
                    dve.wait_ge(s["route"], nth(i, u, 5, 7))
                    dve.tensor_tensor(stat[u][:, 48:56], stat[u][:, 32:40], stat[u][:, 40:48], ADD).then_inc(s["route"], 1)
                for k in range(2):
                    for u in U:
                        dve.wait_ge(s["m_tanh"], nth(i, u, k, 2))
                        dve.scalar_tensor_tensor(MU[u], MT[u], 1.0, PS[u][:, 0:2, 0:HALF // 2], ADD, MUL).then_inc(s["m_u"], 1)
                    for u in U:
                        dve.wait_ge(s["m_u"], nth(i, u, k, 2))
                        dve.wait_ge(s["route"], nth(i, u, 6, 7))
                        for e in range(4):
                            cols = slice(e % 2 * EH, (e % 2 + 1) * EH)
                            a = k * HALF + e * EH
                            last = dve.scalar_tensor_tensor(MG[u][:, a:a + EH], MU[u][:, e // 2, cols],
                                                            stat[u][:, 48 + 4 * k + e:49 + 4 * k + e],
                                                            PS[u][:, 2 + e // 2, cols], MUL, MUL)
                        last.then_inc(s["m_g"], 1)
                for u in U:
                    dve.wait_ge(s["residual_ps"], nth(i, u, 5, 6))
                    dve.tensor_tensor(XN[u][:], X[u][:], PS[u][:, 3, 0:D], ADD).then_inc(s["residual"], 1)


_WEIGHTS = ["W_in", "W_outT", "b_in", "b_out", "gamma", "beta", "decay", "dt_bias", "A_log", "o_norm", "Wqk0", "Wv0",
            "Wo0", "w1T", "w3T", "w2T", "W_kvc", "W_kvcT", "W_dq", "W_uqT", "W_qr", "W_ukT", "W_kr", "W_uvT", "W_o",
            "Wqkv1", "Wgba", "conv", "WoT1", "WgT", "W1T", "W2T", "W3T"]


def lay_out(a):
    def t(v):
        return v.T

    row = lambda v: v.reshape(1, -1)
    qkv = np.concatenate([a["L1_attn_Wq"], a["L1_attn_Wk"], a["L1_attn_Wv"]], 0)
    conv = np.concatenate([a["L1_attn_conv_q"], a["L1_attn_conv_k"], a["L1_attn_conv_v"]], 0)
    pad = QKVC * P - 3 * SV
    return {
        "x": a["x"].reshape(B * S, D),
        "ctxT": a["ctx_2048"].transpose(2, 0, 1),
        "itok": a["itok_BxS_0_1023"].reshape(B * S, 1),
        "consts": constant_table(),
        "W_in": a["L0_xattn_W_in"], "W_outT": t(a["L0_xattn_W_out"]),
        "b_in": a["L0_xattn_b_in"].reshape(DC, P).T, "b_out": row(a["L0_xattn_b_out"]),
        "gamma": row(a["L0_xattn_gamma"]), "beta": row(a["L0_xattn_beta"]), "decay": row(a["L0_xattn_decay"]),
        "dt_bias": row(a["L1_attn_dt_bias"]), "A_log": row(a["L1_attn_A_log"]), "o_norm": row(a["L1_attn_o_norm_w"]),
        "Wqk0": np.concatenate([a["L0_attn_Wq"], a["L0_attn_Wk"]], 1), "Wv0": a["L0_attn_Wv"], "Wo0": a["L0_attn_Wo"],
        "w1T": t(a["L0_ffn_w1"]), "w3T": t(a["L0_ffn_w3"]), "w2T": t(a["L0_ffn_w2"]),
        "W_kvc": a["L1_xattn_W_kvc"], "W_kvcT": t(a["L1_xattn_W_kvc"]), "W_dq": a["L1_xattn_W_dq"],
        "W_uqT": t(a["L1_xattn_W_uq"]), "W_qr": a["L1_xattn_W_qr"], "W_ukT": t(a["L1_xattn_W_uk"]),
        "W_kr": a["L1_xattn_W_kr"], "W_uvT": t(a["L1_xattn_W_uv"]), "W_o": a["L1_xattn_W_o"],
        "Wqkv1": np.pad(qkv.T, ((0, 0), (0, pad))),
        "Wgba": np.concatenate([a["L1_attn_Wg"], a["L1_attn_Wb"], a["L1_attn_Wa"]], 0).T,
        "conv": np.pad(conv, ((0, pad), (0, 0))), "WoT1": t(a["L1_attn_Wo"]),
        "WgT": t(a["L1_ffn_Wg"]), "W1T": a["L1_ffn_W1"].transpose(2, 0, 1).reshape(D, MH),
        "W2T": a["L1_ffn_W2"].transpose(2, 0, 1).reshape(D, MH), "W3T": a["L1_ffn_W3"].transpose(0, 2, 1).reshape(MH, D),
    }


def kernel(**inputs):
    import concourse.bacc as bacc
    from concourse.bass_utils import run_bass_kernel_spmd

    nc = bacc.Bacc("TRN2", target_bir_lowering=False, num_devices=1)
    arrays, aps = {}, {}
    for name, v in lay_out({k: np.asarray(v) for k, v in inputs.items()}).items():
        v = np.ascontiguousarray(v)
        arrays[f"in_{name}"] = v
        aps[name] = nc.dram_tensor(f"in_{name}", v.shape, mybir.dt.from_np(v.dtype), kind="ExternalInput").ap()
    out = nc.dram_tensor("out", (B * S, D), mybir.dt.float32, kind="ExternalOutput").ap()
    perceiver_kernel(nc, aps["x"], aps["ctxT"], aps["itok"], aps["consts"],
                     {n: aps[n] for n in _WEIGHTS}, out)
    r = run_bass_kernel_spmd(nc, [arrays], core_ids=[0])
    return r.results[0]["out"].reshape(B, S, D)
```

```python
from contextlib import ExitStack

import numpy as np
import concourse.bass as bass
from concourse import mybir

B, S, D, T = 64, 32, 256, 257
P = 128
BT = P // S
TILES = B // BT
STREAMS = 2
ROUNDS = TILES // STREAMS
DC = D // P
EPS = 1e-5
L0_HEAD = 8
FF, FFC = 682, 6
FFT = FF - (FFC - 1) * P
XH, HD, KVC, QC, R = 16, 128, 64, 96, 64
LOOKBACK = 8
NEG = -1e30
SH, SD = 6, 32
SV = SH * SD
CK = 4
QKVC = 5
NE, EH = 8, 176
MH = NE * EH
MHC = MH // P
HALF = MH // 2
STEPS = BT * 2
FRONT_STEPS = 6
LEVELS = [2, 4, 8, 16]

TURNS = """
keys keys_1 keys_2 keys_3 scale_front0 probs6 norm_in outputs6 probs7 norm_y outputs7 outputT up up_1
scale_front1 up_2 norm0 scale_front2 up_3 qkv0 qkv0_1 norm5 scale_back0 qkv qkv_1 qkv_2 s0 s0_1 softplus s0_2
s0_3 decay conv_a at0_0 at0_1 conv_b silu av0 decays av0_1 natural av0_out normf scale_front3 unit kqT ffn_up
gram ffn_up_1 mask ffn_up_2 lz0 lt0 lz1 lt1 lz2 lt2 ffn_up_3 ffn_up_4 apply0 ffn_up_5 apply1 apply2 apply3
onorm ffn_down ffn_down_1 onorm_scale oT ffn_down_2 out keysT norm6 normq scale_back1 scale_front4 route qc
route_probs moe0 moe0_1 moe0_2 moe0_3 q q_1 q_2 q_3 rope moe1 moe1_1 moe1_2 moe1_3 qT gT qT_1 down down_1
qT_out down_2 down_3 probs0 outputs0 probs1 outputs1 probs2 outputs2 probs3 outputs3 probs4 outputs4 probs5
outputs5
""".split()

_widths = [("ident", P), ("same", P), ("later", P), ("incl", S), ("strict", S), ("eye", S), ("off1", S)]
_widths += [(f"off{m}", P) for m in LEVELS]
_widths += [("qcos", R), ("qnsin", R // 2), ("qsin", R // 2), ("kcos", 2 * R), ("knsin", R), ("ksin", R),
            ("lcos", R), ("lnsin", R // 2), ("lsin", R // 2), ("spread", BT * P), ("pick", BT * P),
            ("iota", NE), ("key", T)]
CONST = {}
_at = 0
for _n, _w in _widths:
    CONST[_n] = (_at, _at + _w)
    _at += _w
NCONST = _at


def constant_table():
    t = np.zeros((P, NCONST), np.float32)
    p = np.arange(P)[:, None]
    j = np.arange(P)[None, :]
    s = np.arange(S)[None, :]

    def put(name, v):
        a, b = CONST[name]
        t[:v.shape[0], a:b] = v

    put("ident", p == j)
    put("same", p // S == j // S)
    put("later", (p // S == j // S) & (p > j))
    put("incl", p % S <= s)
    put("strict", p % S < s)
    put("eye", p % S == s)
    put("off1", (p % S // 2 == s // 2) & (p % S < s))
    for m in LEVELS:
        put(f"off{m}", (p // (2 * m) == j // (2 * m)) & (p // m < j // m))
    half = R // 2
    inv = 1.0 / 10000.0 ** (np.arange(half, dtype=np.float32) / np.float32(half))

    def angles(pos):
        a = pos.astype(np.float32)[:, None] * inv[None, :].astype(np.float32)
        return np.cos(a).astype(np.float32), np.sin(a).astype(np.float32)

    c, n = angles(np.arange(P) % S)
    put("qcos", np.concatenate([c, c], 1))
    put("qnsin", -n)
    put("qsin", n)
    c0, n0 = angles(np.arange(P))
    c1, n1 = angles(np.arange(P) + P)
    put("kcos", np.concatenate([c0, c0, c1, c1], 1))
    put("knsin", -np.concatenate([n0, n1], 1))
    put("ksin", np.concatenate([n0, n1], 1))
    c, n = angles(np.full(BT, T - 1))
    put("lcos", np.concatenate([c, c], 1))
    put("lnsin", -n)
    put("lsin", n)
    put("spread", np.concatenate([(p // S == b) & (p % S == j % S) for b in range(BT)], 1))
    put("pick", np.concatenate([np.broadcast_to(p == b, (P, P)) for b in range(BT)], 1))
    put("iota", np.broadcast_to(np.arange(NE), (P, NE)))
    put("key", np.broadcast_to(np.arange(T), (P, T)))
    return t


SEMS = """
ld_const ld_x0 ld_xs prep_pool ld_f0 ld_a0 ld_xw ld_s ld_m ternary kleft_ps pool_terms residual_front
residual_back segf ln_rstd_front ln_rstd_back seg8 good_lo good_both maskb kleft
krope1 krope kleft1 kleft2 qr2 qrope qkvn rn gates gl dexp dts atp abd pmp pbd onorm orn prep_ps binrep
prep_act biasrep absum q_scaled ln_x_front ln_x_back lnT_ps_front lnT_ps_back pooledrep residual_ps_front
residual_ps_back lnT_front lnT_back vT_ps vT s0_ps e0 at_ps at av_ps attn0 f_ps ffn kleftT_ps qc_ps qc kleftT
q_ps qT_ps s_ps qT e pT_ps pT oT o_ps oc oT_ps cv_ps gb_ps dec_ps cv_u nat_ps kqT_ps kqT gram_ps t2inv lz_ps
lz xbd lt_ps apply_ps applied uu onT_ps onT rt_ps route m_g m_ps gT_ps gT f_tanh qlat s_max g_tanh softplus
conv cv_tanh natural osq rdiff rtanh m_tanh prep_dve neg_a ln_stats_front ln_stats_back ln_var_front ln_var_back ln_mv_front ln_mv_back
ysum gammad o_rinv o_left cv_pad cvx tri xnew m_u
""".split()


def perceiver_kernel(nc, x, ctxT, itok, consts, w, out):
    f32, bf16, i32, u32 = mybir.dt.float32, mybir.dt.bfloat16, mybir.dt.int32, mybir.dt.uint32
    ALU, ACT, AX = mybir.AluOpType, mybir.ActivationFunctionType, mybir.AxisListType
    MUL, ADD, SUB = ALU.mult, ALU.add, ALU.subtract
    U = range(STREAMS)
    ctx = ExitStack()
    with ctx:
        def sb(name, shape, dt=f32):
            return ctx.enter_context(nc.sbuf_tensor(name, shape, dt))

        C = sb("C", [P, NCONST])
        Wc = sb("Wc", [P, DC, D])
        biasrep = sb("biasrep", [P, D])
        gamma = sb("gamma", [P, D])
        beta = sb("beta", [P, D])
        coef = sb("coef", [P, T])
        Wqk0 = sb("Wqk0", [P, DC, 2 * D])
        Wv0 = sb("Wv0", [P, DC, D])
        Wo0 = sb("Wo0", [P, DC, D])
        W13 = sb("W13", [P, 2, DC, FFC * P])
        W2 = sb("W2", [P, FFC, D])
        Wdq = sb("Wdq", [P, DC, QC])
        WQ = sb("WQ", [QC, XH, P])
        WK = sb("WK", [P, DC, P])
        WVO = sb("WVO", [P, XH // 2, D])
        Wqkv = sb("Wqkv", [P, DC, QKVC * P])
        convw = sb("convw", [P, QKVC, CK])
        Wgba = sb("Wgba", [P, DC, SV + 2 * SH])
        dtb = sb("dtb", [P, SH])
        nega = sb("nega", [P, SH])
        onw = sb("onw", [P, SD])
        Wo1 = sb("Wo1", [P, 2, D])
        Wr = sb("Wr", [P, DC, NE])
        W1m = sb("W1m", [P, DC, MH])
        W2m = sb("W2m", [P, DC, MH])
        W3m = sb("W3m", [P, MHC, D])
        spread = sb("spread", [P, BT, P], bf16)
        mhalf = sb("mhalf", [P, 2 * SH])
        small = sb("small", [P, 16])
        scales = sb("scales", [P, 9])

        def const(name, rows=P):
            a, b = CONST[name]
            return C[0:rows, a:b]

        ident = const("ident")

        BIG = [sb(f"big{u}", [P, 4640]) for u in U]
        MID = [sb(f"mid{u}", [P, 2432]) for u in U]
        xin = [sb(f"xin{u}", [P, D]) for u in U]
        X = [sb(f"X{u}", [P, D]) for u in U]
        XN = [sb(f"XN{u}", [P, D]) for u in U]
        XNT = [sb(f"XNT{u}", [P, DC, P]) for u in U]
        CT = [sb(f"CT{u}", [P, DC, BT, T]) for u in U]
        segi = [sb(f"segi{u}", [P, 1], i32) for u in U]
        seg = [sb(f"seg{u}", [P, 2]) for u in U]
        mask = [sb(f"mask{u}", [P, T], bf16) for u in U]
        st = [sb(f"st{u}", [P, 6]) for u in U]
        mv = [sb(f"mv{u}", [P, 2]) for u in U]
        ve = [sb(f"ve{u}", [P, 2]) for u in U]
        pooled = [sb(f"pooled{u}", [P, DC * BT]) for u in U]
        stat = [sb(f"stat{u}", [P, 64]) for u in U]
        oidx = [sb(f"oidx{u}", [P, NE], u32) for u in U]
        kltmp = [sb(f"kltmp{u}", [BT, R]) for u in U]
        KL = [sb(f"KL{u}", [BT, P + R]) for u in U]

        def view(t, a, *dims):
            n = 1
            for d in dims:
                n *= d
            v = t[:, a:a + n]
            if len(dims) == 2:
                return v.rearrange("p (a b) -> p a b", a=dims[0])
            if len(dims) == 3:
                return v.rearrange("p (a b c) -> p a b c", a=dims[0], b=dims[1])
            return v

        KR = [view(MID[u], 0, BT * 2, P) for u in U]
        KT = [view(MID[u], 1024, BT, T) for u in U]
        VL = [view(MID[u], 2052, BT, KVC) for u in U]
        KRtmp = [sb(f"krt{u}", [P, 2, BT * 2, R]) for u in U]
        good = [sb(f"good{u}", [P, 2, T]) for u in U]
        crep = [view(BIG[u], 1024, DC, BT, S) for u in U]
        prod = [view(BIG[u], 1280, DC * BT, T) for u in U]
        ytmp = [view(BIG[u], 3400, D) for u in U]
        QK0 = [view(BIG[u], 4096, 2 * D) for u in U]
        VT0 = [XN[u][:].rearrange("p (a b) -> p a b", a=DC) for u in U]
        E0 = [view(BIG[u], 0, BT * DC, D) for u in U]
        AT0 = [view(BIG[u], 2048, BT * DC, D) for u in U]
        AV0 = [view(BIG[u], 0, DC, P) for u in U]
        FT = [view(BIG[u], 0, 2, FFC * P // 2) for u in U]
        FU = [view(BIG[u], 768, 2, FFC * P // 2) for u in U]
        FG = [view(BIG[u], 1536, FFC, P) for u in U]
        QR = [view(BIG[u], 0, XH, P) for u in U]
        QT = [view(BIG[u], 2568, BT, XH * S) for u in U]
        QCT = [BIG[u][0:QC, 2048:2048 + P] for u in U]
        QRt = [view(BIG[u], 2568, XH, R) for u in U]
        OT = [view(BIG[u], 0, XH // 2, P) for u in U]
        PT = [view(BIG[u], 1024, 4, P) for u in U]
        EX = [[view(BIG[u], 1536 + 514 * k, 2, T) for k in range(2)] for u in U]
        OC = [[XN[u][:, k * P:(k + 1) * P] for k in range(2)] for u in U]
        CX = [BIG[u][:, 0:QKVC * BT * (S + CK - 1)].rearrange("p (c b s) -> p c b s", c=QKVC, b=BT) for u in U]
        CY = [view(BIG[u], 700, QKVC, P) for u in U]
        CTH = [view(BIG[u], 1340, QKVC, P) for u in U]
        SQ = [view(BIG[u], 1980, 2 * SH, SD) for u in U]
        QKVN = [view(BIG[u], 2364, 3 * SH, SD) for u in U]
        KQT = [view(BIG[u], 3840, 6, P) for u in U]
        ABD = {m: [view(BIG[u], 768 * k, SH, P) for u in U] for k, m in enumerate(LEVELS)}
        XBD = [view(BIG[u], 3072, SH, P) for u in U]
        PBD = [view(BIG[u], 3840, SH, P) for u in U]
        NAT = [view(MID[u], 0, 3 * SH + 6, SD) for u in U]
        BV = [view(MID[u], 576, SH, SD) for u in U]
        GS = [view(MID[u], 768, SH, SD) for u in U]
        DTI = [view(MID[u], 960, SH, S) for u in U]
        DTS = [view(MID[u], 1152, SH, S) for u in U]
        ATP = [view(MID[u], 1344, SH, S) for u in U]
        PMP = [view(MID[u], 1536, SH, S) for u in U]
        TP = [view(MID[u], 1728, SH, S) for u in U]
        XP = [view(MID[u], 1920, SH, S) for u in U]
        ZP = [view(MID[u], 2112, SH, S) for u in U]
        GL = ATP
        DEX = PMP
        WV = [view(MID[u], 0, SH, SD) for u in U]
        RV = [view(MID[u], 192, SH, SD) for u in U]
        UU = [view(MID[u], 384, SH, SD) for u in U]
        ON = [view(MID[u], 1728, SH, SD) for u in U]
        OSQ = [view(MID[u], 1920, SH, SD) for u in U]
        ONT = [view(MID[u], 0, 2, P) for u in U]
        GB = [view(BIG[u], 2940, SV + 2 * SH) for u in U]
        GTH = [view(BIG[u], 3144, SV + 2 * SH) for u in U]
        MT = [view(BIG[u], 0, 2, HALF // 2) for u in U]
        MU = [view(BIG[u], HALF, 2, HALF // 2) for u in U]
        MG = [view(BIG[u], 2 * HALF, MH) for u in U]
        GT = [view(MID[u], 0, MHC, P) for u in U]

        Win_n = view(MID[0], 0, DC, D)
        WoutT = view(MID[0], 512, DC, D)
        binc = MID[0][:, 1024:1024 + DC]
        binrep = view(MID[0], 1032, DC, P)
        boutrep = MID[0][:, 1288:1288 + D]
        ones = MID[0][:, 1544:1544 + T]
        kfill = MID[0][:, 1804:1804 + T]
        crev = MID[0][:, 2064:2064 + T]
        Wo_x = view(BIG[0], 0, XH, D)
        WuqT = view(BIG[1], 0, XH, QC)
        WukT = view(BIG[1], 1536, XH, KVC)
        WuvT = view(BIG[1], 2560, XH, KVC)
        Wqr = BIG[1][0:QC, 3584:3584 + XH * R].rearrange("p (h r) -> p h r", h=XH)
        WkvcT = MID[1][0:KVC, 0:D]
        Wkr = MID[1][0:KVC, 256:256 + R]
        quant = [W[:].rearrange("p c n -> p (c n)")[:, 0:DC * FFC * P] for W in (W1m, W2m)]

        PS = [ctx.enter_context(nc.psum_tensor(f"ps{u}", [P, 4, 512], f32)) for u in U]
        s = {n: ctx.enter_context(nc.semaphore(n)) for n in SEMS}
        ld_xin = [ctx.enter_context(nc.semaphore(f"ld_xin{u}")) for u in U]
        ld_ctx = [ctx.enter_context(nc.semaphore(f"ld_ctx{u}")) for u in U]
        ld_seg = [ctx.enter_context(nc.semaphore(f"ld_seg{u}")) for u in U]
        stored = [ctx.enter_context(nc.semaphore(f"stored{u}")) for u in U]

        x_v = x.rearrange("(t p) d -> t p d", p=P)
        out_v = out.rearrange("(t p) d -> t p d", p=P)
        itok_v = itok.rearrange("(t p) o -> t p o", p=P)

        def nth(i, u, k=0, n=1):
            return 2 * n * i + n * u + k + 1

        def wait_apart(eng, *pairs):
            pairs = [(sem, eng.snap(eng.to_reg(value))) for sem, value in pairs]
            eng.wait_ge(s["ld_const"], 16)
            for sem, value in pairs:
                eng.wait_ge(sem, value)

        LNS = {"front": 5, "back": 2}
        LNT = {"front": 3, "back": 2}

        def together(front, back):
            ahead = [(part, next(part)) for part in (front, back)]
            for stage in TURNS:
                ahead = [(part, next(part, None) if name == stage else name) for part, name in ahead]
            assert ahead == [(front, None), (back, None)]

        def up_to(part, stage):
            while next(part) != stage:
                pass

        def alone(part):
            for _ in part:
                pass

        block = ctx.enter_context(nc.Block())

        @block.sync
        def _(sp):
            def load(t, u):
                sp.dma_start(xin[u][:], x_v[bass.ds(t, 1)].rearrange("a p d -> (a p) d")).then_inc(ld_xin[u], 16)
                sp.dma_start(segi[u][:], itok_v[bass.ds(t, 1)].rearrange("a p d -> (a p) d")).then_inc(ld_seg[u], 16)

            def load_ctx(t, u):
                for c in range(DC):
                    sp.dma_start(CT[u][:, c], ctxT[c * P:(c + 1) * P, bass.ds(t * BT, BT), :]).then_inc(ld_ctx[u], 16)

            for u in U:
                sp.sem_inc(stored[u], 16)
            sp.dma_start(C[:], consts).then_inc(s["ld_const"], 16)
            for src, dst in ((w["W_in"], Win_n), (w["W_outT"], WoutT), (w["Wqk0"], Wqk0[:])):
                sp.dma_start(dst, src.rearrange("(c p) n -> p c n", p=P)).then_inc(s["ld_x0"], 16)
            sp.dma_start(binc, w["b_in"]).then_inc(s["ld_x0"], 16)
            for dst, src in ((boutrep, w["b_out"]), (gamma[:], w["gamma"]), (beta[:], w["beta"]), (small[:, 0:1], w["decay"]),
                             (dtb[:], w["dt_bias"]), (small[:, 8:8 + SH], w["A_log"]), (onw[:], w["o_norm"])):
                sp.dma_start(dst, src.to_broadcast([P, src.shape[1]])).then_inc(s["ld_x0"], 16)
            for dst, src in ((WuqT, w["W_uqT"]), (WukT, w["W_ukT"]), (WuvT, w["W_uvT"]), (Wo_x, w["W_o"])):
                sp.dma_start(dst, src.rearrange("(h p) n -> p h n", p=HD)).then_inc(s["ld_xs"], 16)
            sp.dma_start(Wqr, w["W_qr"].rearrange("p (h r) -> p h r", h=XH)).then_inc(s["ld_xs"], 16)
            sp.dma_start(WkvcT, w["W_kvcT"]).then_inc(s["ld_xs"], 16)
            sp.dma_start(Wkr, w["W_kr"]).then_inc(s["ld_xs"], 16)
            sp.dma_start(WK[:, :, 0:KVC], w["W_kvc"].rearrange("(c p) n -> p c n", p=P)).then_inc(s["ld_xs"], 16)
            sp.wait_ge(s["prep_pool"], 1)
            for k, src in enumerate((w["w1T"], w["w3T"])):
                sp.dma_start(W13[:, k, :, 0:FF], src.rearrange("(c p) n -> p c n", p=P)).then_inc(s["ld_f0"], 16)
            sp.dma_start(W2[:, 0:FFC - 1], w["w2T"][0:(FFC - 1) * P].rearrange("(c p) n -> p c n", p=P)).then_inc(s["ld_f0"], 16)
            sp.dma_start(W2[0:FFT, FFC - 1], w["w2T"][(FFC - 1) * P:FF]).then_inc(s["ld_f0"], 16)
            load_ctx(0, 0)
            for u in U:
                load(u, u)
            for src, dst in ((w["Wv0"], Wv0), (w["Wo0"], Wo0)):
                sp.dma_start(dst[:], src.rearrange("(c p) n -> p c n", p=P)).then_inc(s["ld_a0"], 16)
            sp.dma_start(Wdq[:], w["W_dq"].rearrange("(c p) n -> p c n", p=P)).then_inc(s["ld_xw"], 16)
            for src, dst in ((w["Wqkv1"], Wqkv), (w["Wgba"], Wgba)):
                sp.dma_start(dst[:], src.rearrange("(c p) n -> p c n", p=P)).then_inc(s["ld_s"], 16)
            sp.dma_start(convw[:], w["conv"].rearrange("(c p) n -> p c n", p=P)).then_inc(s["ld_s"], 16)
            sp.dma_start(Wo1[:, 0], w["WoT1"][0:P]).then_inc(s["ld_s"], 16)
            sp.dma_start(Wo1[SV - P:P, 1], w["WoT1"][P:SV]).then_inc(s["ld_s"], 16)
            load_ctx(1, 1)
            sp.wait_ge(s["ternary"], 3)
            for src, dst in ((w["WgT"], Wr), (w["W1T"], W1m), (w["W2T"], W2m), (w["W3T"], W3m)):
                sp.dma_start(dst[:], src.rearrange("(c p) n -> p c n", p=P)).then_inc(s["ld_m"], 16)

            def next_tile(i, u):
                sp.wait_ge(s["kleft_ps"], nth(i, u))
                sp.wait_ge(s["pool_terms"], nth(i, u))
                load_ctx(2 * i + (2 + u), u)
                sp.wait_ge(s["residual_front"], nth(i, u, 0, 3))
                sp.wait_ge(s["segf"], nth(i, u))
                load(2 * i + (2 + u), u)

            def store(i, u):
                sp.wait_ge(s["residual_back"], nth(i, u, 2, 3))
                sp.dma_start(out_v[bass.ds(2 * i + u, 1)].rearrange("a p d -> (a p) d"),
                             X[u][:]).then_inc(stored[u], 16)

            next_tile(0, 0)
            with sp.Fori(0, ROUNDS - 2) as i:
                next_tile(i, 1)
                store(i, 0)
                next_tile(i + 1, 0)
                store(i, 1)
            next_tile(ROUNDS - 2, 1)
            for u in U:
                store(ROUNDS - 2, u)
            for u in U:
                store(ROUNDS - 1, u)
            for u in U:
                sp.wait_ge(stored[u], 16 * (ROUNDS + 1))

        @block.gpsimd
        def _(pool):
            pool.memset(W13[:, :, :, FF:FFC * P], 0.0)
            pool.memset(W2[:, FFC - 1], 0.0).then_inc(s["prep_pool"], 1)
            pool.memset(mhalf[:], -0.5).then_inc(s["prep_pool"], 1)
            pool.wait_ge(s["ld_const"], 16)
            pool.tensor_copy(spread[:], const("spread").rearrange("p (b q) -> p b q", b=BT)).then_inc(s["prep_pool"], 1)
            pool.wait_ge(s["prep_pool"], 2)
            def rstd(i, u, part, k):
                pool.wait_ge(s[f"ln_var_{part}"], nth(i, u, k, LNS[part]))
                pool.tensor_tensor(ve[u][:, 1:2], ve[u][:, 0:1], mhalf[:, 0:1], ALU.pow).then_inc(s[f"ln_rstd_{part}"], 1)

            def front(i, u):
                yield "scale_front0"
                rstd(i, u, "front", 0)
                yield "scale_front1"
                rstd(i, u, "front", 1)
                yield "scale_front2"
                rstd(i, u, "front", 2)
                yield "qkv0_1"
                wait_apart(pool, (ld_seg[u], 16 * i + 16))
                pool.tensor_copy(seg[u][:, 0:1], segi[u][:]).then_inc(s["segf"], 1)
                wait_apart(pool, (s["segf"], nth(i, u)))
                pool.tensor_scalar(seg[u][:, 1:2], seg[u][:, 0:1], float(-LOOKBACK), None, ADD).then_inc(s["seg8"], 1)
                pool.tensor_scalar(good[u][:, 0], const("key"), seg[u][:, 0:1], None, ALU.is_le)
                wait_apart(pool, (s["seg8"], nth(i, u)))
                pool.tensor_scalar(good[u][:, 1], const("key"), seg[u][:, 1:2], None, ALU.is_ge).then_inc(s["good_lo"], 1)
                pool.wait_ge(s["good_lo"], nth(i, u))
                pool.tensor_tensor(good[u][:, 0], good[u][:, 0], good[u][:, 1], MUL).then_inc(s["good_both"], 1)
                wait_apart(pool, (s["good_both"], nth(i, u)))
                pool.tensor_scalar(mask[u][:], good[u][:, 0], -1.0, -NEG, ADD, MUL).then_inc(s["maskb"], 1)
                yield "av0_1"
                pool.wait_ge(s["kleft"], nth(i, u))
                kr = KR[u].rearrange("p (b c) d -> p b c d", b=BT)
                for b in range(BT):
                    kb, t0, t1 = kr[:, b], KRtmp[u][:, 0, 2 * b:2 * b + 2], KRtmp[u][:, 1, 2 * b:2 * b + 2]
                    pool.tensor_tensor(t0, kb[:, :, KVC:P], const("kcos").rearrange("p (c d) -> p c d", c=2), MUL)
                    pool.tensor_tensor(t1[:, :, 0:R // 2], kb[:, :, KVC + R // 2:P],
                                       const("knsin").rearrange("p (c d) -> p c d", c=2), MUL)
                    last = pool.tensor_tensor(t1[:, :, R // 2:R], kb[:, :, KVC:KVC + R // 2],
                                              const("ksin").rearrange("p (c d) -> p c d", c=2), MUL)
                last.then_inc(s["krope1"], 1)
                pool.wait_ge(s["krope1"], nth(i, u))
                pool.tensor_tensor(KR[u][:, :, KVC:P], KRtmp[u][:, 0], KRtmp[u][:, 1], ADD).then_inc(s["krope"], 1)
                yield "av0_out"
                pool.wait_ge(s["kleft"], nth(i, u))
                pool.tensor_tensor(KL[u][:, P:P + R], KL[u][:, KVC:P], const("lcos", BT), MUL)
                pool.tensor_tensor(kltmp[u][:, 0:R // 2], KL[u][:, KVC + R // 2:P], const("lnsin", BT), MUL)
                pool.tensor_tensor(kltmp[u][:, R // 2:R], KL[u][:, KVC:KVC + R // 2], const("lsin", BT),
                                   MUL).then_inc(s["kleft1"], 1)
                pool.wait_ge(s["kleft1"], nth(i, u))
                pool.tensor_tensor(KL[u][:, KVC:P], KL[u][:, P:P + R], kltmp[u][:], ADD).then_inc(s["kleft2"], 1)
                yield "scale_front3"
                rstd(i, u, "front", 3)
                yield "scale_front4"
                rstd(i, u, "front", 4)
                yield "rope"
                pool.wait_ge(s["qr2"], nth(i, u))
                pool.tensor_tensor(QR[u][:, :, KVC:P], QR[u][:, :, KVC:P], QRt[u], ADD).then_inc(s["qrope"], 1)

            def back(i, u):
                yield "scale_back0"
                rstd(i, u, "back", 0)
                yield "decays"
                pool.wait_ge(s["gates"], nth(i, u, 5, 7))
                pool.tensor_tensor(GL[u], const("incl").unsqueeze(1).to_broadcast([P, SH, S]),
                                   stat[u][:, 36:42].unsqueeze(2).to_broadcast([P, SH, S]), MUL).then_inc(s["gl"], 1)
                yield "unit"
                pool.wait_ge(s["dexp"], nth(i, u))
                pool.tensor_tensor(DTI[u], DEX[u], const("incl").unsqueeze(1).to_broadcast([P, SH, S]),
                                   MUL)
                pool.tensor_tensor(DTS[u], DEX[u], const("strict").unsqueeze(1).to_broadcast([P, SH, S]),
                                   MUL).then_inc(s["dts"], 1)
                pool.wait_ge(s["qkvn"], nth(i, u, 1, 4))
                pool.tensor_tensor(stat[u][:, 12:24], stat[u][:, 0:12], mhalf[:], ALU.pow).then_inc(s["rn"], 1)

                def expand(u, dst, src, maskname, done):
                    pool.tensor_tensor(dst.rearrange("p h (b j) -> p h b j", b=BT)[:],
                                       src.unsqueeze(2).to_broadcast([P, SH, BT, S]),
                                       const(maskname).rearrange("p (b j) -> p b j", b=BT).unsqueeze(1)
                                       .to_broadcast([P, SH, BT, S]), MUL).then_inc(done, 1)

                for k, m in enumerate(LEVELS):
                    yield "mask" if k == 0 else f"lz{k - 1}"
                    if k == 0:
                        pool.wait_ge(s["atp"], nth(i, u))
                    expand(u, ABD[m][u], ATP[u], f"off{m}", s["abd"])
                yield "apply0"
                pool.wait_ge(s["pmp"], nth(i, u))
                expand(u, PBD[u], PMP[u], "same", s["pbd"])
                yield "onorm"
                pool.wait_ge(s["onorm"], nth(i, u, 1, 4))
                pool.tensor_tensor(stat[u][:, 48:54], stat[u][:, 42:48], mhalf[:, 0:SH], ALU.pow).then_inc(s["orn"], 1)
                yield "scale_back1"
                rstd(i, u, "back", 1)

            alone(front(0, 0))
            with pool.Fori(0, ROUNDS - 1) as i:
                together(front(i, 1), back(i, 0))
                together(front(i + 1, 0), back(i, 1))
            together(front(ROUNDS - 1, 1), back(ROUNDS - 1, 0))
            alone(back(ROUNDS - 1, 1))

        @block.tensor
        def _(pe):
            mm, tr = pe.matmul, pe.transpose

            def chunks(o, lhs, rhs, n):
                for c in range(n):
                    last = mm(o, lhs(c), rhs(c), start=c == 0, stop=c == n - 1)
                return last

            pe.wait_ge(s["ld_x0"], 16 * 11)
            for d in range(DC):
                last = chunks(PS[0][:, 0, d * D:(d + 1) * D], lambda c: Win_n[:, c, d * P:(d + 1) * P],
                              lambda c: WoutT[:, c], DC)
            last.then_inc(s["prep_ps"], 1)
            pe.wait_ge(s["binrep"], 1)
            chunks(PS[0][:, 1, 0:D], lambda c: binrep[:, c], lambda c: WoutT[:, c], DC).then_inc(s["prep_ps"], 1)
            pe.wait_ge(s["ld_xs"], 16 * 8)
            for h in range(XH):
                slot = h % 2 * 4 + h % 8 // 2
                last = mm(PS[1][0:QC, h // 8, slot * KVC:(slot + 1) * KVC], WuqT[:, h], WukT[:, h],
                          start=True, stop=True)
            last.then_inc(s["prep_ps"], 1)
            for c in range(DC):
                last = mm(PS[1][:, 2, c * R:(c + 1) * R], WkvcT[:, c * P:(c + 1) * P], Wkr, start=True, stop=True)
            last.then_inc(s["prep_ps"], 1)
            pe.wait_ge(s["prep_act"], 3)
            pe.wait_ge(s["biasrep"], 1)
            for h in range(XH):
                q = h % 2
                last = mm(PS[0][64 * q:64 * q + KVC, h // 4, (h // 2 % 2) * D:(h // 2 % 2 + 1) * D],
                          WuvT[:, h], Wo_x[:, h], start=True, stop=True)
            last.then_inc(s["prep_ps"], 1)
            pe.wait_ge(s["absum"], 1)
            mm(PS[1][:, 3, 0:3], ones[:, 0:P], small[:, 1:4], start=True, stop=True).then_inc(s["prep_ps"], 1)
            for sem, n in ((s["ld_a0"], 2), (s["ld_xw"], 1)):
                pe.wait_ge(sem, 16 * n)
            pe.wait_ge(s["prep_act"], 5)
            pe.wait_ge(s["prep_act"], 4)
            pe.wait_ge(s["q_scaled"], 1)
            pe.wait_ge(s["prep_pool"], 3)

            def norm_T(i, u, part, k, need):
                pe.wait_ge(s[f"ln_x_{part}"], nth(i, u, need, LNS[part]))
                for c in range(DC):
                    last = tr(PS[u][:, 3, c * P:(c + 1) * P], XN[u][:, c * P:(c + 1) * P], ident)
                last.then_inc(s[f"lnT_ps_{part}"], 1)

            def scores(i, u, k):
                b, pb = divmod(k, 2)
                for q in range(2):
                    o = PS[u][:, q, 0:T]
                    mm(o, spread[:, b], mask[u][:], start=True, stop=False)
                    last = mm(o, QT[u][:, b, (2 * pb + q) * P:(2 * pb + q + 1) * P], KT[u][:, b],
                              start=False, stop=True)
                last.then_inc(s["s_ps"], 1)

            def output_T(i, u, k):
                pe.wait_ge(s["oc"], nth(i, u, k, STEPS))
                tr(PS[u][:, 3, P:2 * P], OC[u][k % 2], ident).then_inc(s["oT_ps"], 1)

            def probs_T(i, u, k):
                pe.wait_ge(s["e"], nth(i, u, k, STEPS))
                for q in range(2):
                    for tc in range(2):
                        last = tr(PS[u][:, 2, (2 * q + tc) * P:(2 * q + tc + 1) * P],
                                  EX[u][k % 2][:, q, tc * P:(tc + 1) * P], ident)
                last.then_inc(s["pT_ps"], 1)
                if k + 1 < STEPS:
                    scores(i, u, k + 1)
                if k > 0:
                    output_T(i, u, k - 1)

            def outputs(i, u, k):
                b = k // 2
                pe.wait_ge(s["pT"], nth(i, u, k, STEPS))
                if k > 0:
                    pe.wait_ge(s["oT"], nth(i, u, k - 1, STEPS))
                for q in range(2):
                    last = chunks(PS[u][:, 3, q * KVC:(q + 1) * KVC], lambda tc: PT[u][:, 2 * q + tc],
                                  lambda tc: KR[u][:, 2 * b + tc, 0:KVC], 2)
                last.then_inc(s["o_ps"], 1)

            def front(i, u):
                yield "keys"
                pe.wait_ge(ld_ctx[u], 32 * i + 32)
                for b in range(BT):
                    if b:
                        yield f"keys_{b}"
                    for tc in range(2):
                        last = chunks(PS[u][:, b // 2, (b % 2 * 2 + tc) * P:(b % 2 * 2 + tc + 1) * P],
                                      lambda c: CT[u][:, c, b, tc * P:(tc + 1) * P], lambda c: WK[:, c], DC)
                chunks(PS[u][0:BT, 2, 0:P], lambda c: CT[u][:, c, :, T - 1], lambda c: WK[:, c],
                       DC).then_inc(s["kleft_ps"], 1)
                yield "norm_in"
                pe.wait_ge(s["pooledrep"], nth(i, u))
                chunks(PS[u][:, 3, 0:D], lambda c: crep[u][:, c], lambda c: Wc[:, c], DC).then_inc(s["residual_ps_front"], 1)
                yield "norm0"
                norm_T(i, u, "front", 0, 2)
                yield "qkv0"
                pe.wait_ge(s["lnT_front"], nth(i, u, 0, 3))
                pe.wait_ge(s["kleft"], nth(i, u))
                pe.wait_ge(s["kleft"], nth(i, u))
                chunks(PS[u][:, 0], lambda c: XNT[u][:, c], lambda c: Wqk0[:, c], DC)
                yield "qkv0_1"
                for f in range(DC):
                    last = chunks(PS[u][:, 1, f * P:(f + 1) * P], lambda c: Wv0[:, c, f * P:(f + 1) * P],
                                  lambda c: XNT[u][:, c], DC)
                last.then_inc(s["vT_ps"], 1)
                yield "s0"
                pe.wait_ge(s["vT"], nth(i, u))
                for b in range(BT):
                    rows = slice(b * S, (b + 1) * S)
                    if b:
                        yield f"s0_{b}"
                    for e in range(DC):
                        last = mm(PS[u][:, b, e * D:(e + 1) * D], QK0[u][rows, e * P:(e + 1) * P],
                                  QK0[u][rows, D:2 * D], start=True, stop=True)
                    if b % 2:
                        last.then_inc(s["s0_ps"], 1)
                for g in range(2):
                    yield f"at0_{g}"
                    pe.wait_ge(s["e0"], nth(i, u, g, 2))
                    for b in range(2 * g, 2 * g + 2):
                        for f in range(DC):
                            for e in range(DC):
                                last = tr(PS[u][:, b, (f * DC + e) * P:(f * DC + e + 1) * P],
                                          E0[u][:, b * DC + e, f * P:(f + 1) * P], ident)
                    last.then_inc(s["at_ps"], 1)
                yield "av0"
                for b in range(BT):
                    if b == 2:
                        yield "av0_1"
                    if b % 2 == 0:
                        pe.wait_ge(s["at"], nth(i, u, b // 2, 2))
                    for e in range(DC):
                        last = chunks(PS[u][:, 0, e * P + b * S:e * P + (b + 1) * S],
                                      lambda f: AT0[u][:, b * DC + f, e * P:(e + 1) * P],
                                      lambda f: VT0[u][:, f, b * S:(b + 1) * S], DC)
                last.then_inc(s["av_ps"], 1)
                yield "av0_out"
                pe.wait_ge(s["attn0"], nth(i, u, 5, 6))
                chunks(PS[u][:, 1, 0:D], lambda c: AV0[u][:, c], lambda c: Wo0[:, c], DC).then_inc(s["residual_ps_front"], 1)
                yield "normf"
                norm_T(i, u, "front", 1, 3)
                yield "ffn_up"
                pe.wait_ge(s["lnT_front"], nth(i, u, 1, 3))
                for k in range(2):
                    for f in range(FFC):
                        if f % 2 == 0 and k + f:
                            yield f"ffn_up_{3 * k + f // 2}"
                        last = chunks(PS[u][:, 2 * k + f // 3, (f % 3) * P:(f % 3 + 1) * P],
                                      lambda c: W13[:, k, c, f * P:(f + 1) * P], lambda c: XNT[u][:, c], DC)
                last.then_inc(s["f_ps"], 1)
                yield "ffn_down"
                pe.wait_ge(s["ffn"], nth(i, u, 1, 2))
                for f in range(FFC):
                    if f % 2 == 0 and f:
                        yield f"ffn_down_{f // 2}"
                    r = P if f < FFC - 1 else FFT
                    last = mm(PS[u][:, 0, 0:D], FG[u][0:r, f], W2[0:r, f], start=f == 0, stop=f == FFC - 1)
                last.then_inc(s["residual_ps_front"], 1)
                yield "keysT"
                pe.wait_ge(s["krope"], nth(i, u))
                pe.wait_ge(s["kleft2"], nth(i, u))
                pe.wait_ge(s["residual_front"], nth(i, u, 2, 3))
                for k in range(BT * 2):
                    last = tr(PS[u][:, k // 4, (k % 4) * P:(k % 4 + 1) * P], KR[u][:, k], ident)
                tr(PS[u][:, 2, 0:BT], KL[u][:, 0:P], ident[0:BT, 0:BT])
                for b in range(BT):
                    last = mm(PS[u][:, 2, P + b * KVC:P + (b + 1) * KVC], const("pick", BT)[:, b * P:(b + 1) * P],
                              KL[u][:, 0:KVC], start=True, stop=True)
                last.then_inc(s["kleftT_ps"], 1)
                yield "normq"
                norm_T(i, u, "front", 2, 4)
                yield "qc"
                pe.wait_ge(s["lnT_front"], nth(i, u, 2, 3))
                chunks(PS[u][0:QC, 3, 0:P], lambda c: Wdq[:, c], lambda c: XNT[u][:, c], DC).then_inc(s["qc_ps"], 1)
                yield "q"
                pe.wait_ge(s["qc"], nth(i, u))
                pe.wait_ge(s["kleftT"], nth(i, u))
                for g in range(4):
                    if g:
                        yield f"q_{g}"
                    last = mm(PS[u][:, g], QCT[u], WQ[:, 4 * g:4 * g + 4], start=True, stop=True)
                last.then_inc(s["q_ps"], 1)
                yield "qT"
                pe.wait_ge(s["qrope"], nth(i, u))
                for h in range(XH):
                    if h == XH // 2:
                        yield "qT_1"
                    last = tr(PS[u][:, h // 4, (h % 4) * P:(h % 4 + 1) * P], QR[u][:, h], ident)
                last.then_inc(s["qT_ps"], 1)
                yield "qT_out"
                pe.wait_ge(s["qT"], nth(i, u))
                pe.wait_ge(s["maskb"], nth(i, u))
                scores(i, u, 0)
                for k in range(FRONT_STEPS):
                    yield f"probs{k}"
                    probs_T(i, u, k)
                    yield f"outputs{k}"
                    outputs(i, u, k)

            def back(i, u):
                for k in range(FRONT_STEPS, STEPS):
                    yield f"probs{k}"
                    probs_T(i, u, k)
                    yield f"outputs{k}"
                    outputs(i, u, k)
                yield "outputT"
                output_T(i, u, STEPS - 1)
                yield "up"
                pe.wait_ge(s["oT"], nth(i, u, STEPS - 1, STEPS))
                for hp in range(XH // 2):
                    if hp and hp % 2 == 0:
                        yield f"up_{hp // 2}"
                    last = mm(PS[u][:, 0, 0:D], OT[u][:, hp], WVO[:, hp],
                              start=hp == 0, stop=hp == XH // 2 - 1)
                last.then_inc(s["residual_ps_back"], 1)
                yield "norm5"
                norm_T(i, u, "back", 0, 0)
                yield "qkv"
                pe.wait_ge(s["lnT_back"], nth(i, u, 0, 2))
                for f in range(QKVC):
                    if f == 3:
                        yield "qkv_1"
                    last = chunks(PS[u][:, f // 3, (f % 3) * P:(f % 3 + 1) * P],
                                  lambda c: Wqkv[:, c, f * P:(f + 1) * P], lambda c: XNT[u][:, c], DC)
                last.then_inc(s["cv_ps"], 1)
                yield "qkv_2"
                chunks(PS[u][:, 2, 0:SV + 2 * SH], lambda c: XNT[u][:, c], lambda c: Wgba[:, c],
                       DC).then_inc(s["gb_ps"], 1)
                yield "decays"
                pe.wait_ge(s["gl"], nth(i, u))
                mm(PS[u][:, 3, 0:SH * S], const("later"), GL[u].rearrange("p h s -> p (h s)"),
                   start=True, stop=True).then_inc(s["dec_ps"], 1)
                yield "natural"
                pe.wait_ge(s["cv_u"], nth(i, u))
                for f in range(QKVC):
                    r = P if f < QKVC - 1 else 3 * SV - (QKVC - 1) * P
                    last = tr(PS[u][:, f // 3, (f % 3) * P:(f % 3) * P + P][:, 0:r] if r < P else
                              PS[u][:, f // 3, (f % 3) * P:(f % 3 + 1) * P],
                              CTH[u][:, f, :][0:r], ident[0:r, 0:r])
                last.then_inc(s["nat_ps"], 1)
                yield "kqT"
                pe.wait_ge(s["qkvn"], nth(i, u, 3, 4))
                nat = MID[u][:, 0:3 * SV + SV]
                for g in range(2):
                    for k, o in enumerate((SV, 2 * SV, 0)):
                        j = 3 * g + k
                        last = tr(PS[u][:, j // 3, (j % 3) * P:(j % 3 + 1) * P],
                                  nat[:, o + g * P:o + (g + 1) * P], ident)
                last.then_inc(s["kqT_ps"], 1)
                yield "gram"
                wait_apart(pe, (s["kqT"], nth(i, u)), (s["dexp"], nth(i, u)))
                for h in range(SH):
                    r, g = h % 4, h // 4
                    rows = slice(r * SD, (r + 1) * SD)
                    for b in range(BT):
                        ts = slice(b * S, (b + 1) * S)
                        last = mm(PS[u][b * S:(b + 1) * S, r, g * 2 * S:(g + 1) * 2 * S],
                                  KQT[u][rows, 3 * g, ts], KQT[u][rows, 3 * g + 1:3 * g + 3, ts],
                                  start=True, stop=True, tile_position=(r * SD, b * S))
                last.then_inc(s["gram_ps"], 1)

                def product(u, o, stationary, moving, done):
                    for h in range(SH):
                        last = mm(o[:, h * S:(h + 1) * S], stationary[:, h], moving[:, h], start=True, stop=True)
                    last.then_inc(done, 1)

                for k, m in enumerate(LEVELS[:-1]):
                    yield f"lz{k}"
                    pe.wait_ge(s["abd"], nth(i, u, k, 4))
                    pe.wait_ge(s["t2inv"], nth(i, u, k, 4))
                    product(u, PS[u][:, 0], ABD[m][u], TP[u], s["lz_ps"])
                    yield f"lt{k}"
                    pe.wait_ge(s["lz"], nth(i, u, k, 3))
                    pe.wait_ge(s["xbd"], nth(i, u, k, 4))
                    product(u, PS[u][:, 1], XBD[u], ZP[u], s["lt_ps"])
                yield "apply0"
                pe.wait_ge(s["xbd"], nth(i, u, 3, 4))
                product(u, PS[u][:, 0], XBD[u], BV[u], s["apply_ps"])
                yield "apply1"
                pe.wait_ge(s["applied"], nth(i, u, 0, 2))
                pe.wait_ge(s["abd"], nth(i, u, 3, 4))
                product(u, PS[u][:, 1], ABD[LEVELS[-1]][u], WV[u], s["apply_ps"])
                yield "apply2"
                pe.wait_ge(s["applied"], nth(i, u, 1, 2))
                product(u, PS[u][:, 0], XBD[u], RV[u], s["apply_ps"])
                yield "apply3"
                pe.wait_ge(s["uu"], nth(i, u))
                pe.wait_ge(s["pbd"], nth(i, u))
                product(u, PS[u][:, 1], PBD[u], UU[u], s["apply_ps"])
                yield "oT"
                pe.wait_ge(s["onorm"], nth(i, u, 3, 4))
                on = ON[u].rearrange("p h d -> p (h d)")
                tr(PS[u][:, 2, 0:P], on[:, 0:P], ident)
                tr(PS[u][:, 2, P:2 * P], on[:, SV - P:SV], ident).then_inc(s["onT_ps"], 1)
                yield "out"
                pe.wait_ge(s["onT"], nth(i, u))
                mm(PS[u][:, 3, 0:D], ONT[u][:, 0], Wo1[:, 0], start=True, stop=False)
                mm(PS[u][:, 3, 0:D], ONT[u][SV - P:P, 1], Wo1[SV - P:P, 1], start=False,
                   stop=True).then_inc(s["residual_ps_back"], 1)
                yield "norm6"
                norm_T(i, u, "back", 1, 1)
                yield "route"
                pe.wait_ge(s["lnT_back"], nth(i, u, 1, 2))
                chunks(PS[u][:, 3, 0:NE], lambda c: XNT[u][:, c], lambda c: Wr[:, c], DC).then_inc(s["rt_ps"], 1)
                for k in range(2):
                    yield f"moe{k}"
                    if k == 0:
                        pe.wait_ge(s["route"], nth(i, u, 0, 7))
                    else:
                        pe.wait_ge(s["m_g"], nth(i, u, 0, 2))
                    for j, Wm in enumerate((W1m, W2m)):
                        for q in range(2):
                            if j + q:
                                yield f"moe{k}_{2 * j + q}"
                            a = k * HALF + q * HALF // 2
                            last = chunks(PS[u][:, 2 * j + q, 0:HALF // 2], lambda c: XNT[u][:, c],
                                          lambda c: Wm[:, c, a:a + HALF // 2], DC)
                    last.then_inc(s["m_ps"], 1)
                yield "gT"
                pe.wait_ge(s["m_g"], nth(i, u, 1, 2))
                for f in range(MHC):
                    last = tr(PS[u][:, f // 4, (f % 4) * P:(f % 4 + 1) * P], MG[u][:, f * P:(f + 1) * P], ident)
                last.then_inc(s["gT_ps"], 1)
                yield "down"
                pe.wait_ge(s["gT"], nth(i, u))
                for c in range(MHC):
                    if c and c % 3 == 0:
                        yield f"down_{c // 3}"
                    last = mm(PS[u][:, 3, 0:D], GT[u][:, c], W3m[:, c], start=c == 0, stop=c == MHC - 1)
                last.then_inc(s["residual_ps_back"], 1)

            first = front(0, 0)
            for n, stage in ((2, "ffn_up"), (3, "ffn_down")):
                up_to(first, stage)
                pe.wait_ge(s["ternary"], n)
            alone(first)
            pe.wait_ge(s["ld_s"], 16 * 5)
            pe.wait_ge(s["ld_m"], 16 * 4)
            with pe.Fori(0, ROUNDS - 1) as i:
                together(front(i, 1), back(i, 0))
                together(front(i + 1, 0), back(i, 1))
            together(front(ROUNDS - 1, 1), back(ROUNDS - 1, 0))
            alone(back(ROUNDS - 1, 1))

        @block.scalar
        def _(act):
            act.wait_ge(s["ld_x0"], 16 * 11)
            act.activation(small[:, 4:5], small[:, 0:1], ACT.Tanh, scale=0.5).then_inc(s["prep_act"], 1)
            act.activation(small[:, 8:8 + SH], small[:, 8:8 + SH], ACT.Exp).then_inc(s["prep_act"], 1)
            act.wait_ge(s["prep_ps"], 1)
            act.copy(Wc[:].rearrange("p c d -> p (c d)"), PS[0][:, 0]).then_inc(s["prep_act"], 1)
            act.wait_ge(s["prep_ps"], 4)
            act.copy(WK[:, :, KVC:P], PS[1][:, 2, 0:DC * R].rearrange("p (c r) -> p c r", c=DC)).then_inc(s["prep_act"], 1)
            act.wait_ge(s["prep_ps"], 5)
            act.copy(WVO[:].rearrange("p h d -> p (h d)"), PS[0][:].rearrange("p b n -> p (b n)")).then_inc(s["prep_act"], 1)

            def norm_T(i, u, part, k):
                act.wait_ge(s[f"lnT_ps_{part}"], nth(i, u, k, LNT[part]))
                act.copy(XNT[u][:].rearrange("p c n -> p (c n)"), PS[u][:, 3, 0:D]).then_inc(s[f"lnT_{part}"], 1)

            def exps(i, u, k):
                act.wait_ge(s["s_max"], nth(i, u, k, STEPS))
                if k > 1:
                    act.wait_ge(s["oc"], nth(i, u, k - 2, STEPS))
                for q in range(2):
                    m = 4 * (k % 2) + q
                    last = act.activation(EX[u][k % 2][:, q], PS[u][:, q, 0:T], ACT.Exp,
                                          bias=stat[u][:, m:m + 1], accum_out=stat[u][:, m + 2:m + 3])
                last.then_inc(s["e"], 1)

            def output_T(i, u, k):
                act.wait_ge(s["oT_ps"], nth(i, u, k, STEPS))
                b, pb = divmod(k, 2)
                act.copy(OT[u][:, 4 * pb:4 * pb + 4, b * S:(b + 1) * S],
                         PS[u][:, 3, P:2 * P].rearrange("p (j s) -> p j s", s=S)).then_inc(s["oT"], 1)

            def front(i, u):
                yield "keys_3"
                act.wait_ge(s["kleft_ps"], nth(i, u))
                act.copy(MID[u][:, 0:1024].rearrange("p (a b) -> p a b", a=2), PS[u][:, 0:2])
                act.wait_ge(s["kleft_ps"], nth(i, u))
                act.copy(KL[u][:, 0:P], PS[u][0:BT, 2, 0:P]).then_inc(s["kleft"], 1)
                yield "norm0"
                norm_T(i, u, "front", 0)
                yield "qkv0_1"
                act.wait_ge(s["vT_ps"], nth(i, u))
                act.copy(QK0[u], PS[u][:, 0])
                act.wait_ge(s["vT_ps"], nth(i, u))
                act.copy(XN[u][:], PS[u][:, 1, 0:D]).then_inc(s["vT"], 1)
                yield "s0_3"
                for g in range(2):
                    act.wait_ge(s["attn0"], nth(i, u, 2 * g + 1, 6))
                    for k in range(4 * g, 4 * g + 4):
                        last = act.activation(E0[u][:, k], PS[u][:, k // DC, (k % DC) * D:(k % DC + 1) * D], ACT.Exp,
                                              bias=stat[u][:, 8 + k:9 + k], scale=float(1 / np.sqrt(L0_HEAD)),
                                              accum_out=stat[u][:, 16 + k:17 + k])
                    last.then_inc(s["e0"], 1)
                for g in range(2):
                    yield f"at0_{g}"
                    act.wait_ge(s["at_ps"], nth(i, u, g, 2))
                    act.copy(AT0[u].rearrange("p (a c) e -> p a (c e)", a=BT)[:, 2 * g:2 * g + 2],
                             PS[u][:, 2 * g:2 * g + 2]).then_inc(s["at"], 1)
                yield "normf"
                norm_T(i, u, "front", 1)
                yield "ffn_up_5"
                act.wait_ge(s["f_ps"], nth(i, u))
                act.activation(FT[u], PS[u][:, 0:2, 0:3 * P], ACT.Tanh, scale=0.5).then_inc(s["f_tanh"], 1)
                yield "keysT"
                act.wait_ge(s["kleftT_ps"], nth(i, u))
                act.copy(KT[u][:, :, 0:2 * P], PS[u][:, 0:2].rearrange("p a (b n) -> p (a b) n", b=2))
                act.wait_ge(s["kleftT_ps"], nth(i, u))
                act.copy(KT[u][:, :, T - 1:T], PS[u][:, 2, 0:BT].unsqueeze(2))
                act.copy(VL[u].rearrange("p b n -> p (b n)"), PS[u][:, 2, P:P + BT * KVC]).then_inc(s["kleftT"], 1)
                yield "normq"
                norm_T(i, u, "front", 2)
                yield "qc"
                act.wait_ge(s["qc_ps"], nth(i, u))
                act.copy(QCT[u], PS[u][0:QC, 3, 0:P]).then_inc(s["qc"], 1)
                yield "q_3"
                act.wait_ge(s["q_ps"], nth(i, u))
                act.copy(QR[u][:, :, 0:KVC], PS[u][:].rearrange("p g (h d) -> p (g h) d", d=P)[:, :, 0:KVC]).then_inc(s["qlat"], 1)
                yield "qT_1"
                act.wait_ge(s["qT_ps"], nth(i, u))
                act.copy(QT[u].rearrange("p b (h s) -> p h b s", s=S),
                         PS[u][:].rearrange("p g (h b s) -> p (g h) b s", b=BT, s=S)).then_inc(s["qT"], 1)

                exps(i, u, 0)
                for k in range(FRONT_STEPS):
                    yield f"probs{k}"
                    if k > 0:
                        output_T(i, u, k - 1)
                    yield f"outputs{k}"
                    exps(i, u, k + 1)

            def back(i, u):
                for k in range(FRONT_STEPS, STEPS):
                    yield f"probs{k}"
                    output_T(i, u, k - 1)
                    if k + 1 < STEPS:
                        yield f"outputs{k}"
                        exps(i, u, k + 1)
                yield "outputT"
                output_T(i, u, STEPS - 1)
                yield "norm5"
                norm_T(i, u, "back", 0)
                yield "qkv_2"
                act.wait_ge(s["gb_ps"], nth(i, u))
                act.copy(GB[u], PS[u][:, 2, 0:SV + 2 * SH])
                act.activation(GTH[u], PS[u][:, 2, 0:SV + 2 * SH], ACT.Tanh, scale=0.5).then_inc(s["g_tanh"], 1)
                yield "softplus"
                act.wait_ge(s["gates"], nth(i, u, 1, 7))
                act.activation(stat[u][:, 30:36], stat[u][:, 30:36], ACT.Exp).then_inc(s["softplus"], 1)
                act.wait_ge(s["softplus"], nth(i, u, 0, 2))
                act.activation(stat[u][:, 30:36], stat[u][:, 30:36], ACT.Ln, bias=1.0).then_inc(s["softplus"], 1)
                yield "silu"
                act.wait_ge(s["conv"], nth(i, u, CK - 1, CK))
                act.activation(CTH[u], CY[u], ACT.Tanh, scale=0.5).then_inc(s["cv_tanh"], 1)
                yield "decays"
                act.wait_ge(s["dec_ps"], nth(i, u))
                act.activation(DEX[u].rearrange("p h s -> p (h s)"), PS[u][:, 3, 0:SH * S], ACT.Exp).then_inc(s["dexp"], 1)
                yield "natural"
                act.wait_ge(s["nat_ps"], nth(i, u))
                act.copy(QKVN[u].rearrange("p h d -> p (h d)")[:, 0:3 * P], PS[u][:, 0, 0:3 * P])
                act.copy(QKVN[u].rearrange("p h d -> p (h d)")[:, 3 * P:3 * SV], PS[u][:, 1, 0:3 * SV - 3 * P]).then_inc(s["natural"], 1)
                act.wait_ge(s["natural"], nth(i, u, 0, 2))
                act.activation(SQ[u], QKVN[u][:, 0:2 * SH], ACT.Square).then_inc(s["natural"], 1)
                yield "kqT"
                act.wait_ge(s["kqT_ps"], nth(i, u))
                act.copy(KQT[u].rearrange("p (a b) n -> p a (b n)", a=2), PS[u][:, 0:2, 0:3 * P]).then_inc(s["kqT"], 1)
                for k in range(3):
                    yield f"lz{k}"
                    act.wait_ge(s["lz_ps"], nth(i, u, k, 3))
                    act.copy(ZP[u].rearrange("p h s -> p (h s)"), PS[u][:, 0, 0:SH * S]).then_inc(s["lz"], 1)
                yield "apply0"
                act.wait_ge(s["apply_ps"], nth(i, u, 0, 4))
                act.copy(WV[u].rearrange("p h s -> p (h s)"), PS[u][:, 0, 0:SH * S]).then_inc(s["applied"], 1)
                yield "apply1"
                act.wait_ge(s["apply_ps"], nth(i, u, 1, 4))
                act.copy(RV[u].rearrange("p h s -> p (h s)"), PS[u][:, 1, 0:SH * S]).then_inc(s["applied"], 1)
                yield "apply3"
                act.wait_ge(s["apply_ps"], nth(i, u, 3, 4))
                act.activation(OSQ[u].rearrange("p h s -> p (h s)"), PS[u][:, 1, 0:SH * S], ACT.Square).then_inc(s["osq"], 1)
                yield "oT"
                act.wait_ge(s["onT_ps"], nth(i, u))
                act.copy(ONT[u].rearrange("p a n -> p (a n)"), PS[u][:, 2, 0:2 * P]).then_inc(s["onT"], 1)
                yield "norm6"
                norm_T(i, u, "back", 1)
                yield "route"
                act.wait_ge(s["rdiff"], nth(i, u))
                act.activation(stat[u][:, 25:26], stat[u][:, 24:25], ACT.Tanh, scale=0.5).then_inc(s["rtanh"], 1)
                for k in range(2):
                    yield f"moe{k}_3"
                    act.wait_ge(s["m_ps"], nth(i, u, k, 2))
                    act.activation(MT[u], PS[u][:, 0:2, 0:HALF // 2], ACT.Tanh, scale=0.5).then_inc(s["m_tanh"], 1)
                yield "gT"
                act.wait_ge(s["gT_ps"], nth(i, u))
                act.copy(GT[u].rearrange("p c n -> p (c n)"), PS[u][:].rearrange("p b n -> p (b n)")[:, 0:MH]).then_inc(s["gT"], 1)

            alone(front(0, 0))
            with act.Fori(0, ROUNDS - 1) as i:
                together(front(i, 1), back(i, 0))
                together(front(i + 1, 0), back(i, 1))
            together(front(ROUNDS - 1, 1), back(ROUNDS - 1, 0))
            alone(back(ROUNDS - 1, 1))

        @block.vector
        def _(dve):
            steps = [0]

            def then(ins):
                steps[0] += 1
                ins.then_inc(s["prep_dve"], 1)
                dve.wait_ge(s["prep_dve"], steps[0])

            dve.memset(kfill, 1.0 / T)
            then(dve.memset(ones, 1.0))
            dve.wait_ge(s["prep_act"], 1)
            then(dve.tensor_scalar(small[:, 5:6], small[:, 4:5], 0.5, 0.5, MUL, ADD))
            then(dve.tensor_scalar(coef[:], ones, small[:, 5:6], None, MUL))
            then(dve.tensor_tensor_scan(crev, coef[:], kfill, 0.0, MUL, ADD))
            dve.tensor_copy(coef[:], crev[:, ::-1])
            then(dve.reduce_sum(small[:, 6:7], crev, AX.X))
            then(dve.tensor_scalar(small[:, 14:16], binc, small[:, 6:7], None, MUL))
            dve.tensor_copy(binrep, small[:, 14:16].unsqueeze(2).to_broadcast([P, DC, P])).then_inc(s["binrep"], 1)
            dve.wait_ge(s["prep_ps"], 2)
            dve.tensor_tensor(biasrep[:], PS[0][:, 1, 0:D], boutrep, ADD).then_inc(s["biasrep"], 1)
            dve.wait_ge(s["prep_act"], 2)
            dve.tensor_scalar(nega[:], small[:, 8:8 + SH], -1.0, None, MUL).then_inc(s["neg_a"], 1)
            scale = float(1.0 / np.sqrt(np.float32(HD + R)))
            dve.wait_ge(s["prep_ps"], 3)
            dve.tensor_scalar(WQ[:, :, 0:KVC], PS[1][0:QC, 0:2].rearrange("p a (h d) -> p (a h) d", d=KVC), scale,
                              None, MUL)
            dve.wait_ge(s["ld_xs"], 16 * 8)
            for half in range(2):
                last = dve.tensor_scalar(WQ[:, 8 * half:8 * half + 8, KVC:P].rearrange("p (q j) r -> p j q r", q=2),
                                         Wqr[:, 8 * half:8 * half + 8].rearrange("p (j q) r -> p j q r", q=2), scale,
                                         None, MUL)
            last.then_inc(s["q_scaled"], 1)
            dve.wait_ge(s["ld_f0"], 16 * 4)
            dve.wait_ge(s["prep_pool"], 1)
            mats = [W13[:, 0].rearrange("p c n -> p (c n)"), W13[:, 1].rearrange("p c n -> p (c n)"),
                    W2[:].rearrange("p c n -> p (c n)")]
            for k, m in enumerate(mats):
                last = dve.tensor_reduce(small[:, 1 + k:2 + k], m, AX.X, ADD, apply_absolute_value=True)
            last.then_inc(s["absum"], 1)
            dve.wait_ge(s["prep_ps"], 6)
            then(dve.tensor_scalar(scales[:, 0:3], PS[1][:, 3, 0:3], 1.0 / (FF * D), None, MUL))
            dve.tensor_scalar(scales[:, 3:6], scales[:, 0:3], 0.5, None, MUL)
            then(dve.tensor_scalar(scales[:, 6:9], scales[:, 0:3], -0.5, None, MUL))

            def ternary(k):
                m = mats[k]
                above, below = quant
                then(dve.tensor_scalar(below, m, scales[:, 6 + k:7 + k], None, ALU.is_lt))
                then(dve.scalar_tensor_tensor(above, m, scales[:, 3 + k:4 + k], below, ALU.is_gt, SUB))
                then(dve.scalar_tensor_tensor(above, above, scales[:, k:k + 1], m, MUL, SUB))
                dve.tensor_tensor(m, m, above, ADD).then_inc(s["ternary"], 1)
                dve.wait_ge(s["ternary"], k + 1)

            def norm_stats(i, u, part, k, src, src_sem, value):
                dve.wait_ge(src_sem, value)
                dve.bn_stats(st[u][:], src).then_inc(s[f"ln_stats_{part}"], 1)
                wait_apart(dve, (s[f"ln_stats_{part}"], nth(i, u, k, LNS[part])))
                dve.bn_aggr(mv[u][:], st[u][:]).then_inc(s[f"ln_mv_{part}"], 1)
                dve.wait_ge(s[f"ln_mv_{part}"], nth(i, u, k, LNS[part]))
                dve.tensor_scalar(ve[u][:, 0:1], mv[u][:, 1:2], EPS, None, ADD).then_inc(s[f"ln_var_{part}"], 1)

            def norm_scale(i, u, part, k, src):
                dve.wait_ge(s[f"ln_rstd_{part}"], nth(i, u, k, LNS[part]))
                dve.tensor_scalar(XN[u][:], src, mv[u][:, 0:1], ve[u][:, 1:2], SUB, MUL).then_inc(s[f"ln_x_{part}"], 1)

            def maxima(i, u, k):
                dve.wait_ge(s["s_ps"], nth(i, u, k, STEPS))
                m = 4 * (k % 2)
                dve.reduce_max(stat[u][:, m:m + 2], PS[u][:, 0:2, 0:T], AX.X, negate=True).then_inc(s["s_max"], 1)

            def probs_T(i, u, k):
                m = 4 * (k % 2)
                dve.wait_ge(s["pT_ps"], nth(i, u, k, STEPS))
                dve.tensor_copy(PT[u].rearrange("p a n -> p (a n)"), PS[u][:, 2]).then_inc(s["pT"], 1)
                dve.reciprocal(stat[u][:, 8 + m:10 + m], stat[u][:, m + 2:m + 4]).then_inc(s["o_rinv"], 1)
                if k + 1 < STEPS:
                    maxima(i, u, k + 1)

            def outputs(i, u, k):
                m = 4 * (k % 2)
                dve.wait_ge(s["o_ps"], nth(i, u, k, STEPS))
                for q in range(2):
                    last = dve.scalar_tensor_tensor(OC[u][k % 2][:, q * KVC:(q + 1) * KVC], VL[u][:, k // 2],
                                                    EX[u][k % 2][:, q, T - 1:T],
                                                    PS[u][:, 3, q * KVC:(q + 1) * KVC], MUL, ADD)
                last.then_inc(s["o_left"], 1)
                dve.wait_ge(s["o_left"], nth(i, u, k, STEPS))
                dve.wait_ge(s["o_rinv"], nth(i, u, k, STEPS))
                oc = OC[u][k % 2].rearrange("p (q d) -> p q d", q=2)
                dve.tensor_tensor(oc, oc, stat[u][:, 8 + m:10 + m].unsqueeze(2).to_broadcast([P, 2, KVC]),
                                  MUL).then_inc(s["oc"], 1)

            def front(i, u):
                yield "keys"
                norm_stats(i, u, "front", 0, xin[u][:], ld_xin[u], 16 * i + 16)
                dve.wait_ge(ld_ctx[u], 32 * i + 32)
                for c in range(DC):
                    for b in range(BT):
                        k = c * BT + b
                        last = dve.tensor_tensor_reduce(prod[u][:, k], CT[u][:, c, b], coef[:], 1.0, 0.0, MUL, ADD,
                                                        pooled[u][:, k:k + 1])
                last.then_inc(s["pool_terms"], 1)
                dve.wait_ge(s["pool_terms"], nth(i, u))
                dve.tensor_copy(crep[u].rearrange("p c b s -> p (c b) s"),
                                pooled[u][:].unsqueeze(2).to_broadcast([P, DC * BT, S])).then_inc(s["pooledrep"], 1)
                yield "scale_front0"
                norm_scale(i, u, "front", 0, xin[u][:])
                yield "norm_in"
                dve.wait_ge(s["residual_ps_front"], nth(i, u, 0, 3))
                dve.wait_ge(s["ln_x_front"], nth(i, u, 0, LNS["front"]))
                dve.tensor_tensor(ytmp[u], XN[u][:], biasrep[:], ADD).then_inc(s["ysum"], 1)
                dve.wait_ge(s["ysum"], nth(i, u, 0, 2))
                dve.tensor_tensor(ytmp[u], ytmp[u], PS[u][:, 3, 0:D], ADD).then_inc(s["ysum"], 1)
                yield "norm_y"
                norm_stats(i, u, "front", 1, ytmp[u], s["ysum"], nth(i, u, 1, 2))
                yield "scale_front1"
                norm_scale(i, u, "front", 1, ytmp[u])
                dve.wait_ge(s["ln_x_front"], nth(i, u, 1, LNS["front"]))
                dve.tensor_tensor(ytmp[u], XN[u][:], gamma[:], MUL).then_inc(s["gammad"], 1)
                dve.wait_ge(s["gammad"], nth(i, u, 0, 2))
                dve.tensor_tensor(ytmp[u], ytmp[u], beta[:], ADD).then_inc(s["gammad"], 1)
                dve.wait_ge(s["gammad"], nth(i, u, 1, 2))
                dve.wait_ge(stored[u], 16 * i + 16)
                dve.tensor_tensor(X[u][:], ytmp[u], xin[u][:], ADD).then_inc(s["residual_front"], 1)
                yield "norm0"
                norm_stats(i, u, "front", 2, X[u][:], s["residual_front"], nth(i, u, 0, 3))
                yield "scale_front2"
                norm_scale(i, u, "front", 2, X[u][:])
                yield "s0_3"
                for g in range(2):
                    dve.wait_ge(s["s0_ps"], nth(i, u, g, 2))
                    dve.reduce_max(stat[u][:, 4 * g:4 * g + 4],
                                   PS[u][:, 2 * g:2 * g + 2].rearrange("p b (e f) -> p (b e) f", e=DC), AX.X,
                                   negate=True).then_inc(s["attn0"], 1)
                    dve.wait_ge(s["attn0"], nth(i, u, 2 * g, 6))
                    dve.tensor_scalar(stat[u][:, 8 + 4 * g:12 + 4 * g], stat[u][:, 4 * g:4 * g + 4],
                                      float(1 / np.sqrt(L0_HEAD)), None, MUL).then_inc(s["attn0"], 1)
                yield "av0_1"
                dve.wait_ge(s["e0"], nth(i, u, 1, 2))
                dve.reciprocal(stat[u][:, 24:32], stat[u][:, 16:24]).then_inc(s["attn0"], 1)
                dve.wait_ge(s["attn0"], nth(i, u, 4, 6))
                dve.wait_ge(s["av_ps"], nth(i, u))
                for e in range(DC):
                    last = dve.tensor_tensor(
                        AV0[u][:, e].rearrange("p (b s) -> p b s", b=BT),
                        PS[u][:, 0, e * P:(e + 1) * P].rearrange("p (b s) -> p b s", b=BT),
                        stat[u][:, 24 + e:32:2].unsqueeze(2).to_broadcast([P, BT, S]), MUL)
                last.then_inc(s["attn0"], 1)
                dve.wait_ge(s["residual_ps_front"], nth(i, u, 1, 3))
                dve.tensor_tensor(X[u][:], X[u][:], PS[u][:, 1, 0:D], ADD).then_inc(s["residual_front"], 1)
                yield "normf"
                norm_stats(i, u, "front", 3, X[u][:], s["residual_front"], nth(i, u, 1, 3))
                yield "scale_front3"
                norm_scale(i, u, "front", 3, X[u][:])
                yield "ffn_up_5"
                dve.wait_ge(s["f_tanh"], nth(i, u))
                dve.scalar_tensor_tensor(FU[u], FT[u], 1.0, PS[u][:, 0:2, 0:3 * P], ADD, MUL).then_inc(s["ffn"], 1)
                dve.wait_ge(s["ffn"], nth(i, u, 0, 2))
                dve.scalar_tensor_tensor(FG[u].rearrange("p (a c) n -> p a (c n)", a=2), FU[u], 0.5,
                                         PS[u][:, 2:4, 0:3 * P], MUL, MUL).then_inc(s["ffn"], 1)
                yield "ffn_down_2"
                dve.wait_ge(s["residual_ps_front"], nth(i, u, 2, 3))
                dve.tensor_tensor(X[u][:], X[u][:], PS[u][:, 0, 0:D], ADD).then_inc(s["residual_front"], 1)
                yield "normq"
                norm_stats(i, u, "front", 4, X[u][:], s["residual_front"], nth(i, u, 2, 3))
                yield "scale_front4"
                norm_scale(i, u, "front", 4, X[u][:])
                yield "q_3"
                dve.wait_ge(s["qlat"], nth(i, u))
                q = PS[u][:].rearrange("p g (h d) -> p (g h) d", d=P)
                dve.tensor_tensor(QR[u][:, :, KVC:P], q[:, :, KVC:P],
                                  const("qcos").unsqueeze(1).to_broadcast([P, XH, R]), MUL)
                dve.tensor_tensor(QRt[u][:, :, 0:R // 2], q[:, :, KVC + R // 2:P],
                                  const("qnsin").unsqueeze(1).to_broadcast([P, XH, R // 2]), MUL)
                dve.tensor_tensor(QRt[u][:, :, R // 2:R], q[:, :, KVC:KVC + R // 2],
                                  const("qsin").unsqueeze(1).to_broadcast([P, XH, R // 2]), MUL).then_inc(s["qr2"], 1)
                yield "qT_out"
                maxima(i, u, 0)
                for k in range(FRONT_STEPS):
                    yield f"probs{k}"
                    probs_T(i, u, k)
                    yield f"outputs{k}"
                    outputs(i, u, k)

            def back(i, u):
                for k in range(FRONT_STEPS, STEPS):
                    yield f"probs{k}"
                    probs_T(i, u, k)
                    yield f"outputs{k}"
                    outputs(i, u, k)
                yield "up_3"
                dve.wait_ge(s["residual_ps_back"], nth(i, u, 0, 3))
                dve.tensor_tensor(X[u][:], X[u][:], PS[u][:, 0, 0:D], ADD).then_inc(s["residual_back"], 1)
                yield "norm5"
                dve.wait_ge(s["residual_back"], nth(i, u, 0, 3))
                dve.memset(CX[u][:, :, :, 0:CK - 1], 0.0).then_inc(s["cv_pad"], 1)
                norm_stats(i, u, "back", 0, X[u][:], s["residual_back"], nth(i, u, 0, 3))
                yield "scale_back0"
                norm_scale(i, u, "back", 0, X[u][:])
                yield "qkv_2"
                dve.wait_ge(s["cv_ps"], nth(i, u))
                dve.tensor_copy(CX[u][:, 0:3, :, CK - 1:], PS[u][:, 0, 0:3 * P].rearrange("p (c b s) -> p c b s", c=3, b=BT))
                dve.tensor_copy(CX[u][:, 3:5, :, CK - 1:], PS[u][:, 1, 0:2 * P].rearrange("p (c b s) -> p c b s", c=2, b=BT)).then_inc(s["cvx"], 1)
                dve.wait_ge(s["g_tanh"], nth(i, u))
                dve.tensor_tensor(stat[u][:, 24:30], GB[u][:, SV + SH:SV + 2 * SH], dtb[:], ADD).then_inc(s["gates"], 1)
                dve.wait_ge(s["gates"], nth(i, u, 0, 7))
                dve.scalar_tensor_tensor(stat[u][:, 30:36], stat[u][:, 24:30], -1.0, stat[u][:, 24:30], MUL, ALU.min)
                dve.tensor_scalar(stat[u][:, 54:60], stat[u][:, 24:30], 0.0, None, ALU.max).then_inc(s["gates"], 1)
                dve.scalar_tensor_tensor(GS[u].rearrange("p h d -> p (h d)"), GTH[u][:, 0:SV], 1.0, GB[u][:, 0:SV],
                                         ADD, MUL).then_inc(s["gates"], 1)
                dve.wait_ge(s["gates"], nth(i, u, 2, 7))
                dve.tensor_tensor(GS[u], GS[u], onw[:].unsqueeze(1).to_broadcast([P, SH, SD]), MUL).then_inc(s["gates"], 1)

                def tap(k):
                    if k == 0:
                        dve.wait_ge(s["cvx"], nth(i, u))
                        dve.wait_ge(s["cv_pad"], nth(i, u))
                    else:
                        dve.wait_ge(s["conv"], nth(i, u, k - 1, CK))
                    for c in range(QKVC):
                        y = CY[u][:, c].rearrange("p (b s) -> p b s", b=BT)
                        src = CX[u][:, c, :, k:k + S]
                        if k == 0:
                            last = dve.tensor_scalar(y, src, convw[:, c, k:k + 1], None, MUL)
                        else:
                            last = dve.scalar_tensor_tensor(y, src, convw[:, c, k:k + 1], y, MUL, ADD)
                    last.then_inc(s["conv"], 1)

                yield "softplus"
                tap(0)
                yield "decay"
                tap(1)
                dve.wait_ge(s["gates"], nth(i, u, 1, 7))
                dve.wait_ge(s["softplus"], nth(i, u, 1, 2))
                dve.tensor_tensor(stat[u][:, 36:42], stat[u][:, 30:36], stat[u][:, 54:60], ADD).then_inc(s["gates"], 1)
                dve.wait_ge(s["gates"], nth(i, u, 4, 7))
                dve.wait_ge(s["neg_a"], 1)
                dve.tensor_tensor(stat[u][:, 36:42], stat[u][:, 36:42], nega[:], MUL).then_inc(s["gates"], 1)
                dve.tensor_scalar(stat[u][:, 24:30], GTH[u][:, SV:SV + SH], 0.5, 0.5, MUL, ADD)
                dve.tensor_scalar(stat[u][:, 30:36], GTH[u][:, SV:SV + SH], 0.25, 0.25, MUL, ADD).then_inc(s["gates"], 1)
                yield "conv_a"
                tap(2)
                yield "conv_b"
                tap(3)
                yield "silu"
                dve.wait_ge(s["cv_tanh"], nth(i, u))
                dve.scalar_tensor_tensor(CTH[u], CTH[u], 1.0, CY[u], ADD, MUL).then_inc(s["cv_u"], 1)
                yield "natural"
                dve.wait_ge(s["natural"], nth(i, u, 1, 2))
                dve.reduce_sum(stat[u][:, 0:12], SQ[u], AX.X).then_inc(s["qkvn"], 1)
                dve.wait_ge(s["qkvn"], nth(i, u, 0, 4))
                dve.tensor_scalar(stat[u][:, 0:6], stat[u][:, 0:6], 4e-6, float(SD), ADD, MUL)
                dve.tensor_scalar(stat[u][:, 6:12], stat[u][:, 6:12], 4e-6, None, ADD).then_inc(s["qkvn"], 1)
                yield "unit"
                dve.wait_ge(s["rn"], nth(i, u))
                dve.tensor_tensor(NAT[u][:, 0:2 * SH], QKVN[u][:, 0:2 * SH],
                                  stat[u][:, 12:24].unsqueeze(2).to_broadcast([P, 2 * SH, SD]), MUL).then_inc(s["qkvn"], 1)
                dve.wait_ge(s["qkvn"], nth(i, u, 2, 4))
                dve.wait_ge(s["gates"], nth(i, u, 6, 7))
                dve.tensor_tensor(NAT[u][:, 2 * SH:3 * SH], NAT[u][:, SH:2 * SH],
                                  stat[u][:, 24:30].unsqueeze(2).to_broadcast([P, SH, SD]), MUL)
                dve.tensor_tensor(BV[u], QKVN[u][:, 2 * SH:3 * SH],
                                  stat[u][:, 30:36].unsqueeze(2).to_broadcast([P, SH, SD]), MUL).then_inc(s["qkvn"], 1)
                yield "mask"
                dve.wait_ge(s["gram_ps"], nth(i, u))
                dve.wait_ge(s["dts"], nth(i, u))
                for g, n in ((0, 4), (1, 2)):
                    last = dve.tensor_tensor(ATP[u][:, 4 * g:4 * g + n], PS[u][:, 0:n, 2 * g * S:(2 * g + 1) * S],
                                             DTS[u][:, 4 * g:4 * g + n], MUL)
                last.then_inc(s["atp"], 1)
                for g, n in ((0, 4), (1, 2)):
                    last = dve.tensor_tensor(PMP[u][:, 4 * g:4 * g + n], PS[u][:, 0:n, (2 * g + 1) * S:(2 * g + 2) * S],
                                             DTI[u][:, 4 * g:4 * g + n], MUL)
                last.then_inc(s["pmp"], 1)
                dve.wait_ge(s["atp"], nth(i, u))
                dve.tensor_tensor(XP[u], ATP[u], const("off1").unsqueeze(1).to_broadcast([P, SH, S]), MUL).then_inc(s["tri"], 1)
                dve.wait_ge(s["tri"], nth(i, u, 0, 2))
                dve.tensor_tensor(XP[u], const("eye").unsqueeze(1).to_broadcast([P, SH, S]), XP[u], SUB).then_inc(s["tri"], 1)

                def expand_x(k):
                    dve.tensor_tensor(XBD[u].rearrange("p h (b j) -> p h b j", b=BT),
                                      XP[u].unsqueeze(2).to_broadcast([P, SH, BT, S]),
                                      const("same").rearrange("p (b j) -> p b j", b=BT).unsqueeze(1)
                                      .to_broadcast([P, SH, BT, S]), MUL).then_inc(s["xbd"], 1)

                dve.wait_ge(s["tri"], nth(i, u, 1, 2))
                dve.transpose(TP[u].rearrange("p h s -> p (h s)"), XP[u].rearrange("p h s -> p (h s)")).then_inc(s["t2inv"], 1)
                expand_x(0)
                for k in range(3):
                    yield f"lt{k}"
                    dve.wait_ge(s["lt_ps"], nth(i, u, k, 3))
                    if k == 0:
                        dve.wait_ge(s["t2inv"], nth(i, u, 0, 4))
                    dve.tensor_tensor(TP[u].rearrange("p h s -> p (h s)"), TP[u].rearrange("p h s -> p (h s)"),
                                      PS[u][:, 1, 0:SH * S], SUB).then_inc(s["t2inv"], 1)
                    dve.wait_ge(s["t2inv"], nth(i, u, k + 1, 4))
                    dve.transpose(XP[u].rearrange("p h s -> p (h s)"), TP[u].rearrange("p h s -> p (h s)")).then_inc(s["xnew"], 1)
                    dve.wait_ge(s["xnew"], nth(i, u, k, 3))
                    expand_x(k + 1)
                yield "apply2"
                dve.wait_ge(s["apply_ps"], nth(i, u, 2, 4))
                dve.tensor_tensor(UU[u].rearrange("p h s -> p (h s)"), WV[u].rearrange("p h s -> p (h s)"),
                                  PS[u][:, 0, 0:SH * SD], SUB).then_inc(s["uu"], 1)
                yield "onorm"
                dve.wait_ge(s["osq"], nth(i, u))
                dve.reduce_sum(stat[u][:, 42:48], OSQ[u], AX.X).then_inc(s["onorm"], 1)
                dve.wait_ge(s["onorm"], nth(i, u, 0, 4))
                dve.tensor_scalar(stat[u][:, 42:48], stat[u][:, 42:48], 1.0 / SD, EPS, MUL, ADD).then_inc(s["onorm"], 1)
                dve.wait_ge(s["gates"], nth(i, u, 3, 7))
                dve.tensor_tensor(ON[u], PS[u][:, 1, 0:SV].rearrange("p (h d) -> p h d", h=SH), GS[u], MUL).then_inc(s["onorm"], 1)
                yield "onorm_scale"
                dve.wait_ge(s["onorm"], nth(i, u, 2, 4))
                dve.wait_ge(s["orn"], nth(i, u))
                dve.scalar_tensor_tensor(ON[u], ON[u], 0.5, stat[u][:, 48:54].unsqueeze(2).to_broadcast([P, SH, SD]),
                                         MUL, MUL).then_inc(s["onorm"], 1)
                yield "out"
                dve.wait_ge(s["residual_ps_back"], nth(i, u, 1, 3))
                dve.tensor_tensor(X[u][:], X[u][:], PS[u][:, 3, 0:D], ADD).then_inc(s["residual_back"], 1)
                yield "norm6"
                norm_stats(i, u, "back", 1, X[u][:], s["residual_back"], nth(i, u, 1, 3))
                yield "scale_back1"
                norm_scale(i, u, "back", 1, X[u][:])
                yield "route"
                dve.wait_ge(s["rt_ps"], nth(i, u))
                dve.tensor_copy(stat[u][:, 0:8], PS[u][:, 3, 0:NE]).then_inc(s["route"], 1)
                wait_apart(dve, (s["route"], nth(i, u, 0, 7)))
                dve.max(stat[u][:, 8:16], stat[u][:, 0:8]).then_inc(s["route"], 1)
                wait_apart(dve, (s["route"], nth(i, u, 1, 7)))
                dve.max_index(oidx[u][:], stat[u][:, 8:16], stat[u][:, 0:8]).then_inc(s["route"], 1)
                dve.tensor_tensor(stat[u][:, 24:25], stat[u][:, 8:9], stat[u][:, 9:10], SUB).then_inc(s["rdiff"], 1)
                dve.wait_ge(s["route"], nth(i, u, 2, 7))
                dve.tensor_copy(stat[u][:, 16:24], oidx[u][:]).then_inc(s["route"], 1)
                yield "route_probs"
                dve.wait_ge(s["rtanh"], nth(i, u))
                dve.tensor_scalar(stat[u][:, 26:27], stat[u][:, 25:26], 0.25, 0.25, MUL, ADD)
                dve.tensor_scalar(stat[u][:, 27:28], stat[u][:, 25:26], -0.25, 0.25, MUL, ADD).then_inc(s["route"], 1)
                dve.wait_ge(s["route"], nth(i, u, 3, 7))
                dve.wait_ge(s["route"], nth(i, u, 4, 7))
                dve.tensor_scalar(stat[u][:, 32:40], const("iota"), stat[u][:, 16:17], stat[u][:, 26:27],
                                  ALU.is_equal, MUL)
                dve.tensor_scalar(stat[u][:, 40:48], const("iota"), stat[u][:, 17:18], stat[u][:, 27:28],
                                  ALU.is_equal, MUL).then_inc(s["route"], 1)
                dve.wait_ge(s["route"], nth(i, u, 5, 7))
                dve.tensor_tensor(stat[u][:, 48:56], stat[u][:, 32:40], stat[u][:, 40:48], ADD).then_inc(s["route"], 1)
                for k in range(2):
                    yield f"moe{k}_3"
                    dve.wait_ge(s["m_tanh"], nth(i, u, k, 2))
                    dve.scalar_tensor_tensor(MU[u], MT[u], 1.0, PS[u][:, 0:2, 0:HALF // 2], ADD, MUL).then_inc(s["m_u"], 1)
                    dve.wait_ge(s["m_u"], nth(i, u, k, 2))
                    dve.wait_ge(s["route"], nth(i, u, 6, 7))
                    for e in range(4):
                        cols = slice(e % 2 * EH, (e % 2 + 1) * EH)
                        a = k * HALF + e * EH
                        last = dve.scalar_tensor_tensor(MG[u][:, a:a + EH], MU[u][:, e // 2, cols],
                                                        stat[u][:, 48 + 4 * k + e:49 + 4 * k + e],
                                                        PS[u][:, 2 + e // 2, cols], MUL, MUL)
                    last.then_inc(s["m_g"], 1)
                yield "down_3"
                dve.wait_ge(s["residual_ps_back"], nth(i, u, 2, 3))
                dve.tensor_tensor(X[u][:], X[u][:], PS[u][:, 3, 0:D], ADD).then_inc(s["residual_back"], 1)

            first = front(0, 0)
            for k, stage in enumerate(("s0_3", "av0_1", "ffn_up_5")):
                up_to(first, stage)
                ternary(k)
            alone(first)
            with dve.Fori(0, ROUNDS - 1) as i:
                together(front(i, 1), back(i, 0))
                together(front(i + 1, 0), back(i, 1))
            together(front(ROUNDS - 1, 1), back(ROUNDS - 1, 0))
            alone(back(ROUNDS - 1, 1))


_WEIGHTS = ["W_in", "W_outT", "b_in", "b_out", "gamma", "beta", "decay", "dt_bias", "A_log", "o_norm", "Wqk0", "Wv0",
            "Wo0", "w1T", "w3T", "w2T", "W_kvc", "W_kvcT", "W_dq", "W_uqT", "W_qr", "W_ukT", "W_kr", "W_uvT", "W_o",
            "Wqkv1", "Wgba", "conv", "WoT1", "WgT", "W1T", "W2T", "W3T"]


def lay_out(a):
    def t(v):
        return v.T

    row = lambda v: v.reshape(1, -1)
    qkv = np.concatenate([a["L1_attn_Wq"], a["L1_attn_Wk"], a["L1_attn_Wv"]], 0)
    conv = np.concatenate([a["L1_attn_conv_q"], a["L1_attn_conv_k"], a["L1_attn_conv_v"]], 0)
    pad = QKVC * P - 3 * SV
    return {
        "x": a["x"].reshape(B * S, D),
        "ctxT": a["ctx_2048"].transpose(2, 0, 1),
        "itok": a["itok_BxS_0_1023"].reshape(B * S, 1),
        "consts": constant_table(),
        "W_in": a["L0_xattn_W_in"], "W_outT": t(a["L0_xattn_W_out"]),
        "b_in": a["L0_xattn_b_in"].reshape(DC, P).T, "b_out": row(a["L0_xattn_b_out"]),
        "gamma": row(a["L0_xattn_gamma"]), "beta": row(a["L0_xattn_beta"]), "decay": row(a["L0_xattn_decay"]),
        "dt_bias": row(a["L1_attn_dt_bias"]), "A_log": row(a["L1_attn_A_log"]), "o_norm": row(a["L1_attn_o_norm_w"]),
        "Wqk0": np.concatenate([a["L0_attn_Wq"], a["L0_attn_Wk"]], 1), "Wv0": a["L0_attn_Wv"], "Wo0": a["L0_attn_Wo"],
        "w1T": t(a["L0_ffn_w1"]), "w3T": t(a["L0_ffn_w3"]), "w2T": t(a["L0_ffn_w2"]),
        "W_kvc": a["L1_xattn_W_kvc"], "W_kvcT": t(a["L1_xattn_W_kvc"]), "W_dq": a["L1_xattn_W_dq"],
        "W_uqT": t(a["L1_xattn_W_uq"]), "W_qr": a["L1_xattn_W_qr"], "W_ukT": t(a["L1_xattn_W_uk"]),
        "W_kr": a["L1_xattn_W_kr"], "W_uvT": t(a["L1_xattn_W_uv"]), "W_o": a["L1_xattn_W_o"],
        "Wqkv1": np.pad(qkv.T, ((0, 0), (0, pad))),
        "Wgba": np.concatenate([a["L1_attn_Wg"], a["L1_attn_Wb"], a["L1_attn_Wa"]], 0).T,
        "conv": np.pad(conv, ((0, pad), (0, 0))), "WoT1": t(a["L1_attn_Wo"]),
        "WgT": t(a["L1_ffn_Wg"]), "W1T": a["L1_ffn_W1"].transpose(2, 0, 1).reshape(D, MH),
        "W2T": a["L1_ffn_W2"].transpose(2, 0, 1).reshape(D, MH), "W3T": a["L1_ffn_W3"].transpose(0, 2, 1).reshape(MH, D),
    }


def kernel(**inputs):
    import concourse.bacc as bacc
    from concourse.bass_utils import run_bass_kernel_spmd

    nc = bacc.Bacc("TRN2", target_bir_lowering=False, num_devices=1)
    arrays, aps = {}, {}
    for name, v in lay_out({k: np.asarray(v) for k, v in inputs.items()}).items():
        v = np.ascontiguousarray(v)
        arrays[f"in_{name}"] = v
        aps[name] = nc.dram_tensor(f"in_{name}", v.shape, mybir.dt.from_np(v.dtype), kind="ExternalInput").ap()
    out = nc.dram_tensor("out", (B * S, D), mybir.dt.float32, kind="ExternalOutput").ap()
    perceiver_kernel(nc, aps["x"], aps["ctxT"], aps["itok"], aps["consts"],
                     {n: aps[n] for n in _WEIGHTS}, out)
    r = run_bass_kernel_spmd(nc, [arrays], core_ids=[0])
    return r.results[0]["out"].reshape(B, S, D)
```
